# Optimizing a Trainium2 kernel written in Bass

```python
import numpy as np
import jax
import jax.numpy as jnp

def _softmax(x, axis=-1):
    return jax.nn.softmax(x, axis=axis)

def _gelu(x):
    return jax.nn.gelu(x, approximate=True)

def _silu(x):
    return jax.nn.silu(x)

def _sigmoid(x):
    return jax.nn.sigmoid(x)

def _layernorm(x, axis=-1, eps=1e-05):
    m = jnp.mean(x, axis=axis, keepdims=True)
    v = jnp.var(x, axis=axis, keepdims=True)
    return (x - m) / jnp.sqrt(v + eps)

def _scatter_add(tgt, idx, src, axis=0):
    return tgt.at[idx].add(src)

def _segment_sum(src, seg, n):
    return jax.ops.segment_sum(src, seg, n)
kernel_name = 'mk_gnn_resnorm_d4_gnn_r32_26a0b7'

def setup_inputs(seed: int=0):
    np.random.seed(seed)
    _w = jnp.asarray

    def _rec_inputs():
        import jax
        import jax.numpy as jnp
        _gk = jax.random.key(seed)
        x = -0.000202 + 1 * jax.random.normal(jax.random.fold_in(_gk, 1), (3125, 128), jnp.float32)
        src = jax.random.randint(jax.random.fold_in(_gk, 2), (100000,), 0, 3125, jnp.int32)
        dst = jax.random.randint(jax.random.fold_in(_gk, 3), (100000,), 0, 3125, jnp.int32)
        _o = jnp.argsort(dst, stable=True)
        src = src[_o]
        dst = dst[_o]
        edge_attr_16 = 6.40344e-05 + 1.00026 * jax.random.normal(jax.random.fold_in(_gk, 13), (100000, 16), jnp.float32)
        edge_weight1 = 0.000614103 + 0.999867 * jax.random.normal(jax.random.fold_in(_gk, 15), (100000, 1), jnp.float32)
        return (x, src, dst, edge_attr_16, edge_weight1)
    x, src, dst, edge_attr_16, edge_weight1 = _rec_inputs()

    def _L0_gnn_setup():
        import jax, jax.numpy as jnp
        import numpy as np
        import math
        HEADS = 8
        CH = 16
        SCALE = 1.0 / math.sqrt(CH)

        def _transformer_conv(x, src, dst, qw, qb, kw, kb, vw, vb, sw, sb):
            N = x.shape[0]
            q = (x @ qw + qb).reshape(N, HEADS, CH)
            k = (x @ kw + kb).reshape(N, HEADS, CH)
            v = (x @ vw + vb).reshape(N, HEADS, CH)
            alpha = jnp.sum(q[dst] * k[src], axis=-1) * SCALE
            m = jax.ops.segment_max(alpha, dst, num_segments=N)
            a = jnp.exp(alpha - m[dst])
            denom = jax.ops.segment_sum(a, dst, num_segments=N)
            a = a / denom[dst]
            msg = v[src] * a[:, :, None]
            out = jax.ops.segment_sum(msg, dst, num_segments=N).reshape(N, HEADS * CH)
            return out + x @ sw + sb
        key = jax.random.key(seed)
        ks = jax.random.split(key, 16)
        N, E, IN = (50000, 25000, 128)
        D = HEADS * CH

        def lin(k, fi, fo):
            return jax.random.normal(k, (fi, fo), jnp.float32) / math.sqrt(fi)
        inp = {'x': jax.random.normal(ks[0], (N, IN), jnp.float32), 'edge_index': jax.random.randint(ks[1], (2, E), 0, N, dtype=jnp.int64), 'edge_attr': jax.random.normal(ks[2], (E, 1), jnp.float32), 'q_w0': lin(ks[3], IN, D), 'q_b0': jnp.zeros((D,), jnp.float32), 'k_w0': lin(ks[4], IN, D), 'k_b0': jnp.zeros((D,), jnp.float32), 'v_w0': lin(ks[5], IN, D), 'v_b0': jnp.zeros((D,), jnp.float32), 's_w0': lin(ks[6], IN, D), 's_b0': jnp.zeros((D,), jnp.float32), 'q_w1': lin(ks[7], D, D), 'q_b1': jnp.zeros((D,), jnp.float32), 'k_w1': lin(ks[8], D, D), 'k_b1': jnp.zeros((D,), jnp.float32), 'v_w1': lin(ks[9], D, D), 'v_b1': jnp.zeros((D,), jnp.float32), 's_w1': lin(ks[10], D, D), 's_b1': jnp.zeros((D,), jnp.float32)}
        return inp
    _L0_gnn_all = _L0_gnn_setup()
    _L0_gnn_in = {k: v for k, v in _L0_gnn_all.items() if k in ('q_w0', 'q_b0', 'k_w0', 'k_b0', 'v_w0', 'v_b0', 's_w0', 's_b0', 'q_w1', 'q_b1', 'k_w1', 'k_b1', 'v_w1', 'v_b1', 's_w1', 's_b1')}
    del _L0_gnn_all

    def _L1_gnn_setup():
        import jax, jax.numpy as jnp
        import numpy as np
        N_NODES = 10000
        N_EDGES = 20000
        IN_FEATS = 128
        OUT_FEATS = 128
        key = jax.random.key(seed)
        k_x, k_w, k_b, k_row, k_col = jax.random.split(key, 5)
        x = jax.random.normal(k_x, (N_NODES, IN_FEATS), dtype=jnp.float32)
        W = jax.random.normal(k_w, (OUT_FEATS, 2 * IN_FEATS), dtype=jnp.float32) * 0.05
        b = jax.random.normal(k_b, (OUT_FEATS,), dtype=jnp.float32) * 0.05
        row = jax.random.randint(k_row, (N_EDGES,), 0, N_NODES)
        col = jax.random.randint(k_col, (N_EDGES,), 0, N_NODES)
        return {'x': x, 'W': W, 'b': b, 'row': row, 'col': col}
    _L1_gnn_all = _L1_gnn_setup()
    _L1_gnn_in = {k: v for k, v in _L1_gnn_all.items() if k in ('W', 'b')}
    del _L1_gnn_all

    def _L2_gnn_setup():
        import jax, jax.numpy as jnp
        import numpy as np
        N, E = (50000, 25000)
        X_DIM, EA_DIM, H, L = (128, 16, 128, 3)
        BN_EPS = 1e-05
        key = jax.random.key(seed)
        ks = jax.random.split(key, 20)
        s = 0.02
        inp = {'x': jax.random.normal(ks[0], (N, X_DIM), jnp.float32), 'edge_index': jax.random.randint(ks[1], (2, E), 0, N, jnp.int64), 'batch': jnp.sort(jax.random.randint(ks[2], (N,), 0, 128, jnp.int64)), 'edge_attr': jax.random.normal(ks[3], (E, EA_DIM), jnp.float32), 'edge_atten': jax.random.uniform(ks[4], (E, 1), jnp.float32), 'W_enc': jax.random.normal(ks[5], (X_DIM, H), jnp.float32) * s, 'b_enc': jnp.zeros((H,), jnp.float32), 'W_ee': jax.random.normal(ks[6], (EA_DIM, H), jnp.float32) * s, 'b_ee': jnp.zeros((H,), jnp.float32), 'eps': jnp.zeros((L,), jnp.float32), 'W1': jax.random.normal(ks[7], (L, H, H), jnp.float32) * s, 'b1': jnp.zeros((L, H), jnp.float32), 'bn_gamma': jnp.ones((L, H), jnp.float32), 'bn_beta': jnp.zeros((L, H), jnp.float32), 'bn_mean': jnp.zeros((L, H), jnp.float32), 'bn_var': jnp.ones((L, H), jnp.float32), 'W2': jax.random.normal(ks[8], (L, H, H), jnp.float32) * s, 'b2': jnp.zeros((L, H), jnp.float32)}
        return inp
    _L2_gnn_all = _L2_gnn_setup()
    _L2_gnn_in = {k: v for k, v in _L2_gnn_all.items() if k in ('W_enc', 'b_enc', 'W_ee', 'b_ee', 'eps', 'W1', 'b1', 'bn_gamma', 'bn_beta', 'bn_mean', 'bn_var', 'W2', 'b2')}
    del _L2_gnn_all

    def _L3_gnn_setup():
        import jax, jax.numpy as jnp
        import numpy as np
        N = 3125
        E = 100000
        D_IN = 128
        D_OUT = 128
        ALPHA = 0.2
        LN_EPS = 1e-05
        key = jax.random.key(seed)
        k1, k2, k3, k4, k5 = jax.random.split(key, 5)
        x = jax.random.normal(k1, (N, D_IN), dtype=jnp.float32)
        edge = jax.random.randint(k2, (2, E), 0, N, dtype=jnp.int64)
        W = jax.random.normal(k3, (D_OUT, D_IN), dtype=jnp.float32) * np.sqrt(2.0 / D_IN)
        b = jnp.zeros((D_OUT,), dtype=jnp.float32)
        a = jax.random.normal(k4, (2 * D_OUT,), dtype=jnp.float32) * np.sqrt(2.0 / (2 * D_OUT))
        ln_w = jnp.ones((D_OUT,), dtype=jnp.float32)
        ln_b = jnp.zeros((D_OUT,), dtype=jnp.float32)
        return {'x': x, 'W': W, 'b': b, 'a': a, 'ln_w': ln_w, 'ln_b': ln_b, 'edge': edge}
    _L3_gnn_all = _L3_gnn_setup()
    _L3_gnn_in = {k: v for k, v in _L3_gnn_all.items() if k in ('W', 'b', 'a', 'ln_w', 'ln_b')}
    del _L3_gnn_all
    return {'x': x, 'src': src, 'dst': dst, 'edge_attr_16': edge_attr_16, 'edge_weight1': edge_weight1, 'L0_gnn_q_w0': _L0_gnn_in['q_w0'], 'L0_gnn_q_b0': _L0_gnn_in['q_b0'], 'L0_gnn_k_w0': _L0_gnn_in['k_w0'], 'L0_gnn_k_b0': _L0_gnn_in['k_b0'], 'L0_gnn_v_w0': _L0_gnn_in['v_w0'], 'L0_gnn_v_b0': _L0_gnn_in['v_b0'], 'L0_gnn_s_w0': _L0_gnn_in['s_w0'], 'L0_gnn_s_b0': _L0_gnn_in['s_b0'], 'L0_gnn_q_w1': _L0_gnn_in['q_w1'], 'L0_gnn_q_b1': _L0_gnn_in['q_b1'], 'L0_gnn_k_w1': _L0_gnn_in['k_w1'], 'L0_gnn_k_b1': _L0_gnn_in['k_b1'], 'L0_gnn_v_w1': _L0_gnn_in['v_w1'], 'L0_gnn_v_b1': _L0_gnn_in['v_b1'], 'L0_gnn_s_w1': _L0_gnn_in['s_w1'], 'L0_gnn_s_b1': _L0_gnn_in['s_b1'], 'L1_gnn_W': _L1_gnn_in['W'], 'L1_gnn_b': _L1_gnn_in['b'], 'L2_gnn_W_enc': _L2_gnn_in['W_enc'], 'L2_gnn_b_enc': _L2_gnn_in['b_enc'], 'L2_gnn_W_ee': _L2_gnn_in['W_ee'], 'L2_gnn_b_ee': _L2_gnn_in['b_ee'], 'L2_gnn_eps': _L2_gnn_in['eps'], 'L2_gnn_W1': _L2_gnn_in['W1'], 'L2_gnn_b1': _L2_gnn_in['b1'], 'L2_gnn_bn_gamma': _L2_gnn_in['bn_gamma'], 'L2_gnn_bn_beta': _L2_gnn_in['bn_beta'], 'L2_gnn_bn_mean': _L2_gnn_in['bn_mean'], 'L2_gnn_bn_var': _L2_gnn_in['bn_var'], 'L2_gnn_W2': _L2_gnn_in['W2'], 'L2_gnn_b2': _L2_gnn_in['b2'], 'L3_gnn_W': _L3_gnn_in['W'], 'L3_gnn_b': _L3_gnn_in['b'], 'L3_gnn_a': _L3_gnn_in['a'], 'L3_gnn_ln_w': _L3_gnn_in['ln_w'], 'L3_gnn_ln_b': _L3_gnn_in['ln_b']}

def reference(x, src, dst, edge_attr_16, edge_weight1, L0_gnn_q_w0, L0_gnn_q_b0, L0_gnn_k_w0, L0_gnn_k_b0, L0_gnn_v_w0, L0_gnn_v_b0, L0_gnn_s_w0, L0_gnn_s_b0, L0_gnn_q_w1, L0_gnn_q_b1, L0_gnn_k_w1, L0_gnn_k_b1, L0_gnn_v_w1, L0_gnn_v_b1, L0_gnn_s_w1, L0_gnn_s_b1, L1_gnn_W, L1_gnn_b, L2_gnn_W_enc, L2_gnn_b_enc, L2_gnn_W_ee, L2_gnn_b_ee, L2_gnn_eps, L2_gnn_W1, L2_gnn_b1, L2_gnn_bn_gamma, L2_gnn_bn_beta, L2_gnn_bn_mean, L2_gnn_bn_var, L2_gnn_W2, L2_gnn_b2, L3_gnn_W, L3_gnn_b, L3_gnn_a, L3_gnn_ln_w, L3_gnn_ln_b):
    import jax
    import jax.numpy as jnp

    def _L0_gnn_ref(x, edge_index, edge_attr, q_w0, q_b0, k_w0, k_b0, v_w0, v_b0, s_w0, s_b0, q_w1, q_b1, k_w1, k_b1, v_w1, v_b1, s_w1, s_b1):
        import jax, jax.numpy as jnp
        import numpy as np
        import math
        HEADS = 8
        CH = 16
        SCALE = 1.0 / math.sqrt(CH)

        def _transformer_conv(x, src, dst, qw, qb, kw, kb, vw, vb, sw, sb):
            N = x.shape[0]
            q = (x @ qw + qb).reshape(N, HEADS, CH)
            k = (x @ kw + kb).reshape(N, HEADS, CH)
            v = (x @ vw + vb).reshape(N, HEADS, CH)
            alpha = jnp.sum(q[dst] * k[src], axis=-1) * SCALE
            m = jax.ops.segment_max(alpha, dst, num_segments=N)
            a = jnp.exp(alpha - m[dst])
            denom = jax.ops.segment_sum(a, dst, num_segments=N)
            a = a / denom[dst]
            msg = v[src] * a[:, :, None]
            out = jax.ops.segment_sum(msg, dst, num_segments=N).reshape(N, HEADS * CH)
            return out + x @ sw + sb
        src, dst = (edge_index[0], edge_index[1])
        h = _transformer_conv(x, src, dst, q_w0, q_b0, k_w0, k_b0, v_w0, v_b0, s_w0, s_b0)
        h = jax.nn.relu(h)
        h = _transformer_conv(h, src, dst, q_w1, q_b1, k_w1, k_b1, v_w1, v_b1, s_w1, s_b1)
        return h

    def _L1_gnn_ref(x, W, b, row, col):
        import jax, jax.numpy as jnp
        import numpy as np
        N_NODES = 10000
        N_EDGES = 20000
        IN_FEATS = 128
        OUT_FEATS = 128
        n = x.shape[0]
        deg = jax.ops.segment_sum(jnp.ones((row.shape[0],), dtype=x.dtype), row, num_segments=n)
        agg = jax.ops.segment_sum(x[col], row, num_segments=n)
        mean = agg / jnp.maximum(deg, 1.0)[:, None]
        h = jnp.concatenate([x, mean], axis=-1)
        out = h @ W.T + b
        return out

    def _L2_gnn_ref(x, edge_index, batch, edge_attr, edge_atten, W_enc, b_enc, W_ee, b_ee, eps, W1, b1, bn_gamma, bn_beta, bn_mean, bn_var, W2, b2):
        import jax, jax.numpy as jnp
        import numpy as np
        N, E = (50000, 25000)
        X_DIM, EA_DIM, H, L = (128, 16, 128, 3)
        BN_EPS = 1e-05
        h = x @ W_enc + b_enc
        ea = edge_attr @ W_ee + b_ee
        src, dst = (edge_index[0], edge_index[1])
        n = h.shape[0]
        for i in range(L):
            m = jax.nn.relu(h[src] + ea) * edge_atten
            aggr = jax.ops.segment_sum(m, dst, num_segments=n)
            z = (1.0 + eps[i]) * h + aggr
            z = z @ W1[i] + b1[i]
            z = (z - bn_mean[i]) * jax.lax.rsqrt(bn_var[i] + BN_EPS) * bn_gamma[i] + bn_beta[i]
            z = jax.nn.relu(z)
            z = z @ W2[i] + b2[i]
            h = jax.nn.relu(z)
        return h

    def _L3_gnn_ref(x, W, b, a, ln_w, ln_b, edge):
        import jax, jax.numpy as jnp
        import numpy as np
        N = 3125
        E = 100000
        D_IN = 128
        D_OUT = 128
        ALPHA = 0.2
        LN_EPS = 1e-05
        n = x.shape[0]
        d_out = W.shape[0]
        h = x @ W.T + b
        src, dst = (edge[0], edge[1])
        a1, a2 = (a[:d_out], a[d_out:])
        node_s1 = h @ a1
        node_s2 = h @ a2
        z = node_s1[src] + node_s2[dst]
        edge_e = jnp.exp(-jax.nn.leaky_relu(z, ALPHA))
        msgs = edge_e[:, None] * h[dst]
        h_prime = jax.ops.segment_sum(msgs, src, num_segments=n)
        mu = jnp.mean(h_prime, axis=-1, keepdims=True)
        var = jnp.mean(jnp.square(h_prime - mu), axis=-1, keepdims=True)
        h_norm = (h_prime - mu) * jax.lax.rsqrt(var + LN_EPS) * ln_w + ln_b
        return jax.nn.elu(h_norm)
    edge_index = jnp.stack([src, dst])
    batch0 = jnp.zeros((3125,), jnp.int32)
    x = _layernorm(x + _L0_gnn_ref(x, edge_index, edge_weight1, L0_gnn_q_w0, L0_gnn_q_b0, L0_gnn_k_w0, L0_gnn_k_b0, L0_gnn_v_w0, L0_gnn_v_b0, L0_gnn_s_w0, L0_gnn_s_b0, L0_gnn_q_w1, L0_gnn_q_b1, L0_gnn_k_w1, L0_gnn_k_b1, L0_gnn_v_w1, L0_gnn_v_b1, L0_gnn_s_w1, L0_gnn_s_b1), axis=-1)
    x = _layernorm(x + _L1_gnn_ref(x, L1_gnn_W, L1_gnn_b, src, dst), axis=-1)
    x = _layernorm(x + _L2_gnn_ref(x, edge_index, batch0, edge_attr_16, edge_weight1, L2_gnn_W_enc, L2_gnn_b_enc, L2_gnn_W_ee, L2_gnn_b_ee, L2_gnn_eps, L2_gnn_W1, L2_gnn_b1, L2_gnn_bn_gamma, L2_gnn_bn_beta, L2_gnn_bn_mean, L2_gnn_bn_var, L2_gnn_W2, L2_gnn_b2), axis=-1)
    x = _layernorm(x + _L3_gnn_ref(x, L3_gnn_W, L3_gnn_b, L3_gnn_a, L3_gnn_ln_w, L3_gnn_ln_b, edge_index), axis=-1)
    return x

_drawn_inputs = setup_inputs


def setup_inputs(seed=0):
    import zlib

    import numpy as np

    out = dict(_drawn_inputs(seed))
    spreads = {'L0_gnn_q_b0': (0.0, 0.654),
     'L0_gnn_k_b0': (0.0, 2.0),
     'L0_gnn_v_b0': (0.0, 0.323),
     'L0_gnn_s_b0': (0.0, 0.323),
     'L0_gnn_q_b1': (0.0, 2.0),
     'L0_gnn_k_b1': (0.0, 2.0),
     'L0_gnn_v_b1': (0.0, 0.1),
     'L0_gnn_s_b1': (0.0, 0.27),
     'L2_gnn_b_enc': (0.0, 0.8),
     'L2_gnn_b_ee': (0.0, 0.796),
     'L2_gnn_eps': (0.0, 0.8),
     'L2_gnn_b1': (0.0, 2.0),
     'L2_gnn_bn_gamma': (1.0, 0.6),
     'L2_gnn_bn_beta': (0.0, 2.0),
     'L2_gnn_bn_mean': (0.0, 2.0),
     'L2_gnn_bn_var': (1.0, 0.6),
     'L2_gnn_b2': (0.0, 0.8),
     'L3_gnn_b': (0.0, 0.1),
     'L3_gnn_ln_w': (1.0, 0.2),
     'L3_gnn_ln_b': (0.0, 0.1)}
    factors = {'edge_attr_16': 8.0,
     'edge_weight1': 3.742,
     'L2_gnn_W_enc': 8.0,
     'L2_gnn_W_ee': 7.598,
     'L2_gnn_W1': 4.079,
     'L0_gnn_q_w1': 3.091,
     'L1_gnn_b': 3.758}
    for name, (base, spread) in spreads.items():
        noise = np.random.default_rng([zlib.crc32(name.encode()), seed]).standard_normal(out[name].shape)
        drawn = base * np.exp(spread * noise) if base else spread * noise
        out[name] = jnp.asarray(drawn.astype(out[name].dtype))
    for name, factor in factors.items():
        out[name] = (out[name] * factor).astype(out[name].dtype)
    return out
```

```python
from contextlib import ExitStack

import concourse.bass as bass
from concourse import mybir

F32 = mybir.dt.float32
I32 = mybir.dt.int32
ALU = mybir.AluOpType
ACT = mybir.ActivationFunctionType
AX_X = mybir.AxisListType.X

P = 128
N = 3125
E = 100000
D = 128
HEADS = 8
CH = D // HEADS
EA = 16
NT = -(-N // P)
NP = NT * P
TAIL = N - (NT - 1) * P
J = -(-E // P)
JTAIL = E - (P - 1) * J
K = 4
NV = 216
assert P * NV * K >= P * J + (K - 1) * (N + 1) and NV % 4 == 0
NS = NV * K
PHANTOM = NP
ZROW = N
REC = 20
R_W, R_SRC, R_DST, R_ONE = EA, EA + 1, EA + 2, EA + 3
T2 = 808
assert T2 * P >= P * J + NT * (P - 1) and T2 % 8 == 0
ROWS = P * NV
W = D + HEADS
LVROWS = NP + ROWS
HW = D + 4
BIG = 1e37
MASK = 1e30
LN_EPS = 1e-5
SCALE = CH ** -0.5
U = 5
assert NT % U == 0


class Chain:

    def __init__(self, eng, sem):
        self.eng, self.sem, self.n = eng, sem, 0

    def __call__(self, ins):
        self.n += 1
        ins.then_inc(self.sem, 1)
        self.eng.wait_ge(self.sem, self.n)


def build(nc, a, out):
    ctx = ExitStack()
    with ctx:
        def sb(name, cols, dt=F32, parts=P):
            return ctx.enter_context(nc.sbuf_tensor(name, [parts, cols], dt))

        def sem(name):
            return ctx.enter_context(nc.semaphore(name))

        def dram(name, shape, dt=F32):
            return nc.dram_tensor(name, shape, dt, kind="Internal").ap()

        ident, shift_in, shift_back, upper, ones = (sb(n, P) for n in ("ident", "shift_in", "shift_back", "upper", "ones"))
        x = sb("x", NT * D)
        skip = sb("skip", NT * D)
        x3 = x[:, :].rearrange("p (t d) -> p t d", d=D)
        skip3 = skip[:, :].rearrange("p (t d) -> p t d", d=D)
        sums = sb("sums", (NV + 1) * W)
        sums3 = sums[:, :].rearrange("p (j f) -> p j f", f=W)
        ring = sb("ring", 4 * K * 2 * D)
        qring = sb("qring", 4 * D)
        prod = sb("prod", 2 * K * D)
        pv = sb("pv", 2 * K * D)
        rowmax = sb("rowmax", NV * HEADS)
        src_idx = sb("src_idx", NS + 16, I32)
        q_idx = sb("q_idx", NV + 4, I32)
        weight = sb("weight", NS)
        maskneg = sb("maskneg", NS)
        same, same_l, reset, rnext, fs_neg, ls_neg = (sb(n, NV) for n in ("same", "same_l", "reset", "rnext", "fs_neg", "ls_neg"))
        link_row, cont_row = sb("link_row", P), sb("cont_row", P)
        neg_rows = sb("neg_rows", 4 * P)
        last_idx = sb("last_idx", NT * 2, I32)
        wgt = sb("wgt", 512)
        bias = sb("bias", 512)
        idx_slot = sb("idx_slot", 2 * 2 * K, I32)
        qidx_slot = sb("qidx_slot", 2 * 2, I32)
        small = sb("small", 1200)

        bank = [ctx.enter_context(nc.psum_tensor(f"bank{i}", [P, 512], F32)) for i in range(8)]


        def dma_sems(*names):
            count[0] += 1
            return [sem(f"{n}_{count[0]}") for n in names]

        count = [0]

        def fresh(ph, *names):
            count[0] += 1
            sems = [nc.alloc_semaphore(f"{n}_{count[0]}") for n in names]

            def retire():
                for s in sems:
                    nc.gpsimd.sem_clear(s)
                    nc.release_semaphore(s)
            ph.callback(retire)
            return sems

        recs = dram("recs", (P * NS, REC))
        recs2 = dram("recs2", (P * T2, 2))
        last_tab = dram("last_tab", (LVROWS, 2), I32)
        q_tab = dram("q_tab", (NP, D))
        kv_tab = dram("kv_tab", (NP, 2 * D))
        h_tab = dram("h_tab", (NP, D))
        g_tab = dram("g_tab", (NP, HW))
        s1_tab = dram("s1_tab", (1, NP))
        sums_tab = dram("sums_tab", (ROWS + 1, W))
        carry_tab = dram("carry_tab", (P + 1, W))

        def area(off, cols):
            return sums[:, off:off + cols]

        agg = area(0, NT * W).rearrange("p (t f) -> p t f", f=W)
        car = area(NT * W, NT * W).rearrange("p (t f) -> p t f", f=W)
        work = area(2 * NT * W, NT * D)
        work3 = work.rearrange("p (t d) -> p t d", d=D)
        proj3 = area(10000, NT * 384).rearrange("p (t d) -> p t d", d=384)
        sq = area(19600, NT * D)
        sq3 = sq.rearrange("p (t d) -> p t d", d=D)
        col25 = area(22800, 4 * NT)
        stage_in = ring[:, 0:U * D]
        stage_in2 = ring[:, U * D:2 * U * D]
        stage_T = ring[:, 2 * U * D:3 * U * D]
        stage_T2 = ring[:, 3 * U * D:4 * U * D]
        stage_y = ring[:, 4 * U * D:5 * U * D]

        def table(t, cols=None):
            return t.rearrange("(t p) c -> p t c", p=P)

        f = lambda k: area(REC * J + k * J, J)
        rec3 = area(0, REC * J).rearrange("p (j c) -> p j c", c=REC)
        dst_i, src_i = (f(k).bitcast(I32) for k in (0, 1))
        eidx, d1, start, seg, pad, cum = (f(k) for k in (2, 3, 4, 5, 6, 7))
        t0, t1, t2, t3 = (f(k) for k in (8, 9, 10, 11))
        win_f = f(12)
        rec2 = area(REC * J + 13 * J, 2 * J)
        PIECE = 200
        pieces = [(lo, min(lo + PIECE, J)) for lo in range(0, J, PIECE)]
        ea_stage = (skip[:, 0:PIECE * EA], ring[:, 0:PIECE * EA])
        recfill = ring[:, 0:108 * REC]
        rec2fill = ring[:, 108 * REC:108 * REC + 2 * T2]
        assert 108 * 8 == NS and 108 * REC + 2 * T2 <= 4 * K * 2 * D
        lastfill = small[:, 0:50].bitcast(I32)
        zrow = small[:, 64:64 + W]
        rows129 = small[0:1, 256:256 + P + 1]
        colA = small[:, 400:430]
        bcol = small[:, 430:456]
        pos_idx = f(14)
        pos1 = pad.bitcast(I32)
        with ExitStack() as ph:
            fills_ready, loads, fills_out, setup, pool_step = fresh(ph, "fills_ready", "loads0", "fills_out", "setup0", "pool_step0")
            with nc.Block() as block:
                @block.gpsimd
                def _(pool):
                    link = Chain(pool, pool_step)
                    for m, base, cm, step in ((ident, 0, 1, -1), (shift_in, -1, -1, 1), (shift_back, 1, -1, 1)):
                        link(nc.gpsimd.memset(m[:, :], 0.0))
                        link(nc.gpsimd.affine_select(out=m[:, :], in_=m[:, :], compare_op=ALU.not_equal, fill=1.0, base=base, pattern=[[step, P]], channel_multiplier=cm))
                    link(nc.gpsimd.memset(ones[:, :], 1.0))
                    link(nc.gpsimd.affine_select(out=upper[:, :], in_=ones[:, :], compare_op=ALU.is_gt, fill=0.0, base=0, pattern=[[1, P]], channel_multiplier=-1))
                    link(nc.gpsimd.iota(eidx, pattern=[[1, J]], base=0, channel_multiplier=J, allow_small_or_imprecise_dtypes=True))

                @block.vector
                def _(dve):
                    link = Chain(dve, setup)
                    nc.vector.memset(x[:, (NT - 1) * D:], 0.0).then_inc(fills_ready, 1)
                    nc.vector.memset(dst_i, PHANTOM).then_inc(fills_ready, 1)
                    nc.vector.memset(src_i, ZROW).then_inc(fills_ready, 1)
                    nc.vector.memset(area(0, REC * J), 0.0).then_inc(fills_ready, 1)
                    rf = recfill.rearrange("p (j c) -> p j c", c=REC)
                    link(nc.vector.memset(recfill, 0.0))
                    link(nc.vector.memset(rf[:, :, R_SRC], float(ZROW)))
                    nc.vector.memset(rf[:, :, R_DST], float(PHANTOM)).then_inc(fills_ready, 1)
                    r2 = rec2fill.rearrange("p (j c) -> p j c", c=2)
                    link(nc.vector.memset(r2[:, :, 0], -1.0))
                    nc.vector.memset(r2[:, :, 1], float(NP - 1)).then_inc(fills_ready, 1)
                    lf = lastfill.rearrange("p (j c) -> p j c", c=2)
                    link(nc.vector.memset(lf[:, :, 0], ROWS))
                    nc.vector.memset(lf[:, :, 1], P).then_inc(fills_ready, 1)
                    nc.vector.memset(zrow, 0.0).then_inc(fills_ready, 1)
                    nc.vector.memset(src_idx[:, NS:], 0).then_inc(fills_ready, 1)
                    nc.vector.memset(q_idx[:, NV:], 0).then_inc(fills_ready, 1)

                @block.sync
                def _(sp):
                    sp.wait_ge(fills_ready, 11 - 1)
                    sp.dma_start(x3[:, 0:NT - 1, :], a["x"][0:(NT - 1) * P, :].rearrange("(t p) d -> p t d", p=P)).then_inc(loads, 16)
                    sp.dma_start(x3[0:TAIL, NT - 1, :], a["x"][(NT - 1) * P:N, :]).then_inc(loads, 16)
                    for name, tile in (("dst", dst_i), ("src", src_i)):
                        sp.dma_start(tile[0:P - 1, :], a[name][0:(P - 1) * J].rearrange("(p j) -> p j", j=J)).then_inc(loads, 16)
                        sp.dma_start(tile[P - 1:P, 0:JTAIL], a[name][(P - 1) * J:E].rearrange("(p j) -> p j", p=1)).then_inc(loads, 16)
                    r = recs.rearrange("(p i j) c -> i p (j c)", i=8, j=108)
                    for i in range(8):
                        sp.dma_start(r[i], recfill).then_inc(fills_out, 16)
                    sp.dma_start(recs2.rearrange("(p t) c -> p (t c)", t=T2), rec2fill).then_inc(fills_out, 16)
                    sp.dma_start(last_tab[0:NP, :].rearrange("(p t) c -> p (t c)", p=P), lastfill).then_inc(fills_out, 16)
                    sp.dma_start(sums_tab[ROWS:ROWS + 1, :], zrow[0:1, :]).then_inc(fills_out, 16)
                    sp.dma_start(carry_tab[P:P + 1, :], zrow[0:1, :]).then_inc(fills_out, 16)
                    sp.wait_ge(loads, 6 * 16)
                    sp.wait_ge(fills_out, 12 * 16)

        with ExitStack() as ph:
            rec_step, ea_in0, ea_in1, ea_used, w_in, to_pe, from_pe = fresh(ph, "rec_step", "ea_in0", "ea_in1", "ea_used", "w_in", "to_pe1", "from_pe1")
            ea_v = a["edge_attr"]
            ea_in = (ea_in0, ea_in1)
            wcol = t0
            with nc.Block() as block:
                @block.sync
                def _(sp):
                    sp.wait_ge(rec_step, 3)
                    sp.dma_start(wcol[0:P - 1, :], a["edge_weight"][0:(P - 1) * J].rearrange("(p j) -> p j", j=J)).then_inc(w_in, 16)
                    sp.dma_start(wcol[P - 1:P, 0:JTAIL], a["edge_weight"][(P - 1) * J:E].rearrange("(p j) -> p j", p=1)).then_inc(w_in, 16)
                    full = ea_v[0:(P - 1) * J, :].rearrange("(p j) c -> p (j c)", j=J)
                    tail = ea_v[(P - 1) * J:E, :].rearrange("(p j) c -> p (j c)", p=1)
                    for h, (lo, hi) in enumerate(pieces):
                        st = ea_stage[h % 2]
                        if h >= 2:
                            sp.wait_ge(ea_used, h - 1)
                        n = (min(hi, JTAIL) - lo) * EA
                        sp.dma_start(st[0:P - 1, 0:(hi - lo) * EA], full[:, lo * EA:hi * EA]).then_inc(ea_in[h % 2], 16)
                        sp.dma_start(st[P - 1:P, 0:n], tail[:, lo * EA:lo * EA + n]).then_inc(ea_in[h % 2], 16)

                @block.scalar
                def _(act):
                    for h, (lo, hi) in enumerate(pieces):
                        act.wait_ge(ea_in[h % 2], 32 * (h // 2 + 1))
                        nc.scalar.copy(rec3[:, lo:hi, 0:EA],
                                       ea_stage[h % 2][:, 0:(hi - lo) * EA].rearrange("p (j c) -> p j c", c=EA)).then_inc(ea_used, 1)

                @block.tensor
                def _(pe):
                    pe.wait_ge(to_pe, 1)
                    nc.tensor.matmul(bank[0][:, 0:1], shift_in[:, :], d1[:, J - 1:J], start=True, stop=True).then_inc(from_pe, 1)
                    pe.wait_ge(to_pe, 2)
                    nc.tensor.matmul(bank[1][0:1, 0:P], seg[:, J - 1:J], ident[:, :], start=True, stop=True).then_inc(from_pe, 1)
                    pe.wait_ge(to_pe, 3)
                    nc.tensor.matmul(bank[2][:, 0:1], rows129[:, 0:P], ones[0:1, 0:1], start=True, stop=True).then_inc(from_pe, 1)
                    pe.wait_ge(to_pe, 4)
                    nc.tensor.matmul(bank[3][:, 0:1], shift_in[:, :], seg[:, J - 1:J], start=True, stop=True).then_inc(from_pe, 1)
                    pe.wait_ge(to_pe, 5)
                    nc.tensor.matmul(bank[4][:, 0:1], upper[:, :], cum[:, J - 1:J], start=True, stop=True).then_inc(from_pe, 1)

                @block.vector
                def _(dve):
                    link = Chain(dve, rec_step)
                    link(nc.vector.memset(ea_stage[0], 0.0))
                    link(nc.vector.memset(ea_stage[1], 0.0))
                    link(nc.vector.memset(wcol, 0.0))
                    link(nc.vector.tensor_copy(rec3[:, :, R_DST], dst_i))
                    link(nc.vector.tensor_copy(rec3[:, :, R_SRC], src_i))
                    link(nc.vector.memset(rec3[:, :, R_ONE], 1.0))
                    link(nc.vector.tensor_scalar(d1, rec3[:, :, R_DST], 1.0, None, ALU.add))
                    link(nc.vector.memset(rows129, 0.0))
                    nc.vector.engine_nop().then_inc(to_pe, 1)
                    link(nc.vector.tensor_tensor(start[:, 1:], d1[:, 1:], d1[:, 0:J - 1], ALU.not_equal))
                    dve.wait_ge(from_pe, 1)
                    link(nc.vector.tensor_tensor(start[:, 0:1], d1[:, 0:1], bank[0][:, 0:1], ALU.not_equal))
                    link(nc.vector.tensor_tensor(t1, start, eidx, ALU.mult))
                    link(nc.vector.tensor_tensor_scan(seg, t1, t1, 0.0, ALU.max, ALU.max))
                    nc.vector.engine_nop().then_inc(to_pe, 1)
                    dve.wait_ge(from_pe, 2)
                    link(nc.vector.tensor_copy(t2[0:1, 0:P], bank[1][0:1, 0:P]))
                    link(nc.vector.tensor_tensor_scan(rows129[:, 1:P + 1], t2[0:1, 0:P], t2[0:1, 0:P], 0.0, ALU.max, ALU.max))
                    nc.vector.engine_nop().then_inc(to_pe, 1)
                    dve.wait_ge(from_pe, 3)
                    link(nc.vector.tensor_scalar(seg, seg, bank[2][:, 0:1], None, ALU.max))
                    nc.vector.engine_nop().then_inc(to_pe, 1)
                    link(nc.vector.tensor_tensor(t1[:, 1:], seg[:, 0:J - 1], eidx[:, 1:], ALU.subtract))
                    dve.wait_ge(from_pe, 4)
                    link(nc.vector.tensor_tensor(t1[:, 0:1], bank[3][:, 0:1], eidx[:, 0:1], ALU.subtract))
                    link(nc.vector.tensor_copy(t2.bitcast(I32), t1))
                    link(nc.vector.tensor_scalar(t3.bitcast(I32), t2.bitcast(I32), K - 1, None, ALU.bitwise_and))
                    link(nc.vector.tensor_copy(t2, t3.bitcast(I32)))
                    link(nc.vector.tensor_tensor(pad, start, t2, ALU.mult))
                    link(nc.vector.tensor_tensor_scan(cum, pad, pad, 0.0, ALU.add, ALU.max))
                    nc.vector.engine_nop().then_inc(to_pe, 1)
                    dve.wait_ge(from_pe, 5)
                    link(nc.vector.tensor_copy(colA[:, 0:1], bank[4][:, 0:1]))
                    link(nc.vector.scalar_tensor_tensor(pos1, cum, colA[:, 0:1], eidx, ALU.add, ALU.add))
                    dve.wait_ge(w_in, 32)
                    link(nc.vector.tensor_copy(rec3[:, :, R_W], wcol))

        def scatter_loop(nc, pool, act, eng, cols, chunk, rec, width, dt, pos, stage, pos_stage, table_ap, ready, done):
            steps = cols // (2 * chunk)
            assert steps * 2 * chunk == cols
            if eng == "act":
                with nc.scalar.Fori(0, steps) as i:
                    for u in range(2):
                        act.wait_ge(done[u], 16 * chunk * i)
                        nc.scalar.copy(stage[:, u * chunk * width:(u + 1) * chunk * width],
                                       rec[:, bass.ds((2 * i + u) * chunk * width, chunk * width)]).then_inc(ready, 1)
                        nc.scalar.copy(pos_stage[:, u * chunk:(u + 1) * chunk],
                                       pos[:, bass.ds((2 * i + u) * chunk, chunk)]).then_inc(ready, 1)
            else:
                with nc.gpsimd.Fori(0, steps) as i:
                    for u in range(2):
                        pool.wait_ge(ready, 4 * i + 2 * u + 2)
                        nc.gpsimd.nop(nofuse=True)
                        for c in range(chunk):
                            k = u * chunk + c
                            nc.gpsimd.indirect_dma_start(
                                out=table_ap, out_offset=bass.IndirectOffsetOnAxis(ap=pos_stage[:, k:k + 1], axis=0),
                                in_=stage[:, k * width:(k + 1) * width], in_offset=None).then_inc(done[u], 16)

        CHUNK = 17
        stage1 = ring[:, 0:2 * CHUNK * REC]
        pstage1 = ring[:, 1000:1000 + 2 * CHUNK].bitcast(I32)
        stage2 = ring[:, 1100:1100 + 2 * CHUNK * 2]
        pstage2 = ring[:, 1300:1300 + 2 * CHUNK].bitcast(I32)
        window = sb("window", T2, I32, parts=1)
        iota_t = ring[:, 2000:2000 + T2]
        nacc = ring[:, 2900:2900 + T2]
        cnt = small[:, 460:486]
        tot = small[:, 490:516]
        incl = small[:, 520:546]
        offs = small[:, 550:576]
        tmp25 = small[:, 580:606]
        tmp25b = small[:, 610:636]
        with ExitStack() as ph:
            d10, d11, d20, d21 = dma_sems("rec_out0", "rec_out1", "rec2_out0", "rec2_out1")
            ready1, ready2, bucket, to_pe, from_pe, pos2_ready, iotas = fresh(ph, "rec_staged", "rec2_staged", "bucket", "to_pe2", "from_pe2", "pos2_ready", "iotas2")
            steps = J // (2 * CHUNK)
            r1 = area(0, REC * J)
            pos2 = pos_idx.bitcast(I32)
            winf, acc, oh, sc = t0, t1, t2, t3
            pos2 = cum.bitcast(I32)
            with nc.Block() as block:
                @block.scalar
                def _(act):
                    scatter_loop(nc, None, act, "act", J, CHUNK, r1, REC, F32, pos1, stage1, pstage1, recs, ready1, (d10, d11))
                    act.wait_ge(pos2_ready, 1)
                    scatter_loop(nc, None, act, "act", J, CHUNK, rec2, 2, F32, pos2, stage2, pstage2, recs2, ready2, (d20, d21))

                @block.gpsimd
                def _(pool):
                    nc.gpsimd.iota(bcol, pattern=[[1, 26]], base=0, channel_multiplier=0, allow_small_or_imprecise_dtypes=True).then_inc(iotas, 1)
                    nc.gpsimd.iota(iota_t, pattern=[[1, T2]], base=0, channel_multiplier=0, allow_small_or_imprecise_dtypes=True).then_inc(iotas, 1)
                    scatter_loop(nc, pool, None, "pool", J, CHUNK, r1, REC, F32, pos1, stage1, pstage1, recs, ready1, (d10, d11))
                    scatter_loop(nc, pool, None, "pool", J, CHUNK, rec2, 2, F32, pos2, stage2, pstage2, recs2, ready2, (d20, d21))
                    for d in (d10, d11, d20, d21):
                        pool.wait_ge(d, 16 * CHUNK * steps)

                @block.tensor
                def _(pe):
                    pe.wait_ge(to_pe, 1)
                    nc.tensor.matmul(bank[0][:, 0:NT], upper[:, :], cnt[:, 0:NT], start=True, stop=True).then_inc(from_pe, 1)
                    nc.tensor.matmul(bank[1][:, 0:NT], ones[:, :], cnt[:, 0:NT], start=True, stop=True).then_inc(from_pe, 1)

                @block.vector
                def _(dve):
                    link = Chain(dve, bucket)
                    r2 = rec2.rearrange("p (j c) -> p j c", c=2)
                    dve.wait_ge(iotas, 2)
                    link(nc.vector.tensor_copy(r2[:, :, 0], src_i))
                    link(nc.vector.tensor_copy(winf, dst_i))
                    link(nc.vector.tensor_scalar(r2[:, :, 1], winf, float(NP - 1), None, ALU.min))
                    link(nc.vector.tensor_scalar(oh.bitcast(I32), src_i, 7, None, ALU.arith_shift_right))
                    link(nc.vector.tensor_copy(winf, oh.bitcast(I32)))
                    link(nc.vector.memset(acc, 0.0))
                    base = link.n
                    with nc.vector.Fori(0, NT) as b:
                        nc.vector.tensor_scalar(oh, winf, bcol[:, bass.ds(b, 1)], None, ALU.is_equal).then_inc(bucket, 1)
                        dve.wait_ge(bucket, base + 5 * b + 1)
                        nc.vector.tensor_tensor_scan(sc, oh, oh, 0.0, ALU.add, ALU.max).then_inc(bucket, 1)
                        dve.wait_ge(bucket, base + 5 * b + 2)
                        nc.vector.tensor_copy(cnt[:, bass.ds(b, 1)], sc[:, J - 1:J]).then_inc(bucket, 1)
                        nc.vector.tensor_tensor(oh, oh, sc, ALU.mult).then_inc(bucket, 1)
                        dve.wait_ge(bucket, base + 5 * b + 4)
                        nc.vector.tensor_tensor(acc, acc, oh, ALU.add).then_inc(bucket, 1)
                        dve.wait_ge(bucket, base + 5 * b + 5)
                    link.n += 5 * NT
                    nc.vector.engine_nop().then_inc(to_pe, 1)
                    dve.wait_ge(from_pe, 2)
                    link(nc.vector.tensor_copy(tot[:, 0:NT], bank[1][:, 0:NT]))
                    link(nc.vector.tensor_scalar(tmp25.bitcast(I32)[:, 0:NT], tot[:, 0:NT], float(P - 1), None, ALU.add))
                    link(nc.vector.tensor_scalar(tmp25b.bitcast(I32)[:, 0:NT], tmp25.bitcast(I32)[:, 0:NT], 7, None, ALU.arith_shift_right))
                    link(nc.vector.tensor_copy(tmp25[:, 0:NT], tmp25b.bitcast(I32)[:, 0:NT]))
                    link(nc.vector.tensor_tensor_scan(incl[:, 0:NT], tmp25[:, 0:NT], tmp25[:, 0:NT], 0.0, ALU.add, ALU.max))
                    link(nc.vector.tensor_tensor(tmp25[:, 0:NT], incl[:, 0:NT], tmp25[:, 0:NT], ALU.subtract))
                    link(nc.vector.tensor_scalar(tmp25[:, 0:NT], tmp25[:, 0:NT], float(P), -1.0, ALU.mult, ALU.add))
                    link(nc.vector.tensor_tensor(offs[:, 0:NT], bank[0][:, 0:NT], tmp25[:, 0:NT], ALU.add))
                    base2 = link.n
                    with nc.vector.Fori(0, NT) as b:
                        nc.vector.tensor_scalar(oh, winf, bcol[:, bass.ds(b, 1)], offs[:, bass.ds(b, 1)], ALU.is_equal, ALU.mult).then_inc(bucket, 1)
                        dve.wait_ge(bucket, base2 + 2 * b + 1)
                        nc.vector.tensor_tensor(acc, acc, oh, ALU.add).then_inc(bucket, 1)
                        dve.wait_ge(bucket, base2 + 2 * b + 2)
                    link.n += 2 * NT
                    link(nc.vector.tensor_copy(oh.bitcast(I32), acc))
                    link(nc.vector.tensor_scalar(sc.bitcast(I32), oh.bitcast(I32), 7, None, ALU.arith_shift_right))
                    link(nc.vector.tensor_copy(acc, sc.bitcast(I32)))
                    link(nc.vector.tensor_scalar(sc.bitcast(I32), oh.bitcast(I32), P - 1, None, ALU.bitwise_and))
                    link(nc.vector.tensor_copy(winf, sc.bitcast(I32)))
                    link(nc.vector.scalar_tensor_tensor(pos2, winf, float(T2), acc, ALU.mult, ALU.add))
                    nc.vector.engine_nop().then_inc(pos2_ready, 1)
                    link(nc.vector.memset(nacc, 0.0))
                    base3 = link.n
                    with nc.vector.Fori(0, NT - 1) as b:
                        nc.vector.scalar_tensor_tensor(nacc, iota_t, incl[:, bass.ds(b, 1)], nacc, ALU.is_ge, ALU.add).then_inc(bucket, 1)
                        dve.wait_ge(bucket, base3 + b + 1)
                    link.n += NT - 1
                    link(nc.vector.tensor_copy(window[:, :], nacc[0:1, :]))

        back = area(0, NS * REC)
        back4 = back.rearrange("p (j s c) -> p j s c", s=K, c=REC)
        g = lambda k: area(NS * REC + k * NV, NV)
        vn1, snext, fs, ls, dump, last, vidx, tA, tB = (g(k) for k in range(9))
        rec3w = area(NS * REC + 9 * NV, 2 * NV)
        srows = area(NS * REC + 11 * NV, NS)
        lpos = area(NS * REC + 11 * NV + NS, NV)
        rec3i = rec3w.bitcast(I32)
        stage3 = ring[:, 0:2 * 12 * 2].bitcast(I32)
        pstage3 = ring[:, 100:124].bitcast(I32)
        with ExitStack() as ph:
            d30, d31 = dma_sems("last_out0", "last_out1")
            back_in, row_step, to_pe, from_pe, iotas, ready3, tab_in = fresh(ph, "back_in", "row_step", "to_pe3", "from_pe3", "iotas3", "last_staged", "last_in")
            lane_m = small[:, 702:703]
            colB = small[:, 710:730]
            with nc.Block() as block:
                @block.sync
                def _(sp):
                    sp.dma_start(back, recs.rearrange("(p j) c -> p (j c)", j=NS)).then_inc(back_in, 16)
                    sp.wait_ge(d30, 16 * NV // 2)
                    sp.wait_ge(d31, 16 * NV // 2)
                    sp.dma_start(last_idx[:, :].rearrange("p (t c) -> p t c", c=2), table(last_tab[0:NP, :])).then_inc(tab_in, 16)
                    sp.wait_ge(tab_in, 16)

                @block.gpsimd
                def _(pool):
                    nc.gpsimd.iota(lane_m, pattern=[[0, 1]], base=-P, channel_multiplier=1, allow_small_or_imprecise_dtypes=True).then_inc(iotas, 1)
                    nc.gpsimd.iota(vidx, pattern=[[1, NV]], base=0, channel_multiplier=NV, allow_small_or_imprecise_dtypes=True).then_inc(iotas, 1)
                    scatter_loop(nc, pool, None, "pool", NV, 12, rec3i, 2, I32, lpos.bitcast(I32), stage3, pstage3, last_tab, ready3, (d30, d31))

                @block.scalar
                def _(act):
                    act.wait_ge(to_pe, 8)
                    scatter_loop(nc, None, act, "act", NV, 12, rec3i, 2, I32, lpos.bitcast(I32), stage3, pstage3, last_tab, ready3, (d30, d31))

                @block.tensor
                def _(pe):
                    pe.wait_ge(to_pe, 1)
                    nc.tensor.matmul(bank[0][:, 0:1], shift_in[:, :], vn1[:, NV - 1:NV], start=True, stop=True).then_inc(from_pe, 1)
                    pe.wait_ge(to_pe, 2)
                    nc.tensor.matmul(bank[1][:, 0:1], shift_back[:, :], same[:, 0:1], start=True, stop=True).then_inc(from_pe, 1)
                    pe.wait_ge(to_pe, 3)
                    nc.tensor.matmul(bank[2][:, 0:1], shift_in[:, :], fs[:, NV - 1:NV], start=True, stop=True).then_inc(from_pe, 1)
                    nc.tensor.matmul(bank[3][:, 0:1], shift_back[:, :], ls[:, 0:1], start=True, stop=True).then_inc(from_pe, 1)
                    for k in range(4):
                        pe.wait_ge(to_pe, 4 + k)
                        nc.tensor.matmul(bank[4 + k][:, 0:P], srows[:, k * P:(k + 1) * P], ident[:, :], start=True, stop=True).then_inc(from_pe, 1)

                @block.vector
                def _(dve):
                    link = Chain(dve, row_step)
                    dve.wait_ge(iotas, 2)
                    dve.wait_ge(back_in, 16)
                    link(nc.vector.tensor_copy(src_idx[:, 0:NS], back4[:, :, :, R_SRC].rearrange("p j s -> p (j s)")))
                    link(nc.vector.tensor_copy(weight[:, :], back4[:, :, :, R_W].rearrange("p j s -> p (j s)")))
                    link(nc.vector.tensor_scalar(maskneg[:, :], back4[:, :, :, R_SRC].rearrange("p j s -> p (j s)"), float(ZROW), -MASK, ALU.is_ge, ALU.mult))
                    link(nc.vector.tensor_scalar(vn1, back4[:, :, 0, R_DST], 1.0, None, ALU.add))
                    nc.vector.engine_nop().then_inc(to_pe, 1)
                    link(nc.vector.tensor_scalar(q_idx[:, 0:NV], back4[:, :, 0, R_DST], float(NP - 1), None, ALU.min))
                    link(nc.vector.tensor_tensor(same[:, 1:], vn1[:, 1:], vn1[:, 0:NV - 1], ALU.is_equal))
                    dve.wait_ge(from_pe, 1)
                    link(nc.vector.tensor_tensor(same[:, 0:1], vn1[:, 0:1], bank[0][:, 0:1], ALU.is_equal))
                    nc.vector.engine_nop().then_inc(to_pe, 1)
                    link(nc.vector.tensor_copy(same_l[:, 1:], same[:, 1:]))
                    link(nc.vector.memset(same_l[:, 0:1], 0.0))
                    link(nc.vector.tensor_scalar(reset[:, :], same_l[:, :], -1.0, BIG, ALU.add, ALU.mult))
                    link(nc.vector.tensor_copy(snext[:, 0:NV - 1], same[:, 1:]))
                    dve.wait_ge(from_pe, 2)
                    link(nc.vector.tensor_copy(snext[:, NV - 1:NV], bank[1][:, 0:1]))
                    link(nc.vector.tensor_scalar(rnext[:, :], snext, -1.0, BIG, ALU.add, ALU.mult))
                    link(nc.vector.memset(rnext[:, NV - 1:NV], -BIG))
                    link(nc.vector.tensor_tensor_scan(fs, same[:, :], same[:, :], 1.0, ALU.mult, ALU.min))
                    link(nc.vector.tensor_tensor_scan(ls[:, ::-1], snext[:, ::-1], snext[:, ::-1], 1.0, ALU.mult, ALU.min))
                    nc.vector.engine_nop().then_inc(to_pe, 1)
                    link(nc.vector.tensor_scalar(fs_neg[:, :], fs, -1.0, BIG, ALU.add, ALU.mult))
                    link(nc.vector.tensor_scalar(ls_neg[:, :], ls, -1.0, BIG, ALU.add, ALU.mult))
                    dve.wait_ge(from_pe, 4)
                    link(nc.vector.tensor_copy(colB[:, 0:1], same[:, 0:1]))
                    link(nc.vector.tensor_tensor(colB[:, 1:2], same[:, 0:1], bank[2][:, 0:1], ALU.mult))
                    link(nc.vector.tensor_copy(colB[:, 2:3], snext[:, NV - 1:NV]))
                    link(nc.vector.tensor_tensor(colB[:, 3:4], snext[:, NV - 1:NV], bank[3][:, 0:1], ALU.mult))
                    for k in range(4):
                        link(nc.vector.tensor_scalar(srows[:, k * P:(k + 1) * P], ones[:, :], colB[:, k:k + 1], None, ALU.mult))
                        nc.vector.engine_nop().then_inc(to_pe, 1)
                    dve.wait_ge(from_pe, 8)
                    link(nc.vector.tensor_copy(link_row[:, :], bank[4][:, 0:P]))
                    link(nc.vector.tensor_copy(cont_row[:, :], bank[5][:, 0:P]))
                    for k in range(4):
                        link(nc.vector.tensor_scalar(neg_rows[:, k * P:(k + 1) * P], bank[4 + k][:, 0:P], -1.0, BIG, ALU.add, ALU.mult))
                    link(nc.vector.tensor_scalar(last, snext, -1.0, -1.0, ALU.add, ALU.mult))
                    link(nc.vector.tensor_scalar(dump, vidx, float(NP), None, ALU.add))
                    link(nc.vector.scalar_tensor_tensor(tA, vn1, -1.0, dump, ALU.add, ALU.subtract))
                    link(nc.vector.tensor_tensor(tA, tA, last, ALU.mult))
                    link(nc.vector.tensor_tensor(lpos.bitcast(I32), tA, dump, ALU.add))
                    r3 = rec3i.rearrange("p (j c) -> p j c", c=2)
                    link(nc.vector.tensor_copy(r3[:, :, 0], vidx))
                    link(nc.vector.tensor_scalar(tB, fs, lane_m, None, ALU.mult))
                    link(nc.vector.tensor_scalar(r3[:, :, 1], tB, float(P), None, ALU.add))
                    nc.vector.engine_nop().then_inc(to_pe, 1)

        STEPS = NV // 4

        def index_copies(act, i, half, with_q):
            nc.scalar.copy(idx_slot[:, half * 2 * K:(half + 1) * 2 * K], src_idx[:, bass.ds(4 * K * i + 2 * K * half, 2 * K)] if not isinstance(i, int)
                           else src_idx[:, 4 * K * i + 2 * K * half:4 * K * i + 2 * K * half + 2 * K]).then_inc(with_q[0], 1)
            if len(with_q) > 1:
                nc.scalar.copy(qidx_slot[:, half * 2:(half + 1) * 2], q_idx[:, bass.ds(4 * i + 2 * half, 2)] if not isinstance(i, int)
                               else q_idx[:, 4 * i + 2 * half:4 * i + 2 * half + 2]).then_inc(with_q[0], 1)

        def gather_step(tab, width, u, slot_in, q):
            for s in range(K):
                nc.gpsimd.indirect_dma_start(
                    out=ring[:, (u * K + s) * width:(u * K + s + 1) * width], out_offset=None, in_=tab,
                    in_offset=bass.IndirectOffsetOnAxis(ap=idx_slot[:, u * K + s:u * K + s + 1], axis=0)).then_inc(slot_in[u], 16)
            if q:
                nc.gpsimd.indirect_dma_start(
                    out=qring[:, u * D:(u + 1) * D], out_offset=None, in_=q_tab,
                    in_offset=bass.IndirectOffsetOnAxis(ap=qidx_slot[:, u:u + 1], axis=0)).then_inc(slot_in[u], 16)

        def conv_edges():
            with ExitStack() as ph:
                s0, s1, s2, s3 = dma_sems("slot0", "slot1", "slot2", "slot3")
                idx_ready, dve_step, exp_done, cleared = fresh(ph, "idx_ready", "dve_step", "exp_done", "cleared")
                slot_in = (s0, s1, s2, s3)
                PER = 16 * (K + 1)
                OPS = 8
                kv = ring[:, :].rearrange("p (u s c) -> p u s c", u=4, s=K)
                al = small[:, 0:2 * 3 * K * HEADS].rearrange("p (r k c) -> p r k c", r=2, k=3)
                ex = small[:, 256:256 + 2 * K * HEADS].rearrange("p (r c) -> p r c", r=2)
                with nc.Block() as block:
                    @block.gpsimd
                    def _(pool):
                        pool.wait_ge(idx_ready, 4)
                        for u in range(4):
                            if u == 3:
                                pool.wait_ge(dve_step, 2)
                            gather_step(kv_tab, 2 * D, u, slot_in, True)
                        with nc.gpsimd.Fori(1, STEPS) as i:
                            for u in range(4):
                                if u % 2 == 0:
                                    pool.wait_ge(idx_ready, 4 * i + 2 * (u // 2) + 2)
                                    nc.gpsimd.nop(nofuse=True)
                                pool.wait_ge(dve_step, OPS * (4 * i + u - 3) + 2)
                                nc.gpsimd.nop(nofuse=True)
                                gather_step(kv_tab, 2 * D, u, slot_in, True)

                    @block.scalar
                    def _(act):
                        for half in range(2):
                            index_copies(act, 0, half, (idx_ready, True))
                        with nc.scalar.Fori(0, STEPS) as i:
                            for u in range(4):
                                act.wait_ge(dve_step, OPS * (4 * i + u + 1))
                                nc.scalar.activation(ex[:, u % 2, :], al[:, u % 2, 2, :], ACT.Exp).then_inc(exp_done, 1)
                                if u % 2 == 1:
                                    act.wait_ge(slot_in[u - 1], PER * (i + 1))
                                    act.wait_ge(slot_in[u], PER * (i + 1))
                                    index_copies(act, i + 1, u // 2, (idx_ready, True))

                    @block.vector
                    def _(dve):
                        nc.vector.memset(kv[:, 3, :, :], 0.0).then_inc(cleared, 1)
                        nc.vector.memset(ex[:, 1, :], 0.0).then_inc(cleared, 1)
                        dve.wait_ge(cleared, 2)

                        def weigh(u, at, k):
                            w = (u - 1) % 4
                            nc.vector.tensor_tensor(
                                pv[:, (u - 1) % 2 * K * D:((u - 1) % 2 + 1) * K * D].rearrange("p (s h c) -> p s h c", s=K, h=HEADS),
                                kv[:, w, :, D:].rearrange("p s (h c) -> p s h c", h=HEADS),
                                ex[:, (u - 1) % 2, :].rearrange("p (s h) -> p s h", s=K).unsqueeze(3).to_broadcast([P, K, HEADS, CH]),
                                ALU.mult).then_inc(dve_step, 1)

                        def add_up(u, at, first):
                            dve.wait_ge(dve_step, first)
                            nc.vector.tensor_reduce(sums[:, bass.ds(at * W, D)],
                                                    pv[:, (u - 1) % 2 * K * D:((u - 1) % 2 + 1) * K * D].rearrange("p (s f) -> p f s", s=K), AX_X, ALU.add).then_inc(dve_step, 1)
                            nc.vector.tensor_reduce(sums[:, bass.ds(at * W + D, HEADS)],
                                                    ex[:, (u - 1) % 2, :].rearrange("p (s h) -> p h s", s=K), AX_X, ALU.add).then_inc(dve_step, 1)

                        with nc.vector.Fori(0, STEPS) as i:
                            for u in range(4):
                                t = 4 * i + u
                                r = u % 2
                                done = OPS * t
                                pr = prod[:, r * K * D:(r + 1) * K * D]
                                dve.wait_ge(slot_in[u], PER * (i + 1))
                                nc.vector.tensor_tensor(pr.rearrange("p (s c) -> p s c", s=K), kv[:, u, :, 0:D],
                                                        qring[:, u * D:(u + 1) * D].unsqueeze(1).to_broadcast([P, K, D]), ALU.mult).then_inc(dve_step, 1)
                                dve.wait_ge(exp_done, t)
                                weigh(u, t, 2)
                                dve.wait_ge(dve_step, done + 1)
                                nc.vector.tensor_reduce(al[:, r, 0, :], pr.rearrange("p (a c) -> p a c", c=CH), AX_X, ALU.add).then_inc(dve_step, 1)
                                add_up(u, t, done + 2)
                                a0 = al[:, r, 0, :].rearrange("p (s h) -> p s h", s=K)
                                a1 = al[:, r, 1, :].rearrange("p (s h) -> p s h", s=K)
                                a2 = al[:, r, 2, :].rearrange("p (s h) -> p s h", s=K)
                                dve.wait_ge(dve_step, done + 3)
                                nc.vector.scalar_tensor_tensor(a1, a0, SCALE, maskneg[:, bass.ds(t * K, K)].unsqueeze(2).to_broadcast([P, K, HEADS]),
                                                               ALU.mult, ALU.add).then_inc(dve_step, 1)
                                dve.wait_ge(dve_step, done + 6)
                                nc.vector.tensor_reduce(rowmax[:, bass.ds(t * HEADS, HEADS)], al[:, r, 1, :].rearrange("p (s h) -> p h s", s=K), AX_X, ALU.max).then_inc(dve_step, 1)
                                dve.wait_ge(dve_step, done + 7)
                                nc.vector.tensor_tensor(a2, a1, rowmax[:, bass.ds(t * HEADS, HEADS)].unsqueeze(1).to_broadcast([P, K, HEADS]), ALU.subtract).then_inc(dve_step, 1)
                        dve.wait_ge(exp_done, NV)
                        weigh(4, NV, 2)
                        add_up(4, NV, OPS * NV + 1)
                        dve.wait_ge(dve_step, OPS * NV + 3)

        def segment_max():
            with ExitStack() as ph:
                step, to_pe, from_pe, exp_done = fresh(ph, "max_step", "to_pe", "from_pe", "exp_done")
                fwd = ring[:, 0:HEADS * NV].rearrange("p (h j) -> p h j", h=HEADS)
                seg_max = ring[:, HEADS * NV:2 * HEADS * NV].rearrange("p (h j) -> p h j", h=HEADS)
                rm = rowmax[:, :].rearrange("p (j h) -> p j h", h=HEADS)
                ends = small[:, 0:2 * HEADS]
                tails, heads = small[0:HEADS, 32:32 + P + 1], small[0:HEADS, 192:192 + P + 1]
                cf, cb = small[0:HEADS, 352:352 + P], small[0:HEADS, 512:512 + P]
                cfb = small[:, 680:680 + 2 * HEADS]
                with nc.Block() as block:
                    @block.tensor
                    def _(pe):
                        pe.wait_ge(to_pe, 1)
                        nc.tensor.transpose(bank[0][0:HEADS, 0:P], ends[:, 0:HEADS], ident[:, :])
                        nc.tensor.transpose(bank[1][0:HEADS, 0:P], ends[:, HEADS:2 * HEADS], ident[:, :]).then_inc(from_pe, 1)
                        pe.wait_ge(to_pe, 2)
                        nc.tensor.transpose(bank[2][:, 0:HEADS], cf, ident[0:HEADS, 0:HEADS])
                        nc.tensor.transpose(bank[3][:, 0:HEADS], cb, ident[0:HEADS, 0:HEADS]).then_inc(from_pe, 1)

                    @block.scalar
                    def _(act):
                        act.wait_ge(to_pe, 3)
                        nc.scalar.activation(rowmax[:, :], rowmax[:, :], ACT.Exp).then_inc(exp_done, 1)

                    @block.vector
                    def _(dve):
                        link = Chain(dve, step)
                        for h in range(HEADS):
                            link(nc.vector.tensor_tensor_scan(fwd[:, h, :], reset[:, :], rm[:, :, h], -BIG, ALU.add, ALU.max))
                            link(nc.vector.tensor_tensor_scan(seg_max[:, h, ::-1], rnext[:, ::-1], fwd[:, h, ::-1], -BIG, ALU.add, ALU.max))
                        link(nc.vector.tensor_copy(ends[:, 0:HEADS], fwd[:, :, NV - 1]))
                        link(nc.vector.tensor_copy(ends[:, HEADS:], seg_max[:, :, 0]))
                        nc.vector.engine_nop().then_inc(to_pe, 1)
                        link(nc.vector.memset(tails[:, 0:1], 0.0))
                        link(nc.vector.memset(heads[:, P:P + 1], 0.0))
                        dve.wait_ge(from_pe, 1)
                        link(nc.vector.tensor_copy(tails[:, 1:P + 1], bank[0][0:HEADS, 0:P]))
                        link(nc.vector.tensor_copy(heads[:, 0:P], bank[1][0:HEADS, 0:P]))
                        link(nc.vector.tensor_tensor(tails[:, 0:P], tails[:, 0:P], neg_rows[0:HEADS, 0:P], ALU.add))
                        link(nc.vector.tensor_tensor(heads[:, 1:P + 1], heads[:, 1:P + 1], neg_rows[0:HEADS, 2 * P:3 * P], ALU.add))
                        link(nc.vector.tensor_tensor_scan(cf, neg_rows[0:HEADS, P:2 * P], tails[:, 0:P], -BIG, ALU.add, ALU.max))
                        link(nc.vector.tensor_tensor_scan(cb[:, ::-1], neg_rows[0:HEADS, 3 * P:4 * P][:, ::-1], heads[:, 1:P + 1][:, ::-1], -BIG, ALU.add, ALU.max))
                        nc.vector.engine_nop().then_inc(to_pe, 1)
                        dve.wait_ge(from_pe, 2)
                        link(nc.vector.tensor_copy(cfb[:, 0:HEADS], bank[2][:, 0:HEADS]))
                        link(nc.vector.tensor_copy(cfb[:, HEADS:], bank[3][:, 0:HEADS]))
                        for h in range(HEADS):
                            link(nc.vector.scalar_tensor_tensor(seg_max[:, h, :], fs_neg[:, :], cfb[:, h:h + 1], seg_max[:, h, :], ALU.add, ALU.max))
                            link(nc.vector.scalar_tensor_tensor(seg_max[:, h, :], ls_neg[:, :], cfb[:, HEADS + h:HEADS + h + 1], seg_max[:, h, :], ALU.add, ALU.max))
                        link(nc.vector.tensor_tensor(rm, rm, ring[:, HEADS * NV:2 * HEADS * NV].rearrange("p (h j) -> p j h", h=HEADS), ALU.subtract))
                        nc.vector.engine_nop().then_inc(to_pe, 1)
                        dve.wait_ge(exp_done, 1)
                        body = sums3[:, 1:, 0:D].rearrange("p j (h c) -> p j h c", h=HEADS)
                        link(nc.vector.tensor_tensor(body, body, rm.unsqueeze(3).to_broadcast([P, NV, HEADS, CH]), ALU.mult))
                        link(nc.vector.tensor_tensor(sums3[:, 1:, D:], sums3[:, 1:, D:], rm, ALU.mult))
                        base = link.n
                        with nc.vector.Fori(0, W) as c:
                            col = sums3[:, 1:, bass.ds(c, 1)].rearrange("p j o -> p (j o)")
                            nc.vector.tensor_tensor_scan(col, same_l[:, :], col, 0.0, ALU.mult, ALU.add).then_inc(step, 1)
                        dve.wait_ge(step, base + W)

        def carry_and_gather():
            with ExitStack() as ph:
                g_in, c_in = dma_sems("agg_in", "car_in")
                step, to_pe, from_pe, out_done, car_done, carry_ready = fresh(ph, "carry_step", "to_pe", "from_pe", "sums_out", "carry_out", "carry_ready")
                tails = ring[:, 0:P + 1]
                tails8 = ring[0:HEADS, 200:200 + P + 1]
                c_t, c8 = ring[:, 400:400 + P], ring[0:HEADS, 600:600 + P]
                carry = ring[:, 800:800 + W]
                with nc.Block() as block:
                    @block.sync
                    def _(sp):
                        sp.dma_start(sums_tab[0:ROWS, :].rearrange("(p j) f -> p (j f)", j=NV), sums[:, W:]).then_inc(out_done, 16)
                        sp.wait_ge(carry_ready, 1)
                        sp.dma_start(carry_tab[0:P, :], carry).then_inc(car_done, 16)
                        sp.wait_ge(out_done, 16)
                        sp.wait_ge(car_done, 16)

                    @block.tensor
                    def _(pe):
                        nc.tensor.transpose(bank[0][:, 0:P], sums3[:, NV, 0:D], ident[:, :])
                        nc.tensor.transpose(bank[1][0:HEADS, 0:P], sums3[:, NV, D:], ident[:, :]).then_inc(from_pe, 1)
                        pe.wait_ge(to_pe, 1)
                        nc.tensor.transpose(bank[2][:, 0:D], c_t, ident[:, :])
                        nc.tensor.transpose(bank[3][:, 0:HEADS], c8, ident[0:HEADS, 0:HEADS]).then_inc(from_pe, 1)

                    @block.vector
                    def _(dve):
                        link = Chain(dve, step)
                        link(nc.vector.memset(tails[:, 0:1], 0.0))
                        link(nc.vector.memset(tails8[:, 0:1], 0.0))
                        dve.wait_ge(from_pe, 1)
                        link(nc.vector.tensor_copy(tails[:, 1:], bank[0][:, 0:P]))
                        link(nc.vector.tensor_copy(tails8[:, 1:], bank[1][0:HEADS, 0:P]))
                        link(nc.vector.tensor_tensor(tails[:, 0:P], tails[:, 0:P], link_row[:, :], ALU.mult))
                        link(nc.vector.tensor_tensor(tails8[:, 0:P], tails8[:, 0:P], link_row[0:HEADS, :], ALU.mult))
                        link(nc.vector.tensor_tensor_scan(c_t, cont_row[:, :], tails[:, 0:P], 0.0, ALU.mult, ALU.add))
                        link(nc.vector.tensor_tensor_scan(c8, cont_row[0:HEADS, :], tails8[:, 0:P], 0.0, ALU.mult, ALU.add))
                        nc.vector.engine_nop().then_inc(to_pe, 1)
                        dve.wait_ge(from_pe, 2)
                        link(nc.vector.tensor_copy(carry[:, 0:D], bank[2][:, 0:D]))
                        link(nc.vector.tensor_copy(carry[:, D:], bank[3][:, 0:HEADS]))
                        nc.vector.engine_nop().then_inc(carry_ready, 1)
                        dve.wait_ge(g_in, 16 * NT)
                        dve.wait_ge(c_in, 16 * NT)
                        link(nc.vector.tensor_tensor(agg, agg, car, ALU.add))

                    @block.gpsimd
                    def _(pool):
                        pool.wait_ge(out_done, 16)
                        pool.wait_ge(car_done, 16)
                        for t in range(NT):
                            nc.gpsimd.indirect_dma_start(out=agg[:, t, :], out_offset=None, in_=sums_tab,
                                                         in_offset=bass.IndirectOffsetOnAxis(ap=last_idx[:, 2 * t:2 * t + 1], axis=0)).then_inc(g_in, 16)
                            nc.gpsimd.indirect_dma_start(out=car[:, t, :], out_offset=None, in_=carry_tab,
                                                         in_offset=bass.IndirectOffsetOnAxis(ap=last_idx[:, 2 * t + 1:2 * t + 2], axis=0)).then_inc(c_in, 16)

        def norm_ops(link, act_sqrt, src3, dst3, after=None):
            mean, var, inv, tmp = (col25[:, k * NT:(k + 1) * NT] for k in range(4))
            bc = lambda c: c.unsqueeze(2).to_broadcast([P, NT, D])
            link(nc.vector.tensor_reduce(mean, src3, AX_X, ALU.add))
            link(nc.vector.tensor_scalar(mean, mean, 1.0 / D, None, ALU.mult))
            link(nc.vector.tensor_tensor(dst3, src3, bc(mean), ALU.subtract))
            link(nc.vector.tensor_tensor(sq3, dst3, dst3, ALU.mult))
            link(nc.vector.tensor_reduce(var, sq3, AX_X, ALU.add))
            link(nc.vector.tensor_scalar(var, var, 1.0 / D, LN_EPS, ALU.mult, ALU.add))
            act_sqrt(var, tmp)
            link(nc.vector.reciprocal(inv, tmp))
            link(nc.vector.tensor_tensor(dst3, dst3, bc(inv), ALU.mult))

        def node_math(body, roots):
            with ExitStack() as ph:
                step, to_act, from_act = fresh(ph, "math_step", "to_act", "from_act")
                asked = []
                with nc.Block() as block:
                    @block.vector
                    def _(dve):
                        link = Chain(dve, step)

                        def on_act(func):
                            def run(src, dst, **kw):
                                asked.append((func, src, dst, kw))
                                nc.vector.engine_nop().then_inc(to_act, 1)
                                dve.wait_ge(from_act, len(asked))
                            return run
                        body(link, on_act)

                    @block.scalar
                    def _(act):
                        for n, (func, src, dst, kw) in enumerate(roots):
                            act.wait_ge(to_act, n + 1)
                            nc.scalar.activation(dst, src, func, **kw).then_inc(from_act, 1)
                assert [(f, k) for f, _, _, k in asked] == [(f, k) for f, _, _, k in roots]

        SQRT = (ACT.Sqrt, col25[:, NT:2 * NT], col25[:, 3 * NT:4 * NT], {})

        def node_linear(sources, loads, cols, parts, tabs):
            with ExitStack() as ph:
                w_in, staged, tr_done, copied, mm_done, evac, tab_out = fresh(ph, "w_in", "staged", "tr_done", "copied", "mm_done", "evac", "tab_out")
                ins = (stage_in, stage_in2)[:len(sources)]
                outs = (stage_T, stage_T2)[:len(sources)]
                S = len(sources)
                with nc.Block() as block:
                    @block.sync
                    def _(sp):
                        for dst, src in loads:
                            sp.dma_start(dst, src).then_inc(w_in, 16)
                        sp.wait_ge(w_in, 16 * len(loads))
                        sp.wait_ge(evac, NT * len(parts))
                        for dst, src in tabs:
                            sp.dma_start(dst, src).then_inc(tab_out, 16)
                        sp.wait_ge(tab_out, 16 * len(tabs))

                    @block.scalar
                    def _(act):
                        with nc.scalar.Fori(0, NT // U) as i:
                            for s in range(S):
                                act.wait_ge(tr_done, S * i)
                                nc.scalar.copy(ins[s], sources[s][:, bass.ds(U * D * i, U * D)]).then_inc(staged, 1)
                            for s in range(S):
                                act.wait_ge(tr_done, S * i + s + 1)
                                act.wait_ge(mm_done, U * i)
                                nc.scalar.copy(outs[s][:, 0:512], bank[2 * s][:, 0:512]).then_inc(copied, 1)
                                nc.scalar.copy(outs[s][:, 512:U * D], bank[2 * s + 1][:, 0:U * D - 512]).then_inc(copied, 1)

                    @block.tensor
                    def _(pe):
                        pe.wait_ge(w_in, 16 * len(loads))
                        with nc.tensor.Fori(0, NT // U) as i:
                            for s in range(S):
                                pe.wait_ge(staged, S * i + s + 1)
                                pe.wait_ge(copied, 2 * S * i)
                                for u in range(U):
                                    ins_ = nc.tensor.transpose(bank[2 * s + u // 4][:, (u % 4) * P:(u % 4 + 1) * P], ins[s][:, u * D:(u + 1) * D], ident[:, :])
                                ins_.then_inc(tr_done, 1)
                            pe.wait_ge(copied, 2 * S * (i + 1))
                            for u in range(U):
                                b = bank[4 + u % 4]
                                pe.wait_ge(evac, len(parts) * (U * i + max(u - 3, 0)))
                                for s in range(S):
                                    ins_ = nc.tensor.matmul(b[:, 0:cols], outs[s][:, u * D:(u + 1) * D], wgt[:, s * cols:(s + 1) * cols], start=(s == 0), stop=(s == S - 1))
                                ins_.then_inc(mm_done, 1)

                    @block.vector
                    def _(dve):
                        dve.wait_ge(w_in, 16 * len(loads))
                        with nc.vector.Fori(0, NT // U) as i:
                            for u in range(U):
                                dve.wait_ge(mm_done, U * i + u + 1)
                                for dst, stride, lo, hi in parts:
                                    nc.vector.tensor_tensor(dst[:, bass.ds((U * i + u) * stride, hi - lo)], bank[4 + u % 4][:, lo:hi], bias[:, lo:hi], ALU.add).then_inc(evac, 1)

        def gine_edges():
            with ExitStack() as ph:
                s0, s1, s2, s3 = dma_sems("slot0", "slot1", "slot2", "slot3")
                idx_ready, rec_in0, rec_in1, tr_done, rt_done, mm_done, dve_step, relu_done, run0 = fresh(
                    ph, "idx_ready", "rec_in0", "rec_in1", "tr_done", "rt_done", "mm_done", "dve_step", "relu_done", "run0")
                slot_in = (s0, s1, s2, s3)
                rec_in = (rec_in0, rec_in1)
                PER = 16 * K
                KR = K * REC
                recs_r = ring[:, 4 * K * D:4 * K * D + 4 * KR]
                rec_t = ring[:, 4 * K * D + 512:4 * K * D + 512 + 2 * P]
                rv = recs.rearrange("(p j) c -> p (j c)", j=NS)
                with nc.Block() as block:
                    @block.gpsimd
                    def _(pool):
                        pool.wait_ge(idx_ready, 2)
                        for u in range(4):
                            gather_step(h_tab, D, u, slot_in, False)
                        with nc.gpsimd.Fori(1, STEPS) as i:
                            for u in range(4):
                                if u % 2 == 0:
                                    pool.wait_ge(idx_ready, 2 * i + u // 2 + 1)
                                    nc.gpsimd.nop(nofuse=True)
                                pool.wait_ge(dve_step, 4 * (4 * i + u - 3) - 3)
                                nc.gpsimd.nop(nofuse=True)
                                gather_step(h_tab, D, u, slot_in, False)

                    @block.sync
                    def _(sp):
                        with nc.sync.Fori(0, STEPS) as i:
                            for half in range(2):
                                sp.wait_ge(tr_done, 4 * i)
                                sp.dma_start(recs_r[:, half * 2 * KR:(half + 1) * 2 * KR], rv[:, bass.ds((4 * i + 2 * half) * KR, 2 * KR)]).then_inc(rec_in[half], 16)

                    @block.tensor
                    def _(pe):
                        with nc.tensor.Fori(0, STEPS) as i:
                            for u in range(4):
                                t = 4 * i + u
                                if u % 2 == 0:
                                    pe.wait_ge(rec_in[u // 2], 16 * (i + 1))
                                pe.wait_ge(rt_done, 4 * i + max(u - 1, 0))
                                nc.tensor.transpose(bank[u % 2][0:KR, 0:P], recs_r[:, u * KR:(u + 1) * KR], ident[:, :]).then_inc(tr_done, 1)
                                pe.wait_ge(rt_done, t + 1)
                                pe.wait_ge(dve_step, 4 * 4 * i if u < 2 else 4 * (4 * i + u - 1) - 3)
                                nc.tensor.matmul(bank[2 + u % 2][:, 0:K * D], rec_t[0:KR, (u % 2) * P:(u % 2 + 1) * P], wgt[0:KR, 0:K * D], start=True, stop=True).then_inc(mm_done, 1)

                    @block.scalar
                    def _(act):
                        for half in range(2):
                            index_copies(act, 0, half, (idx_ready,))
                        with nc.scalar.Fori(0, STEPS) as i:
                            for u in range(4):
                                t = 4 * i + u
                                act.wait_ge(tr_done, t + 1)
                                act.wait_ge(mm_done, 4 * i + max(u - 1, 0))
                                nc.scalar.copy(rec_t[0:KR, (u % 2) * P:(u % 2 + 1) * P], bank[u % 2][0:KR, 0:P]).then_inc(rt_done, 1)
                                act.wait_ge(dve_step, 4 * t + 1)
                                pr = prod[:, (u % 2) * K * D:(u % 2 + 1) * K * D]
                                nc.scalar.activation(pr, pr, ACT.Relu).then_inc(relu_done, 1)
                                if u % 2 == 1:
                                    act.wait_ge(slot_in[u - 1], PER * (i + 1))
                                    act.wait_ge(slot_in[u], PER * (i + 1))
                                    index_copies(act, i + 1, u // 2, (idx_ready,))

                    @block.vector
                    def _(dve):
                        nc.vector.memset(sums3[:, 0, :], 0.0).then_inc(run0, 1)
                        nc.vector.memset(sums3[:, 1:, D:], 0.0).then_inc(run0, 1)
                        dve.wait_ge(run0, 2)
                        with nc.vector.Fori(0, STEPS) as i:
                            for u in range(4):
                                t = 4 * i + u
                                pr = prod[:, (u % 2) * K * D:(u % 2 + 1) * K * D]
                                pw = pv[:, 0:K * D]
                                tmp = pv[:, K * D:K * D + D]
                                dve.wait_ge(slot_in[u], PER * (i + 1))
                                dve.wait_ge(mm_done, t + 1)
                                nc.vector.tensor_tensor(pr, bank[2 + u % 2][:, 0:K * D], ring[:, u * K * D:(u + 1) * K * D], ALU.add).then_inc(dve_step, 1)
                                dve.wait_ge(relu_done, t + 1)
                                dve.wait_ge(dve_step, 4 * t)
                                nc.vector.tensor_tensor(pw.rearrange("p (s f) -> p s f", s=K), pr.rearrange("p (s f) -> p s f", s=K),
                                                        weight[:, bass.ds(t * K, K)].unsqueeze(2).to_broadcast([P, K, D]), ALU.mult).then_inc(dve_step, 1)
                                dve.wait_ge(dve_step, 4 * t + 2)
                                nc.vector.tensor_reduce(tmp, pw.rearrange("p (s f) -> p f s", s=K), AX_X, ALU.add).then_inc(dve_step, 1)
                                dve.wait_ge(dve_step, 4 * t + 3)
                                nc.vector.scalar_tensor_tensor(sums[:, bass.ds((t + 1) * W, D)], sums[:, bass.ds(t * W, D)], same_l[:, bass.ds(t, 1)], tmp,
                                                               ALU.mult, ALU.add).then_inc(dve_step, 1)
                        dve.wait_ge(dve_step, 4 * NV)

        bn = sb("bn", 5 * 3)
        bnc = sb("bnc", 4 * 3)
        epsb = sb("epsb", 4)

        def gine_nodes(layer):
            with ExitStack() as ph:
                w_in, step, z_ready, staged, tr_done, copied, m1_done, y_done, m2_done, evac, tab_out, root = fresh(
                    ph, "w_in", "mlp_step", "z_ready", "staged", "tr_done", "copied", "m1_done", "y_done", "m2_done", "evac", "tab_out", "root")
                scale, shift = bnc[:, 0:1], bnc[:, 1:2]
                pick = lambda k: bn[:, 3 * k + layer:3 * k + layer + 1]
                with nc.Block() as block:
                    @block.sync
                    def _(sp):
                        sp.dma_start(wgt[:, 0:D], a["L2_W1"][layer]).then_inc(w_in, 16)
                        sp.dma_start(wgt[:, D:2 * D], a["L2_W2"][layer]).then_inc(w_in, 16)
                        sp.dma_start(bias[:, 0:D], a["L2_b2"][layer:layer + 1, :].to_broadcast([P, D])).then_inc(w_in, 16)
                        sp.wait_ge(evac, 2 * NT)
                        sp.dma_start(table(h_tab), skip3).then_inc(tab_out, 16)
                        sp.wait_ge(tab_out, 16)

                    @block.vector
                    def _(dve):
                        link = Chain(dve, step)
                        link(nc.vector.tensor_scalar(epsb[:, 3:4], epsb[:, layer:layer + 1], 1.0, None, ALU.add))
                        link(nc.vector.scalar_tensor_tensor(work3, skip3, epsb[:, 3:4], agg[:, :, 0:D], ALU.mult, ALU.add))
                        nc.vector.engine_nop().then_inc(z_ready, 1)
                        link(nc.vector.tensor_scalar(bnc[:, 2:3], pick(3), LN_EPS, None, ALU.add))
                        nc.vector.engine_nop().then_inc(z_ready, 1)
                        dve.wait_ge(root, 1)
                        link(nc.vector.reciprocal(bnc[:, 2:3], bnc[:, 3:4]))
                        link(nc.vector.tensor_tensor(scale, bnc[:, 2:3], pick(0), ALU.mult))
                        link(nc.vector.tensor_tensor(bnc[:, 4:5], pick(4), pick(2), ALU.subtract))
                        link(nc.vector.scalar_tensor_tensor(shift, bnc[:, 4:5], scale, pick(1), ALU.mult, ALU.add))
                        nc.vector.engine_nop().then_inc(z_ready, 1)
                        dve.wait_ge(w_in, 48)
                        with nc.vector.Fori(0, NT // U) as i:
                            for u in range(U):
                                h = skip[:, bass.ds((U * i + u) * D, D)]
                                dve.wait_ge(m2_done, U * i + u + 1)
                                nc.vector.tensor_tensor(h, bank[4 + u % 4][:, 0:D], bias[:, 0:D], ALU.add).then_inc(evac, 1)
                                dve.wait_ge(evac, 2 * (U * i + u) + 1)
                                nc.vector.tensor_scalar(h, h, 0.0, None, ALU.max).then_inc(evac, 1)

                    @block.scalar
                    def _(act):
                        act.wait_ge(z_ready, 2)
                        nc.scalar.activation(bnc[:, 3:4], bnc[:, 2:3], ACT.Sqrt).then_inc(root, 1)
                        act.wait_ge(z_ready, 3)
                        with nc.scalar.Fori(0, NT // U) as i:
                            act.wait_ge(tr_done, i)
                            nc.scalar.copy(stage_in, work[:, bass.ds(U * D * i, U * D)]).then_inc(staged, 1)
                            act.wait_ge(tr_done, i + 1)
                            act.wait_ge(m1_done, i)
                            nc.scalar.copy(stage_T[:, 0:512], bank[0][:, 0:512]).then_inc(copied, 1)
                            nc.scalar.copy(stage_T[:, 512:U * D], bank[1][:, 0:U * D - 512]).then_inc(copied, 1)
                            act.wait_ge(m1_done, i + 1)
                            act.wait_ge(m2_done, U * i)
                            nc.scalar.activation(stage_y[:, 0:512], bank[2][:, 0:512], ACT.Relu, bias=shift, scale=scale).then_inc(y_done, 1)
                            nc.scalar.activation(stage_y[:, 512:U * D], bank[3][:, 0:U * D - 512], ACT.Relu, bias=shift, scale=scale).then_inc(y_done, 1)

                    @block.tensor
                    def _(pe):
                        pe.wait_ge(w_in, 48)
                        with nc.tensor.Fori(0, NT // U) as i:
                            pe.wait_ge(staged, i + 1)
                            pe.wait_ge(copied, 2 * i)
                            for u in range(U):
                                ins_ = nc.tensor.transpose(bank[u // 4][:, (u % 4) * P:(u % 4 + 1) * P], stage_in[:, u * D:(u + 1) * D], ident[:, :])
                            ins_.then_inc(tr_done, 1)
                            pe.wait_ge(copied, 2 * (i + 1))
                            pe.wait_ge(y_done, 2 * i)
                            nc.tensor.matmul(bank[2][:, 0:512], wgt[:, 0:D], stage_T[:, 0:512], start=True, stop=True)
                            nc.tensor.matmul(bank[3][:, 0:U * D - 512], wgt[:, 0:D], stage_T[:, 512:U * D], start=True, stop=True).then_inc(m1_done, 1)
                            pe.wait_ge(y_done, 2 * (i + 1))
                            for u in range(U):
                                pe.wait_ge(evac, 2 * (U * i + max(u - 3, 0)))
                                nc.tensor.matmul(bank[4 + u % 4][:, 0:D], stage_y[:, u * D:(u + 1) * D], wgt[:, D:2 * D], start=True, stop=True).then_inc(m2_done, 1)

        for c in range(2):
            src = x if c == 0 else work
            loads = []
            for k, n in enumerate("qkvs"):
                loads.append((wgt[:, k * D:(k + 1) * D], a[f"L0_{n}_w{c}"]))
                loads.append((bias[:, k * D:(k + 1) * D], a[f"L0_{n}_b{c}"].to_broadcast([P, D])))
            node_linear([src[:, :] if c == 0 else work], loads, 4 * D,
                        [(area(10000, NT * 384), 384, 0, 384), (skip[:, :], D, 384, 512)],
                        [(table(q_tab), proj3[:, :, 0:D]), (table(kv_tab), proj3[:, :, D:3 * D])])
            conv_edges()
            segment_max()
            carry_and_gather()

            def conv_nodes(link, on_act):
                den = sq3[:, :, 0:HEADS]
                link(nc.vector.tensor_scalar(den, agg[:, :, D:], 1e-30, None, ALU.max))
                link(nc.vector.reciprocal(den, den))
                body = agg[:, :, 0:D].rearrange("p t (h c) -> p t h c", h=HEADS)
                link(nc.vector.tensor_tensor(body, body, den.unsqueeze(3).to_broadcast([P, NT, HEADS, CH]), ALU.mult))
                link(nc.vector.tensor_tensor(work3, agg[:, :, 0:D], skip3, ALU.add))
                if c == 0:
                    link(nc.vector.tensor_scalar(work, work, 0.0, None, ALU.max))
                else:
                    link(nc.vector.tensor_tensor(work3, work3, x3, ALU.add))
                    norm_ops(link, on_act(ACT.Sqrt), work3, x3)
            node_math(conv_nodes, [] if c == 0 else [SQRT])

        HTOT = NT * D
        off = [0]

        def place(cols):
            off[0] += cols
            return area(off[0] - cols, cols)

        hh, s1bc, acc, iota_n, g_flat = place(HTOT), place(NP), place(NT * HW), place(NP), place(NT * HW)
        a12, s12, s1t, r2in, src2, dst2, lnwb = place(2 * D), place(2 * NT), place(P), place(2 * T2), place(T2), place(T2 + 8).bitcast(I32), place(2 * D)
        g_out = g_flat.rearrange("p (t c) -> p t c", c=HW)
        hh3 = hh.rearrange("p (t d) -> p t d", d=D)
        acc3 = acc.rearrange("p (t c) -> p t c", c=HW)

        def by_src_setup(loads, attention):
            with ExitStack() as ph:
                load_in, step, iota_s, to_pe, from_pe, g_ready, g_done, s1_out, s1_in = fresh(
                    ph, "load_in", "by_src_step", "iota_s", "to_pe", "from_pe", "g_ready", "g_done", "s1_out", "s1_in")
                loads = loads + [(r2in, recs2.rearrange("(p t) c -> p (t c)", t=T2))]
                with nc.Block() as block:
                    @block.gpsimd
                    def _(pool):
                        nc.gpsimd.iota(iota_n, pattern=[[1, NP]], base=0, channel_multiplier=0, allow_small_or_imprecise_dtypes=True).then_inc(iota_s, 1)

                    @block.sync
                    def _(sp):
                        for dst, src in loads:
                            sp.dma_start(dst, src).then_inc(load_in, 16)
                        sp.wait_ge(g_ready, 1)
                        sp.dma_start(table(g_tab), g_out).then_inc(g_done, 16)
                        if attention:
                            sp.wait_ge(g_ready, 2)
                            sp.dma_start(s1_tab.rearrange("a (t p) -> (a t) p", p=P), s1t[0:NT, :]).then_inc(s1_out, 16)
                            sp.wait_ge(s1_out, 16)
                            sp.dma_start(s1bc, s1_tab.to_broadcast([P, NP])).then_inc(s1_in, 16)
                            sp.wait_ge(s1_in, 16)
                        sp.wait_ge(g_done, 16)

                    @block.tensor
                    def _(pe):
                        if attention:
                            pe.wait_ge(to_pe, 1)
                            nc.tensor.transpose(bank[0][0:NT, 0:P], s12[:, 0:NT], ident[:, :]).then_inc(from_pe, 1)

                    @block.vector
                    def _(dve):
                        link = Chain(dve, step)
                        dve.wait_ge(load_in, 16 * len(loads))
                        link(nc.vector.memset(g_out[:, :, D:], 0.0))
                        if attention:
                            for k in range(2):
                                link(nc.vector.tensor_tensor(hh3, skip3, a12[:, k * D:(k + 1) * D].unsqueeze(1).to_broadcast([P, NT, D]), ALU.mult))
                                link(nc.vector.tensor_reduce(s12[:, k * NT:(k + 1) * NT], hh3, AX_X, ALU.add))
                            nc.vector.engine_nop().then_inc(to_pe, 1)
                            link(nc.vector.tensor_copy(g_out[:, :, 0:D], skip3))
                            link(nc.vector.tensor_copy(g_out[:, :, D], s12[:, NT:]))
                        else:
                            link(nc.vector.tensor_copy(g_out[:, :, 0:D], x3))
                            link(nc.vector.memset(g_out[:, :, D], 1.0))
                        nc.vector.engine_nop().then_inc(g_ready, 1)
                        if attention:
                            dve.wait_ge(from_pe, 1)
                            link(nc.vector.tensor_copy(s1t[0:NT, :], bank[0][0:NT, 0:P]))
                            nc.vector.engine_nop().then_inc(g_ready, 1)
                        r2 = r2in.rearrange("p (j c) -> p j c", c=2)
                        link(nc.vector.tensor_copy(src2, r2[:, :, 0]))
                        link(nc.vector.tensor_copy(dst2[:, 0:T2], r2[:, :, 1]))
                        link(nc.vector.memset(dst2[:, T2:], 0))
                        link(nc.vector.memset(acc, 0.0))

        def by_src_edges(attention):
            width = D if attention else D + 4
            with ExitStack() as ph:
                in0, in1 = dma_sems("half_in0", "half_in1")
                idx_ready, z_step, exp_done, oh_step, mm_done, add_step = fresh(ph, "idx_ready", "z_step", "exp_done", "oh_step", "mm_done", "add_step")
                half_in = (in0, in1)
                B = 4
                S2 = T2 // (2 * B)
                gr = ring[:, 0:2 * B * HW].rearrange("p (k c) -> p k c", c=HW)
                ohr = ring[:, 2 * B * HW:2 * B * HW + 2 * B * P]
                z1, z2, z3, ee = ((lambda h, k=k: small[:, 8 * k + 4 * h:8 * k + 4 * h + 4]) for k in range(4))
                junk = lambda k: prod[:, k * P:(k + 1) * P]

                def fetch(h):
                    for b in range(B):
                        k = h * B + b
                        nc.gpsimd.indirect_dma_start(out=gr[:, k, :], out_offset=None, in_=g_tab,
                                                     in_offset=bass.IndirectOffsetOnAxis(ap=idx_slot[:, k:k + 1], axis=0)).then_inc(half_in[h], 16)

                with nc.Block() as block:
                    @block.gpsimd
                    def _(pool):
                        for h in range(2):
                            pool.wait_ge(idx_ready, h + 1)
                            fetch(h)
                        with nc.gpsimd.Fori(1, S2) as i:
                            for h in range(2):
                                pool.wait_ge(idx_ready, 2 * i + h + 1)
                                pool.wait_ge(mm_done, B * (2 * i + h - 1))
                                nc.gpsimd.nop(nofuse=True)
                                fetch(h)

                    @block.scalar
                    def _(act):
                        for h in range(2):
                            nc.scalar.copy(idx_slot[:, h * B:(h + 1) * B], dst2[:, h * B:(h + 1) * B]).then_inc(idx_ready, 1)
                        with nc.scalar.Fori(0, S2) as i:
                            for h in range(2):
                                act.wait_ge(half_in[h], 16 * B * (i + 1))
                                nc.scalar.copy(idx_slot[:, h * B:(h + 1) * B], dst2[:, bass.ds((2 * i + h) * B + 2 * B, B)]).then_inc(idx_ready, 1)
                                if attention:
                                    act.wait_ge(z_step, (B + 2) * (2 * i + h + 1))
                                    nc.scalar.activation(ee(h), z3(h), ACT.Exp, scale=-1.0).then_inc(exp_done, 1)

                    @block.tensor
                    def _(pe):
                        with nc.tensor.Fori(0, S2) as i:
                            for h in range(2):
                                pe.wait_ge(half_in[h], 16 * B * (i + 1))
                                for b in range(B):
                                    k = h * B + b
                                    pe.wait_ge(oh_step, (2 * i + h) * B + b + 1)
                                    nc.tensor.matmul(bank[k][:, 0:width], ohr[:, k * P:(k + 1) * P], gr[:, k, 0:width], start=True, stop=True).then_inc(mm_done, 1)

                    @block.vector
                    def _(dve):
                        with nc.vector.Fori(0, S2) as i:
                            for h in range(2):
                                wins = []
                                for b in range(B):
                                    t = (2 * i + h) * B + b
                                    wins.append(nc.vector.value_load(window[0:1, bass.ds(t, 1)], min_val=0, max_val=NT - 1))
                                if attention:
                                    for b in range(B):
                                        t = (2 * i + h) * B + b
                                        nc.vector.scalar_tensor_tensor(junk(h * B + b), iota_n[:, bass.ds(wins[b] * P, P)], src2[:, bass.ds(t, 1)], s1bc[:, bass.ds(wins[b] * P, P)],
                                                                       ALU.is_equal, ALU.mult, accum_out=z1(h)[:, b:b + 1]).then_inc(z_step, 1)
                                    dve.wait_ge(half_in[h], 16 * B * (i + 1))
                                    dve.wait_ge(z_step, (B + 2) * (2 * i + h) + B)
                                    nc.vector.tensor_tensor(z2(h), z1(h), gr[:, h * B:(h + 1) * B, D], ALU.add).then_inc(z_step, 1)
                                    dve.wait_ge(z_step, (B + 2) * (2 * i + h) + B + 1)
                                    nc.vector.scalar_tensor_tensor(z3(h), z2(h), 0.2, z2(h), ALU.mult, ALU.max).then_inc(z_step, 1)
                                    dve.wait_ge(exp_done, 2 * i + h + 1)
                                dve.wait_ge(mm_done, B * 2 * i)
                                for b in range(B):
                                    t = (2 * i + h) * B + b
                                    k = h * B + b
                                    scale = (ee(h)[:, b:b + 1], ALU.mult) if attention else (None,)
                                    nc.vector.tensor_scalar(ohr[:, k * P:(k + 1) * P], iota_n[:, bass.ds(wins[b] * P, P)], src2[:, bass.ds(t, 1)], scale[0],
                                                            ALU.is_equal, *scale[1:]).then_inc(oh_step, 1)
                                for b in range(B):
                                    t = (2 * i + h) * B + b
                                    k = h * B + b
                                    dve.wait_ge(mm_done, t + 1)
                                    dve.wait_ge(add_step, t)
                                    to = acc[:, bass.ds(wins[b] * HW, width)]
                                    nc.vector.tensor_tensor(to, to, bank[k][:, 0:width], ALU.add).then_inc(add_step, 1)
                        dve.wait_ge(add_step, T2)

        by_src_setup([], False)
        by_src_edges(False)

        def mean_nodes(link, on_act):
            inv = s12[:, 0:NT]
            link(nc.vector.tensor_scalar(inv, acc3[:, :, D], 1.0, None, ALU.max))
            link(nc.vector.reciprocal(inv, inv))
            link(nc.vector.tensor_tensor(hh3, acc3[:, :, 0:D], inv.unsqueeze(2).to_broadcast([P, NT, D]), ALU.mult))
        node_math(mean_nodes, [])
        node_linear([x[:, :], hh], [(wgt[:, 0:D], a["L1_WT"][0:D, :]), (wgt[:, D:2 * D], a["L1_WT"][D:2 * D, :]), (bias[:, 0:D], a["L1_b"].to_broadcast([P, D]))],
                    D, [(skip[:, :], D, 0, D)], [])

        def add_norm(link, on_act):
            link(nc.vector.tensor_tensor(work3, skip3, x3, ALU.add))
            norm_ops(link, on_act(ACT.Sqrt), work3, x3)
        node_math(add_norm, [SQRT])

        node_linear([x[:, :]], [(wgt[:, 0:D], a["L2_W_enc"]), (bias[:, 0:D], a["L2_b_enc"].to_broadcast([P, D])),
                                (bn[:, :], a["L2_bn"]), (epsb[:, 0:3], a["L2_eps"].to_broadcast([P, 3]))],
                    D, [(skip[:, :], D, 0, D)], [(table(h_tab), skip3)])
        for layer in range(3):
            with ExitStack() as ph:
                w_in, clear = fresh(ph, "w_in", "clear")
                with nc.Block() as block:
                    @block.vector
                    def _(dve):
                        nc.vector.memset(wgt[:, :], 0.0).then_inc(clear, 1)

                    @block.sync
                    def _(sp):
                        sp.wait_ge(clear, 1)
                        for s in range(K):
                            sp.dma_start(wgt[s * REC:s * REC + EA, s * D:(s + 1) * D], a["L2_W_ee"]).then_inc(w_in, 16)
                            sp.dma_start(wgt[s * REC + R_ONE:s * REC + R_ONE + 1, s * D:(s + 1) * D], a["L2_b_ee"]).then_inc(w_in, 16)
                        sp.wait_ge(w_in, 32 * K)
            gine_edges()
            carry_and_gather()
            gine_nodes(layer)
        node_math(add_norm, [SQRT])

        node_linear([x[:, :]], [(wgt[:, 0:D], a["L3_WT"]), (bias[:, 0:D], a["L3_b"].to_broadcast([P, D]))], D, [(skip[:, :], D, 0, D)], [])
        by_src_setup([(a12[:, 0:D], a["L3_a"][:, 0:D].to_broadcast([P, D])), (a12[:, D:], a["L3_a"][:, D:].to_broadcast([P, D])),
                      (lnwb[:, 0:D], a["L3_ln_w"].to_broadcast([P, D])), (lnwb[:, D:], a["L3_ln_b"].to_broadcast([P, D]))], True)
        by_src_edges(True)

        def gat_nodes(link, on_act):
            ln_mean, ln_var, ln_inv, ln_tmp = (small[:, 100 + k * NT:100 + (k + 1) * NT] for k in range(4))
            bc = lambda c: c.unsqueeze(2).to_broadcast([P, NT, D])
            row = lambda r: r.unsqueeze(1).to_broadcast([P, NT, D])

            def norm(src, dst, scratch, sqrt):
                link(nc.vector.tensor_reduce(ln_mean, src, AX_X, ALU.add))
                link(nc.vector.tensor_scalar(ln_mean, ln_mean, 1.0 / D, None, ALU.mult))
                link(nc.vector.tensor_tensor(dst, src, bc(ln_mean), ALU.subtract))
                link(nc.vector.tensor_tensor(scratch, dst, dst, ALU.mult))
                link(nc.vector.tensor_reduce(ln_var, scratch, AX_X, ALU.add))
                link(nc.vector.tensor_scalar(ln_var, ln_var, 1.0 / D, LN_EPS, ALU.mult, ALU.add))
                sqrt(ln_var, ln_tmp)
                link(nc.vector.reciprocal(ln_inv, ln_tmp))
                link(nc.vector.tensor_tensor(dst, dst, bc(ln_inv), ALU.mult))

            norm(acc3[:, :, 0:D], skip3, hh3, on_act(ACT.Sqrt))
            link(nc.vector.tensor_tensor(skip3, skip3, row(lnwb[:, 0:D]), ALU.mult))
            link(nc.vector.tensor_tensor(skip3, skip3, row(lnwb[:, D:]), ALU.add))
            link(nc.vector.tensor_scalar(hh, skip[:, :], 0.0, None, ALU.min))
            on_act(ACT.Exp)(hh, g_flat[:, 0:HTOT])
            link(nc.vector.tensor_scalar(skip[:, :], skip[:, :], 0.0, -1.0, ALU.max, ALU.add))
            link(nc.vector.tensor_tensor(skip[:, :], skip[:, :], g_flat[:, 0:HTOT], ALU.add))
            link(nc.vector.tensor_tensor(hh3, skip3, x3, ALU.add))
            norm(hh3, x3, skip3, on_act(ACT.Sqrt))
        lv, lt = small[:, 100 + NT:100 + 2 * NT], small[:, 100 + 3 * NT:100 + 4 * NT]
        node_math(gat_nodes, [(ACT.Sqrt, lv, lt, {}), (ACT.Exp, hh, g_flat[:, 0:HTOT], {}), (ACT.Sqrt, lv, lt, {})])

        out_done = sem("out_done")
        with nc.Block() as block:
            @block.sync
            def _(sp):
                sp.dma_start(out[0:(NT - 1) * P, :].rearrange("(t p) d -> p t d", p=P), x3[:, 0:NT - 1, :]).then_inc(out_done, 16)
                sp.dma_start(out[(NT - 1) * P:N, :], x3[0:TAIL, NT - 1, :]).then_inc(out_done, 16)
                sp.wait_ge(out_done, 32)


def layout(i):
    import numpy as np

    c = np.ascontiguousarray
    a = {"x": c(i["x"]), "src": c(i["src"]), "dst": c(i["dst"]), "edge_attr": c(i["edge_attr_16"]), "edge_weight": c(np.asarray(i["edge_weight1"]).reshape(-1))}
    for n in "qkvs":
        for l in range(2):
            a[f"L0_{n}_w{l}"] = c(i[f"L0_gnn_{n}_w{l}"])
            a[f"L0_{n}_b{l}"] = c(np.asarray(i[f"L0_gnn_{n}_b{l}"]).reshape(1, -1))
    a["L1_WT"] = c(np.asarray(i["L1_gnn_W"]).T)
    a["L1_b"] = c(np.asarray(i["L1_gnn_b"]).reshape(1, -1))
    for n in ("W_enc", "W_ee", "W1", "W2", "b2"):
        a[f"L2_{n}"] = c(i[f"L2_gnn_{n}"])
    for n in ("b_enc", "b_ee", "eps"):
        a[f"L2_{n}"] = c(np.asarray(i[f"L2_gnn_{n}"]).reshape(1, -1))
    a["L2_bn"] = c(np.concatenate([np.asarray(i[f"L2_gnn_{n}"]).T for n in ("bn_gamma", "bn_beta", "bn_mean", "bn_var", "b1")], axis=1))
    a["L3_WT"] = c(np.asarray(i["L3_gnn_W"]).T)
    for n in ("b", "a", "ln_w", "ln_b"):
        a[f"L3_{n}"] = c(np.asarray(i[f"L3_gnn_{n}"]).reshape(1, -1))
    return a


def kernel(**inputs):
    import concourse.bacc as bacc
    from concourse.bass_utils import run_bass_kernel_spmd

    nc = bacc.Bacc("TRN2", target_bir_lowering=False, num_devices=1)
    arrays, aps = {}, {}
    for name, arr in layout(inputs).items():
        arrays[f"in_{name}"] = arr
        aps[name] = nc.dram_tensor(f"in_{name}", arr.shape, mybir.dt.from_np(arr.dtype), kind="ExternalInput").ap()
    out = nc.dram_tensor("out_x", (N, D), F32, kind="ExternalOutput").ap()
    build(nc, aps, out)
    r = run_bass_kernel_spmd(nc, [arrays], core_ids=[0])
    return r.results[0]["out_x"]
```

```python
from contextlib import ExitStack

import concourse.bass as bass
from concourse import mybir

F32 = mybir.dt.float32
I32 = mybir.dt.int32
ALU = mybir.AluOpType
ACT = mybir.ActivationFunctionType
AX_X = mybir.AxisListType.X

P = 128
N = 3125
E = 100000
D = 128
HEADS = 8
CH = D // HEADS
EA = 16
NT = -(-N // P)
NP = NT * P
TAIL = N - (NT - 1) * P
G = 8
NG = -(-E // (P * G))
J = NG * G
JTAIL = E - (P - 1) * J
K = 4
NV = 216
assert P * NV * K >= P * J + (K - 1) * (N + 1) and NV % 4 == 0
NS = NV * K
PHANTOM = NP
ZROW = N
REC = 20
R_W, R_SRC, R_DST, R_ONE = EA, EA + 1, EA + 2, EA + 3
ITEMS = NG + NT - 1
ROWS = P * NV
W = D + HEADS
LVROWS = NP + ROWS
BIG = 1e37
MASK = 1e30
LN_EPS = 1e-5
SCALE = CH ** -0.5
U = 5
assert NT % U == 0


class Chain:

    def __init__(self, eng, sem):
        self.eng, self.sem, self.n = eng, sem, 0

    def __call__(self, ins):
        self.n += 1
        ins.then_inc(self.sem, 1)
        self.eng.wait_ge(self.sem, self.n)


def build(nc, a, out):
    ctx = ExitStack()
    with ctx:
        def sb(name, cols, dt=F32, parts=P):
            return ctx.enter_context(nc.sbuf_tensor(name, [parts, cols], dt))

        def sem(name):
            return ctx.enter_context(nc.semaphore(name))

        def dram(name, shape, dt=F32):
            return nc.dram_tensor(name, shape, dt, kind="Internal").ap()

        ident, shift_in, shift_back, upper, ones = (sb(n, P) for n in ("ident", "shift_in", "shift_back", "upper", "ones"))
        x = sb("x", NT * D)
        skip = sb("skip", NT * D)
        x3 = x[:, :].rearrange("p (t d) -> p t d", d=D)
        skip3 = skip[:, :].rearrange("p (t d) -> p t d", d=D)
        sums = sb("sums", (NV + 1) * W)
        sums3 = sums[:, :].rearrange("p (j f) -> p j f", f=W)
        ring = sb("ring", 4 * K * 2 * D)
        qring = sb("qring", 4 * D)
        prod = sb("prod", 2 * K * D)
        pv = sb("pv", 2 * K * D)
        rowmax = sb("rowmax", NV * HEADS)
        src_idx = sb("src_idx", NS + 16, I32)
        q_idx = sb("q_idx", NV + 4, I32)
        weight = sb("weight", NS)
        maskneg = sb("maskneg", NS)
        same, same_l, reset, rnext, fs_neg, ls_neg = (sb(n, NV) for n in ("same", "same_l", "reset", "rnext", "fs_neg", "ls_neg"))
        link_row, cont_row = sb("link_row", P), sb("cont_row", P)
        neg_rows = sb("neg_rows", 4 * P)
        last_idx = sb("last_idx", NT * 2, I32)
        wgt = sb("wgt", 512)
        bias = sb("bias", 512)
        idx_slot = sb("idx_slot", 2 * 2 * K, I32)
        qidx_slot = sb("qidx_slot", 2 * 2, I32)
        small = sb("small", 1200)

        psum = ctx.enter_context(nc.psum_tensor("psum", [P, 8 * 512], F32))
        bank = [psum[:, i * 512:(i + 1) * 512] for i in range(8)]


        def dma_sems(*names):
            count[0] += 1
            return [sem(f"{n}_{count[0]}") for n in names]

        count = [0]

        def fresh(ph, *names):
            count[0] += 1
            sems = [nc.alloc_semaphore(f"{n}_{count[0]}") for n in names]

            def retire():
                for s in sems:
                    nc.gpsimd.sem_clear(s)
                    nc.release_semaphore(s)
            ph.callback(retire)
            return sems

        recs = dram("recs", (P * NS, REC))
        count_tab = dram("count_tab", (NP, NP))
        last_tab = dram("last_tab", (LVROWS, 2), I32)
        q_tab = dram("q_tab", (NP, D))
        kv_tab = dram("kv_tab", (NP, 2 * D))
        h_tab = dram("h_tab", (NP, D))
        s1_tab = dram("s1_tab", (1, NP))
        sums_tab = dram("sums_tab", (ROWS + 1, W))
        carry_tab = dram("carry_tab", (P + 1, W))

        def area(off, cols):
            return sums[:, off:off + cols]

        agg = area(0, NT * W).rearrange("p (t f) -> p t f", f=W)
        car = area(NT * W, NT * W).rearrange("p (t f) -> p t f", f=W)
        work = area(2 * NT * W, NT * D)
        work3 = work.rearrange("p (t d) -> p t d", d=D)
        proj3 = area(10000, NT * 384).rearrange("p (t d) -> p t d", d=384)
        sq = area(19600, NT * D)
        sq3 = sq.rearrange("p (t d) -> p t d", d=D)
        col25 = area(22800, 4 * NT)
        stage_in = ring[:, 0:U * D]
        stage_in2 = ring[:, U * D:2 * U * D]
        stage_T = ring[:, 2 * U * D:3 * U * D]
        stage_T2 = ring[:, 3 * U * D:4 * U * D]
        stage_y = ring[:, 4 * U * D:5 * U * D]

        def table(t, cols=None):
            return t.rearrange("(t p) c -> p t c", p=P)

        f = lambda k: area(REC * J + k * J, J)
        rec3 = area(0, REC * J).rearrange("p (j c) -> p j c", c=REC)
        dst_i, src_i = (f(k).bitcast(I32) for k in (0, 1))
        eidx, d1, start, seg, pad, cum = (f(k) for k in (2, 3, 4, 5, 6, 7))
        t0, t1, t2, t3 = (f(k) for k in (8, 9, 10, 11))
        PIECE = 200
        pieces = [(lo, min(lo + PIECE, J)) for lo in range(0, J, PIECE)]
        ea_stage = (skip[:, 0:PIECE * EA], ring[:, 0:PIECE * EA])
        recfill = ring[:, 0:108 * REC]
        assert 108 * 8 == NS
        lastfill = small[:, 0:50].bitcast(I32)
        zrow = small[:, 64:64 + W]
        rows129 = small[0:1, 256:256 + P + 1]
        colA = small[:, 400:430]
        bcol = small[:, 430:456]
        pos1 = pad.bitcast(I32)
        with ExitStack() as ph:
            fills_ready, loads, fills_out, setup, pool_step = fresh(ph, "fills_ready", "loads0", "fills_out", "setup0", "pool_step0")
            with nc.Block() as block:
                @block.gpsimd
                def _(pool):
                    link = Chain(pool, pool_step)
                    for m, base, cm, step in ((ident, 0, 1, -1), (shift_in, -1, -1, 1), (shift_back, 1, -1, 1)):
                        link(nc.gpsimd.memset(m[:, :], 0.0))
                        link(nc.gpsimd.affine_select(out=m[:, :], in_=m[:, :], compare_op=ALU.not_equal, fill=1.0, base=base, pattern=[[step, P]], channel_multiplier=cm))
                    link(nc.gpsimd.memset(ones[:, :], 1.0))
                    link(nc.gpsimd.affine_select(out=upper[:, :], in_=ones[:, :], compare_op=ALU.is_gt, fill=0.0, base=0, pattern=[[1, P]], channel_multiplier=-1))
                    link(nc.gpsimd.iota(eidx, pattern=[[1, J]], base=0, channel_multiplier=J, allow_small_or_imprecise_dtypes=True))

                @block.vector
                def _(dve):
                    link = Chain(dve, setup)
                    nc.vector.memset(x[:, (NT - 1) * D:], 0.0).then_inc(fills_ready, 1)
                    nc.vector.memset(dst_i, PHANTOM).then_inc(fills_ready, 1)
                    nc.vector.memset(src_i, ZROW).then_inc(fills_ready, 1)
                    nc.vector.memset(area(0, REC * J), 0.0).then_inc(fills_ready, 1)
                    rf = recfill.rearrange("p (j c) -> p j c", c=REC)
                    link(nc.vector.memset(recfill, 0.0))
                    link(nc.vector.memset(rf[:, :, R_SRC], float(ZROW)))
                    nc.vector.memset(rf[:, :, R_DST], float(PHANTOM)).then_inc(fills_ready, 1)
                    lf = lastfill.rearrange("p (j c) -> p j c", c=2)
                    link(nc.vector.memset(lf[:, :, 0], ROWS))
                    nc.vector.memset(lf[:, :, 1], P).then_inc(fills_ready, 1)
                    nc.vector.memset(zrow, 0.0).then_inc(fills_ready, 1)
                    nc.vector.memset(src_idx[:, NS:], 0).then_inc(fills_ready, 1)
                    nc.vector.memset(q_idx[:, NV:], 0).then_inc(fills_ready, 1)

                @block.sync
                def _(sp):
                    sp.wait_ge(fills_ready, 9)
                    sp.dma_start(x3[:, 0:NT - 1, :], a["x"][0:(NT - 1) * P, :].rearrange("(t p) d -> p t d", p=P)).then_inc(loads, 16)
                    sp.dma_start(x3[0:TAIL, NT - 1, :], a["x"][(NT - 1) * P:N, :]).then_inc(loads, 16)
                    for name, tile in (("dst", dst_i), ("src", src_i)):
                        sp.dma_start(tile[0:P - 1, :], a[name][0:(P - 1) * J].rearrange("(p j) -> p j", j=J)).then_inc(loads, 16)
                        sp.dma_start(tile[P - 1:P, 0:JTAIL], a[name][(P - 1) * J:E].rearrange("(p j) -> p j", p=1)).then_inc(loads, 16)
                    r = recs.rearrange("(p i j) c -> i p (j c)", i=8, j=108)
                    for i in range(8):
                        sp.dma_start(r[i], recfill).then_inc(fills_out, 16)
                    sp.dma_start(last_tab[0:NP, :].rearrange("(p t) c -> p (t c)", p=P), lastfill).then_inc(fills_out, 16)
                    sp.dma_start(sums_tab[ROWS:ROWS + 1, :], zrow[0:1, :]).then_inc(fills_out, 16)
                    sp.dma_start(carry_tab[P:P + 1, :], zrow[0:1, :]).then_inc(fills_out, 16)
                    sp.wait_ge(loads, 6 * 16)
                    sp.wait_ge(fills_out, 11 * 16)

        with ExitStack() as ph:
            rec_step, ea_in0, ea_in1, ea_used, w_in, to_pe, from_pe = fresh(ph, "rec_step", "ea_in0", "ea_in1", "ea_used", "w_in", "to_pe1", "from_pe1")
            ea_v = a["edge_attr"]
            ea_in = (ea_in0, ea_in1)
            wcol = t0
            with nc.Block() as block:
                @block.sync
                def _(sp):
                    sp.wait_ge(rec_step, 3)
                    sp.dma_start(wcol[0:P - 1, :], a["edge_weight"][0:(P - 1) * J].rearrange("(p j) -> p j", j=J)).then_inc(w_in, 16)
                    sp.dma_start(wcol[P - 1:P, 0:JTAIL], a["edge_weight"][(P - 1) * J:E].rearrange("(p j) -> p j", p=1)).then_inc(w_in, 16)
                    full = ea_v[0:(P - 1) * J, :].rearrange("(p j) c -> p (j c)", j=J)
                    tail = ea_v[(P - 1) * J:E, :].rearrange("(p j) c -> p (j c)", p=1)
                    for h, (lo, hi) in enumerate(pieces):
                        st = ea_stage[h % 2]
                        if h >= 2:
                            sp.wait_ge(ea_used, h - 1)
                        n = (min(hi, JTAIL) - lo) * EA
                        sp.dma_start(st[0:P - 1, 0:(hi - lo) * EA], full[:, lo * EA:hi * EA]).then_inc(ea_in[h % 2], 16)
                        if n > 0:
                            sp.dma_start(st[P - 1:P, 0:n], tail[:, lo * EA:lo * EA + n]).then_inc(ea_in[h % 2], 16)

                @block.scalar
                def _(act):
                    due = [0, 0]
                    for h, (lo, hi) in enumerate(pieces):
                        due[h % 2] += 32 if lo < JTAIL else 16
                        act.wait_ge(ea_in[h % 2], due[h % 2])
                        nc.scalar.copy(rec3[:, lo:hi, 0:EA],
                                       ea_stage[h % 2][:, 0:(hi - lo) * EA].rearrange("p (j c) -> p j c", c=EA)).then_inc(ea_used, 1)

                @block.tensor
                def _(pe):
                    pe.wait_ge(to_pe, 1)
                    nc.tensor.matmul(bank[0][:, 0:1], shift_in[:, :], d1[:, J - 1:J], start=True, stop=True).then_inc(from_pe, 1)
                    pe.wait_ge(to_pe, 2)
                    nc.tensor.matmul(bank[1][0:1, 0:P], seg[:, J - 1:J], ident[:, :], start=True, stop=True).then_inc(from_pe, 1)
                    pe.wait_ge(to_pe, 3)
                    nc.tensor.matmul(bank[2][:, 0:1], rows129[:, 0:P], ones[0:1, 0:1], start=True, stop=True).then_inc(from_pe, 1)
                    pe.wait_ge(to_pe, 4)
                    nc.tensor.matmul(bank[3][:, 0:1], shift_in[:, :], seg[:, J - 1:J], start=True, stop=True).then_inc(from_pe, 1)
                    pe.wait_ge(to_pe, 5)
                    nc.tensor.matmul(bank[4][:, 0:1], upper[:, :], cum[:, J - 1:J], start=True, stop=True).then_inc(from_pe, 1)

                @block.vector
                def _(dve):
                    link = Chain(dve, rec_step)
                    link(nc.vector.memset(ea_stage[0], 0.0))
                    link(nc.vector.memset(ea_stage[1], 0.0))
                    link(nc.vector.memset(wcol, 0.0))
                    link(nc.vector.tensor_copy(rec3[:, :, R_DST], dst_i))
                    link(nc.vector.tensor_copy(rec3[:, :, R_SRC], src_i))
                    link(nc.vector.memset(rec3[:, :, R_ONE], 1.0))
                    link(nc.vector.tensor_scalar(d1, rec3[:, :, R_DST], 1.0, None, ALU.add))
                    link(nc.vector.memset(rows129, 0.0))
                    nc.vector.engine_nop().then_inc(to_pe, 1)
                    link(nc.vector.tensor_tensor(start[:, 1:], d1[:, 1:], d1[:, 0:J - 1], ALU.not_equal))
                    dve.wait_ge(from_pe, 1)
                    link(nc.vector.tensor_tensor(start[:, 0:1], d1[:, 0:1], bank[0][:, 0:1], ALU.not_equal))
                    link(nc.vector.tensor_tensor(t1, start, eidx, ALU.mult))
                    link(nc.vector.tensor_tensor_scan(seg, t1, t1, 0.0, ALU.max, ALU.max))
                    nc.vector.engine_nop().then_inc(to_pe, 1)
                    dve.wait_ge(from_pe, 2)
                    link(nc.vector.tensor_copy(t2[0:1, 0:P], bank[1][0:1, 0:P]))
                    link(nc.vector.tensor_tensor_scan(rows129[:, 1:P + 1], t2[0:1, 0:P], t2[0:1, 0:P], 0.0, ALU.max, ALU.max))
                    nc.vector.engine_nop().then_inc(to_pe, 1)
                    dve.wait_ge(from_pe, 3)
                    link(nc.vector.tensor_scalar(seg, seg, bank[2][:, 0:1], None, ALU.max))
                    nc.vector.engine_nop().then_inc(to_pe, 1)
                    link(nc.vector.tensor_tensor(t1[:, 1:], seg[:, 0:J - 1], eidx[:, 1:], ALU.subtract))
                    dve.wait_ge(from_pe, 4)
                    link(nc.vector.tensor_tensor(t1[:, 0:1], bank[3][:, 0:1], eidx[:, 0:1], ALU.subtract))
                    link(nc.vector.tensor_copy(t2.bitcast(I32), t1))
                    link(nc.vector.tensor_scalar(t3.bitcast(I32), t2.bitcast(I32), K - 1, None, ALU.bitwise_and))
                    link(nc.vector.tensor_copy(t2, t3.bitcast(I32)))
                    link(nc.vector.tensor_tensor(pad, start, t2, ALU.mult))
                    link(nc.vector.tensor_tensor_scan(cum, pad, pad, 0.0, ALU.add, ALU.max))
                    nc.vector.engine_nop().then_inc(to_pe, 1)
                    dve.wait_ge(from_pe, 5)
                    link(nc.vector.tensor_copy(colA[:, 0:1], bank[4][:, 0:1]))
                    link(nc.vector.scalar_tensor_tensor(pos1, cum, colA[:, 0:1], eidx, ALU.add, ALU.add))
                    dve.wait_ge(w_in, 32)
                    link(nc.vector.tensor_copy(rec3[:, :, R_W], wcol))

        def scatter_loop(nc, pool, act, eng, cols, chunk, rec, width, dt, pos, stage, pos_stage, table_ap, ready, done):
            steps = cols // (2 * chunk)
            assert steps * 2 * chunk == cols
            if eng == "act":
                with nc.scalar.Fori(0, steps) as i:
                    for u in range(2):
                        act.wait_ge(done[u], 16 * chunk * i)
                        nc.scalar.copy(stage[:, u * chunk * width:(u + 1) * chunk * width],
                                       rec[:, bass.ds((2 * i + u) * chunk * width, chunk * width)]).then_inc(ready, 1)
                        nc.scalar.copy(pos_stage[:, u * chunk:(u + 1) * chunk],
                                       pos[:, bass.ds((2 * i + u) * chunk, chunk)]).then_inc(ready, 1)
            else:
                with nc.gpsimd.Fori(0, steps) as i:
                    for u in range(2):
                        pool.wait_ge(ready, 4 * i + 2 * u + 2)
                        nc.gpsimd.nop(nofuse=True)
                        for c in range(chunk):
                            k = u * chunk + c
                            nc.gpsimd.indirect_dma_start(
                                out=table_ap, out_offset=bass.IndirectOffsetOnAxis(ap=pos_stage[:, k:k + 1], axis=0),
                                in_=stage[:, k * width:(k + 1) * width], in_offset=None).then_inc(done[u], 16)

        CHUNK = J // 112
        assert CHUNK * 112 == J
        QS = NP // 2
        BF, F16 = mybir.dt.bfloat16, mybir.dt.float16
        stage1 = ring[:, 0:2 * CHUNK * REC]
        pstage1 = ring[:, 1000:1000 + 2 * CHUNK].bitcast(I32)
        o = REC * J
        src_lo, src_hi, dst_tm = (area(o + k * 7 * P, 7 * P) for k in range(3))
        dloc = area(o + 2720, 2 * G)
        oh_dst = area(o + 2752, G * P).bitcast(BF)
        nb, ntab = area(o + 3776, ITEMS), area(o + 3900, 2 * ITEMS).bitcast(I32)
        gcol, gend, cmp_i, iota_i = area(o + 4150, 2), area(o + 4152, 2), area(o + 4160, ITEMS), area(o + 4300, ITEMS)
        assert 4300 + ITEMS <= 6 * J
        snap = area(o + 7 * J, NP)
        oh_src = area(o + 7 * J + NP, NP).bitcast(BF)
        iota16 = area(o + 7 * J + 2 * NP, QS // 2).bitcast(F16)
        raw = [skip[:, k * 7 * P:(k + 1) * 7 * P] for k in range(2)]
        rawf = [pv[:, 0:7 * P], prod[:, 0:7 * P]]
        assert o + 7 * J + 2 * NP + QS // 2 <= (NV + 1) * W
        TF = E // P
        with ExitStack() as ph:
            d10, d11 = dma_sems("rec_out0", "rec_out1")
            ready1, pstep, loads_s, iotas, to_pe, from_pe, ohd, ohs, mm_done, snapped, stored, cleared_s = fresh(
                ph, "rec_staged", "pair_step", "edges_in", "iotas", "to_pe", "from_pe", "oh_dst", "oh_src", "mm_done", "snapped", "stored", "cleared")
            r1 = area(0, REC * J)
            done = (d10, d11)
            with nc.Block() as block:
                @block.gpsimd
                def _(pool):
                    nc.gpsimd.iota(iota16, pattern=[[1, QS]], base=0, channel_multiplier=0, allow_small_or_imprecise_dtypes=True).then_inc(iotas, 1)
                    nc.gpsimd.iota(iota_i, pattern=[[1, ITEMS]], base=0, channel_multiplier=0, allow_small_or_imprecise_dtypes=True).then_inc(iotas, 1)
                    nc.gpsimd.iota(gcol[:, 1:2], pattern=[[0, 1]], base=0, channel_multiplier=1, allow_small_or_imprecise_dtypes=True).then_inc(iotas, 1)
                    with nc.gpsimd.Fori(0, 56) as i:
                        for u in range(2):
                            pool.wait_ge(ready1, 4 * i + 2 * u + 2)
                            nc.gpsimd.nop(nofuse=True)
                            for c in range(CHUNK):
                                k = u * CHUNK + c
                                nc.gpsimd.indirect_dma_start(
                                    out=recs, out_offset=bass.IndirectOffsetOnAxis(ap=pstage1[:, k:k + 1], axis=0),
                                    in_=stage1[:, k * REC:(k + 1) * REC], in_offset=None).then_inc(done[u], 16)
                    for d in done:
                        pool.wait_ge(d, 16 * CHUNK * 56)

                @block.sync
                def _(sp):
                    sp.wait_ge(cleared_s, 3)
                    for k, n in enumerate(("dst", "src")):
                        for b in range(7):
                            rows = min(P, TF - b * P)
                            sp.dma_start(raw[k].bitcast(I32)[0:rows, b * P:(b + 1) * P],
                                         a[n][b * P * P:(b * P + rows) * P].rearrange("(t e) -> t e", e=P)).then_inc(loads_s, 16)
                        sp.dma_start(raw[k].bitcast(I32)[TF - 6 * P:TF - 6 * P + 1, 6 * P:6 * P + E - TF * P],
                                     a[n][TF * P:E].rearrange("(t e) -> t e", t=1)).then_inc(loads_s, 16)
                    sp.dma_start(gcol.bitcast(I32)[0:NG - 1, 0:1], a["dst"][0:(NG - 1) * G * P].rearrange("(g e) -> g e", e=G * P)[:, G * P - 1:], allow_slow_non_contiguous=True).then_inc(loads_s, 16)
                    with nc.sync.Fori(0, ITEMS // 2) as i:
                        for u in range(2):
                            sp.wait_ge(snapped, 2 * i + u + 2)
                            nc.sync.nop(nofuse=True)
                            n = nc.sync.value_load(ntab[0:1, bass.ds(2 * i + u, 1)], min_val=0, max_val=NT - 1)
                            sp.dma_start(count_tab[bass.ds(n * P, P), :], snap).then_inc(stored, 16)
                            sp.wait_ge(stored, 16 * (2 * i + u + 1))
                            nc.sync.nop(nofuse=True)

                @block.tensor
                def _(pe):
                    for k in range(2):
                        pe.wait_ge(to_pe, k + 1)
                        for b in range(7):
                            ins_ = nc.tensor.transpose(bank[2 * k + b // 4][:, (b % 4) * P:(b % 4 + 1) * P], rawf[k][:, b * P:(b + 1) * P], ident[:, :])
                        ins_.then_inc(from_pe, 1)
                    pe.wait_ge(to_pe, 3)
                    nc.tensor.matmul(bank[4][:, 0:ITEMS], ones[:, :], cmp_i, start=True, stop=True).then_inc(from_pe, 1)
                    pe.wait_ge(to_pe, 4)
                    for b in range(7):
                        w = min(512, NP - b * 512)
                        nc.tensor.matmul(bank[b][:, 0:w], oh_dst[:, 0:P], oh_src[:, 0:w], start=True, stop=True)
                    for _ in range(2):
                        nc.tensor.matmul(bank[7][:, 0:1], ones[:, :], ones[:, 0:1], start=True, stop=True).then_inc(mm_done, 1)
                    with nc.tensor.Fori(0, ITEMS // 2) as i:
                        for u in range(2):
                            for k in range(G):
                                t = G * (2 * i + u) + k
                                pe.wait_ge(ohs, t + 1)
                                if k == 0:
                                    pe.wait_ge(snapped, 2 * i + u + 1)
                                for b in range(7):
                                    w = min(512, NP - b * 512)
                                    ins_ = nc.tensor.matmul(bank[b][:, 0:w], oh_dst[:, (u * G + k) * P:(u * G + k + 1) * P],
                                                            oh_src[:, (k % 2) * NP + b * 512:(k % 2) * NP + b * 512 + w], start=False, stop=True, skip_group_check=True)
                                ins_.then_inc(mm_done, 1)

                @block.scalar
                def _(act):
                    nc.scalar.copy(snap[:, 0:1], ones[:, 0:1]).then_inc(snapped, 1)

                    def snapshot(i, u):
                        act.wait_ge(mm_done, G * (2 * i + u + 1) + 2)
                        act.wait_ge(stored, 16 * (2 * i + u))
                        nc.scalar.copy(snap, psum[:, 0:NP]).then_inc(snapped, 1)
                    with nc.scalar.Fori(0, 56) as i:
                        for u in range(2):
                            act.wait_ge(done[u], 16 * CHUNK * i)
                            nc.scalar.copy(stage1[:, u * CHUNK * REC:(u + 1) * CHUNK * REC], r1[:, bass.ds((2 * i + u) * CHUNK * REC, CHUNK * REC)]).then_inc(ready1, 1)
                            nc.scalar.copy(pstage1[:, u * CHUNK:(u + 1) * CHUNK], pos1[:, bass.ds((2 * i + u) * CHUNK, CHUNK)]).then_inc(ready1, 1)
                            snapshot(i, u)
                    with nc.scalar.Fori(56, ITEMS // 2) as i:
                        for u in range(2):
                            snapshot(i, u)

                @block.vector
                def _(dve):
                    link = Chain(dve, pstep)
                    nc.vector.memset(raw[0].bitcast(I32), PHANTOM).then_inc(cleared_s, 1)
                    nc.vector.memset(raw[1].bitcast(I32), 0).then_inc(cleared_s, 1)
                    nc.vector.memset(gcol.bitcast(I32)[:, 0:1], PHANTOM).then_inc(cleared_s, 1)
                    dve.wait_ge(loads_s, 16 * 17)
                    dve.wait_ge(iotas, 3)
                    link(nc.vector.tensor_copy(rawf[0], raw[0].bitcast(I32)))
                    nc.vector.engine_nop().then_inc(to_pe, 1)
                    link(nc.vector.tensor_copy(rawf[1], raw[1].bitcast(I32)))
                    nc.vector.engine_nop().then_inc(to_pe, 1)
                    link(nc.vector.tensor_scalar(gend.bitcast(I32)[:, 0:1], gcol.bitcast(I32)[:, 0:1], 7, None, ALU.arith_shift_right))
                    link(nc.vector.tensor_copy(gend[:, 1:2], gend.bitcast(I32)[:, 0:1]))
                    link(nc.vector.scalar_tensor_tensor(gend[:, 0:1], gend[:, 1:2], float(NT - 1), gcol[:, 1:2], ALU.min, ALU.add))
                    link(nc.vector.tensor_scalar(cmp_i, iota_i, gend[:, 0:1], None, ALU.is_gt))
                    link(nc.vector.memset(oh_dst, 0.0))
                    link(nc.vector.memset(oh_src, 0.0))
                    nc.vector.engine_nop().then_inc(to_pe, 1)
                    dve.wait_ge(from_pe, 2)
                    link(nc.vector.tensor_copy(dst_tm, psum[:, 0:7 * P]))
                    link(nc.vector.tensor_copy(src_lo, psum[:, 1024:1024 + 7 * P]))
                    link(nc.vector.tensor_scalar(src_hi, src_lo, -float(QS), None, ALU.add))
                    dve.wait_ge(from_pe, 3)
                    link(nc.vector.tensor_copy(nb, bank[4][:, 0:ITEMS]))
                    link(nc.vector.tensor_scalar(ntab[:, ITEMS:], nb, float(G), None, ALU.mult))
                    link(nc.vector.tensor_tensor(nb, iota_i, nb, ALU.subtract))
                    link(nc.vector.tensor_copy(ntab[:, 0:ITEMS], nb))
                    link(nc.vector.tensor_scalar(nb, nb, float(P), None, ALU.mult))
                    nc.vector.engine_nop().then_inc(to_pe, 1)
                    with nc.vector.Fori(0, ITEMS // 2) as i:
                        for u in range(2):
                            t0 = nc.vector.value_load(ntab[0:1, bass.ds(ITEMS + 2 * i + u, 1)], min_val=0, max_val=(NG - 1) * G)
                            dl = dloc[:, u * G:(u + 1) * G]
                            nc.vector.tensor_scalar(dl, dst_tm[:, bass.ds(t0, G)], nb[:, bass.ds(2 * i + u, 1)], None, ALU.subtract).then_inc(ohd, 1)
                            dve.wait_ge(ohd, 2 * i + u + 1)
                            for k in range(G):
                                t = G * (2 * i + u) + k
                                dve.wait_ge(mm_done, t + 1)
                                c = (k % 2) * NP
                                nc.vector.tensor_scalar(oh_dst[:, (u * G + k) * P:(u * G + k + 1) * P], iota16[:, 0:P], dl[:, k:k + 1], None, ALU.is_equal)
                                nc.vector.tensor_scalar(oh_src[:, c:c + QS], iota16, src_lo[:, bass.ds(t0 + k, 1)], None, ALU.is_equal)
                                nc.vector.tensor_scalar(oh_src[:, c + QS:c + NP], iota16, src_hi[:, bass.ds(t0 + k, 1)], None, ALU.is_equal).then_inc(ohs, 1)

        back = area(0, NS * REC)
        back4 = back.rearrange("p (j s c) -> p j s c", s=K, c=REC)
        g = lambda k: area(NS * REC + k * NV, NV)
        vn1, snext, fs, ls, dump, last, vidx, tA, tB = (g(k) for k in range(9))
        rec3w = area(NS * REC + 9 * NV, 2 * NV)
        srows = area(NS * REC + 11 * NV, NS)
        lpos = area(NS * REC + 11 * NV + NS, NV)
        rec3i = rec3w.bitcast(I32)
        stage3 = ring[:, 0:2 * 12 * 2].bitcast(I32)
        pstage3 = ring[:, 100:124].bitcast(I32)
        with ExitStack() as ph:
            d30, d31 = dma_sems("last_out0", "last_out1")
            back_in, row_step, to_pe, from_pe, iotas, ready3, tab_in = fresh(ph, "back_in", "row_step", "to_pe3", "from_pe3", "iotas3", "last_staged", "last_in")
            lane_m = small[:, 702:703]
            colB = small[:, 710:730]
            with nc.Block() as block:
                @block.sync
                def _(sp):
                    sp.dma_start(back, recs.rearrange("(p j) c -> p (j c)", j=NS)).then_inc(back_in, 16)
                    sp.wait_ge(d30, 16 * NV // 2)
                    sp.wait_ge(d31, 16 * NV // 2)
                    sp.dma_start(last_idx[:, :].rearrange("p (t c) -> p t c", c=2), table(last_tab[0:NP, :])).then_inc(tab_in, 16)
                    sp.wait_ge(tab_in, 16)

                @block.gpsimd
                def _(pool):
                    nc.gpsimd.iota(lane_m, pattern=[[0, 1]], base=-P, channel_multiplier=1, allow_small_or_imprecise_dtypes=True).then_inc(iotas, 1)
                    nc.gpsimd.iota(vidx, pattern=[[1, NV]], base=0, channel_multiplier=NV, allow_small_or_imprecise_dtypes=True).then_inc(iotas, 1)
                    scatter_loop(nc, pool, None, "pool", NV, 12, rec3i, 2, I32, lpos.bitcast(I32), stage3, pstage3, last_tab, ready3, (d30, d31))

                @block.scalar
                def _(act):
                    act.wait_ge(to_pe, 8)
                    scatter_loop(nc, None, act, "act", NV, 12, rec3i, 2, I32, lpos.bitcast(I32), stage3, pstage3, last_tab, ready3, (d30, d31))

                @block.tensor
                def _(pe):
                    pe.wait_ge(to_pe, 1)
                    nc.tensor.matmul(bank[0][:, 0:1], shift_in[:, :], vn1[:, NV - 1:NV], start=True, stop=True).then_inc(from_pe, 1)
                    pe.wait_ge(to_pe, 2)
                    nc.tensor.matmul(bank[1][:, 0:1], shift_back[:, :], same[:, 0:1], start=True, stop=True).then_inc(from_pe, 1)
                    pe.wait_ge(to_pe, 3)
                    nc.tensor.matmul(bank[2][:, 0:1], shift_in[:, :], fs[:, NV - 1:NV], start=True, stop=True).then_inc(from_pe, 1)
                    nc.tensor.matmul(bank[3][:, 0:1], shift_back[:, :], ls[:, 0:1], start=True, stop=True).then_inc(from_pe, 1)
                    for k in range(4):
                        pe.wait_ge(to_pe, 4 + k)
                        nc.tensor.matmul(bank[4 + k][:, 0:P], srows[:, k * P:(k + 1) * P], ident[:, :], start=True, stop=True).then_inc(from_pe, 1)

                @block.vector
                def _(dve):
                    link = Chain(dve, row_step)
                    dve.wait_ge(iotas, 2)
                    dve.wait_ge(back_in, 16)
                    link(nc.vector.tensor_copy(src_idx[:, 0:NS], back4[:, :, :, R_SRC].rearrange("p j s -> p (j s)")))
                    link(nc.vector.tensor_copy(weight[:, :], back4[:, :, :, R_W].rearrange("p j s -> p (j s)")))
                    link(nc.vector.tensor_scalar(maskneg[:, :], back4[:, :, :, R_SRC].rearrange("p j s -> p (j s)"), float(ZROW), -MASK, ALU.is_ge, ALU.mult))
                    link(nc.vector.tensor_scalar(vn1, back4[:, :, 0, R_DST], 1.0, None, ALU.add))
                    nc.vector.engine_nop().then_inc(to_pe, 1)
                    link(nc.vector.tensor_scalar(q_idx[:, 0:NV], back4[:, :, 0, R_DST], float(NP - 1), None, ALU.min))
                    link(nc.vector.tensor_tensor(same[:, 1:], vn1[:, 1:], vn1[:, 0:NV - 1], ALU.is_equal))
                    dve.wait_ge(from_pe, 1)
                    link(nc.vector.tensor_tensor(same[:, 0:1], vn1[:, 0:1], bank[0][:, 0:1], ALU.is_equal))
                    nc.vector.engine_nop().then_inc(to_pe, 1)
                    link(nc.vector.tensor_copy(same_l[:, 1:], same[:, 1:]))
                    link(nc.vector.memset(same_l[:, 0:1], 0.0))
                    link(nc.vector.tensor_scalar(reset[:, :], same_l[:, :], -1.0, BIG, ALU.add, ALU.mult))
                    link(nc.vector.tensor_copy(snext[:, 0:NV - 1], same[:, 1:]))
                    dve.wait_ge(from_pe, 2)
                    link(nc.vector.tensor_copy(snext[:, NV - 1:NV], bank[1][:, 0:1]))
                    link(nc.vector.tensor_scalar(rnext[:, :], snext, -1.0, BIG, ALU.add, ALU.mult))
                    link(nc.vector.memset(rnext[:, NV - 1:NV], -BIG))
                    link(nc.vector.tensor_tensor_scan(fs, same[:, :], same[:, :], 1.0, ALU.mult, ALU.min))
                    link(nc.vector.tensor_tensor_scan(ls[:, ::-1], snext[:, ::-1], snext[:, ::-1], 1.0, ALU.mult, ALU.min))
                    nc.vector.engine_nop().then_inc(to_pe, 1)
                    link(nc.vector.tensor_scalar(fs_neg[:, :], fs, -1.0, BIG, ALU.add, ALU.mult))
                    link(nc.vector.tensor_scalar(ls_neg[:, :], ls, -1.0, BIG, ALU.add, ALU.mult))
                    dve.wait_ge(from_pe, 4)
                    link(nc.vector.tensor_copy(colB[:, 0:1], same[:, 0:1]))
                    link(nc.vector.tensor_tensor(colB[:, 1:2], same[:, 0:1], bank[2][:, 0:1], ALU.mult))
                    link(nc.vector.tensor_copy(colB[:, 2:3], snext[:, NV - 1:NV]))
                    link(nc.vector.tensor_tensor(colB[:, 3:4], snext[:, NV - 1:NV], bank[3][:, 0:1], ALU.mult))
                    for k in range(4):
                        link(nc.vector.tensor_scalar(srows[:, k * P:(k + 1) * P], ones[:, :], colB[:, k:k + 1], None, ALU.mult))
                        nc.vector.engine_nop().then_inc(to_pe, 1)
                    dve.wait_ge(from_pe, 8)
                    link(nc.vector.tensor_copy(link_row[:, :], bank[4][:, 0:P]))
                    link(nc.vector.tensor_copy(cont_row[:, :], bank[5][:, 0:P]))
                    for k in range(4):
                        link(nc.vector.tensor_scalar(neg_rows[:, k * P:(k + 1) * P], bank[4 + k][:, 0:P], -1.0, BIG, ALU.add, ALU.mult))
                    link(nc.vector.tensor_scalar(last, snext, -1.0, -1.0, ALU.add, ALU.mult))
                    link(nc.vector.tensor_scalar(dump, vidx, float(NP), None, ALU.add))
                    link(nc.vector.scalar_tensor_tensor(tA, vn1, -1.0, dump, ALU.add, ALU.subtract))
                    link(nc.vector.tensor_tensor(tA, tA, last, ALU.mult))
                    link(nc.vector.tensor_tensor(lpos.bitcast(I32), tA, dump, ALU.add))
                    r3 = rec3i.rearrange("p (j c) -> p j c", c=2)
                    link(nc.vector.tensor_copy(r3[:, :, 0], vidx))
                    link(nc.vector.tensor_scalar(tB, fs, lane_m, None, ALU.mult))
                    link(nc.vector.tensor_scalar(r3[:, :, 1], tB, float(P), None, ALU.add))
                    nc.vector.engine_nop().then_inc(to_pe, 1)

        STEPS = NV // 4

        def index_copies(act, i, half, with_q):
            nc.scalar.copy(idx_slot[:, half * 2 * K:(half + 1) * 2 * K], src_idx[:, bass.ds(4 * K * i + 2 * K * half, 2 * K)] if not isinstance(i, int)
                           else src_idx[:, 4 * K * i + 2 * K * half:4 * K * i + 2 * K * half + 2 * K]).then_inc(with_q[0], 1)
            if len(with_q) > 1:
                nc.scalar.copy(qidx_slot[:, half * 2:(half + 1) * 2], q_idx[:, bass.ds(4 * i + 2 * half, 2)] if not isinstance(i, int)
                               else q_idx[:, 4 * i + 2 * half:4 * i + 2 * half + 2]).then_inc(with_q[0], 1)

        def gather_step(tab, width, u, slot_in, q):
            for s in range(K):
                nc.gpsimd.indirect_dma_start(
                    out=ring[:, (u * K + s) * width:(u * K + s + 1) * width], out_offset=None, in_=tab,
                    in_offset=bass.IndirectOffsetOnAxis(ap=idx_slot[:, u * K + s:u * K + s + 1], axis=0)).then_inc(slot_in[u], 16)
            if q:
                nc.gpsimd.indirect_dma_start(
                    out=qring[:, u * D:(u + 1) * D], out_offset=None, in_=q_tab,
                    in_offset=bass.IndirectOffsetOnAxis(ap=qidx_slot[:, u:u + 1], axis=0)).then_inc(slot_in[u], 16)

        def conv_edges():
            with ExitStack() as ph:
                s0, s1, s2, s3 = dma_sems("slot0", "slot1", "slot2", "slot3")
                idx_ready, dve_step, exp_done, cleared = fresh(ph, "idx_ready", "dve_step", "exp_done", "cleared")
                slot_in = (s0, s1, s2, s3)
                PER = 16 * (K + 1)
                OPS = 8
                kv = ring[:, :].rearrange("p (u s c) -> p u s c", u=4, s=K)
                al = small[:, 0:2 * 3 * K * HEADS].rearrange("p (r k c) -> p r k c", r=2, k=3)
                ex = small[:, 256:256 + 2 * K * HEADS].rearrange("p (r c) -> p r c", r=2)
                with nc.Block() as block:
                    @block.gpsimd
                    def _(pool):
                        pool.wait_ge(idx_ready, 4)
                        for u in range(4):
                            if u == 3:
                                pool.wait_ge(dve_step, 2)
                            gather_step(kv_tab, 2 * D, u, slot_in, True)
                        with nc.gpsimd.Fori(1, STEPS) as i:
                            for u in range(4):
                                if u % 2 == 0:
                                    pool.wait_ge(idx_ready, 4 * i + 2 * (u // 2) + 2)
                                    nc.gpsimd.nop(nofuse=True)
                                pool.wait_ge(dve_step, OPS * (4 * i + u - 3) + 2)
                                nc.gpsimd.nop(nofuse=True)
                                gather_step(kv_tab, 2 * D, u, slot_in, True)

                    @block.scalar
                    def _(act):
                        for half in range(2):
                            index_copies(act, 0, half, (idx_ready, True))
                        with nc.scalar.Fori(0, STEPS) as i:
                            for u in range(4):
                                act.wait_ge(dve_step, OPS * (4 * i + u + 1))
                                nc.scalar.activation(ex[:, u % 2, :], al[:, u % 2, 2, :], ACT.Exp).then_inc(exp_done, 1)
                                if u % 2 == 1:
                                    act.wait_ge(slot_in[u - 1], PER * (i + 1))
                                    act.wait_ge(slot_in[u], PER * (i + 1))
                                    index_copies(act, i + 1, u // 2, (idx_ready, True))

                    @block.vector
                    def _(dve):
                        nc.vector.memset(kv[:, 3, :, :], 0.0).then_inc(cleared, 1)
                        nc.vector.memset(ex[:, 1, :], 0.0).then_inc(cleared, 1)
                        dve.wait_ge(cleared, 2)

                        def weigh(u, at, k):
                            w = (u - 1) % 4
                            nc.vector.tensor_tensor(
                                pv[:, (u - 1) % 2 * K * D:((u - 1) % 2 + 1) * K * D].rearrange("p (s h c) -> p s h c", s=K, h=HEADS),
                                kv[:, w, :, D:].rearrange("p s (h c) -> p s h c", h=HEADS),
                                ex[:, (u - 1) % 2, :].rearrange("p (s h) -> p s h", s=K).unsqueeze(3).to_broadcast([P, K, HEADS, CH]),
                                ALU.mult).then_inc(dve_step, 1)

                        def add_up(u, at, first):
                            dve.wait_ge(dve_step, first)
                            nc.vector.tensor_reduce(sums[:, bass.ds(at * W, D)],
                                                    pv[:, (u - 1) % 2 * K * D:((u - 1) % 2 + 1) * K * D].rearrange("p (s f) -> p f s", s=K), AX_X, ALU.add).then_inc(dve_step, 1)
                            nc.vector.tensor_reduce(sums[:, bass.ds(at * W + D, HEADS)],
                                                    ex[:, (u - 1) % 2, :].rearrange("p (s h) -> p h s", s=K), AX_X, ALU.add).then_inc(dve_step, 1)

                        with nc.vector.Fori(0, STEPS) as i:
                            for u in range(4):
                                t = 4 * i + u
                                r = u % 2
                                done = OPS * t
                                pr = prod[:, r * K * D:(r + 1) * K * D]
                                dve.wait_ge(slot_in[u], PER * (i + 1))
                                nc.vector.tensor_tensor(pr.rearrange("p (s c) -> p s c", s=K), kv[:, u, :, 0:D],
                                                        qring[:, u * D:(u + 1) * D].unsqueeze(1).to_broadcast([P, K, D]), ALU.mult).then_inc(dve_step, 1)
                                dve.wait_ge(exp_done, t)
                                weigh(u, t, 2)
                                dve.wait_ge(dve_step, done + 1)
                                nc.vector.tensor_reduce(al[:, r, 0, :], pr.rearrange("p (a c) -> p a c", c=CH), AX_X, ALU.add).then_inc(dve_step, 1)
                                add_up(u, t, done + 2)
                                a0 = al[:, r, 0, :].rearrange("p (s h) -> p s h", s=K)
                                a1 = al[:, r, 1, :].rearrange("p (s h) -> p s h", s=K)
                                a2 = al[:, r, 2, :].rearrange("p (s h) -> p s h", s=K)
                                dve.wait_ge(dve_step, done + 3)
                                nc.vector.scalar_tensor_tensor(a1, a0, SCALE, maskneg[:, bass.ds(t * K, K)].unsqueeze(2).to_broadcast([P, K, HEADS]),
                                                               ALU.mult, ALU.add).then_inc(dve_step, 1)
                                dve.wait_ge(dve_step, done + 6)
                                nc.vector.tensor_reduce(rowmax[:, bass.ds(t * HEADS, HEADS)], al[:, r, 1, :].rearrange("p (s h) -> p h s", s=K), AX_X, ALU.max).then_inc(dve_step, 1)
                                dve.wait_ge(dve_step, done + 7)
                                nc.vector.tensor_tensor(a2, a1, rowmax[:, bass.ds(t * HEADS, HEADS)].unsqueeze(1).to_broadcast([P, K, HEADS]), ALU.subtract).then_inc(dve_step, 1)
                        dve.wait_ge(exp_done, NV)
                        weigh(4, NV, 2)
                        add_up(4, NV, OPS * NV + 1)
                        dve.wait_ge(dve_step, OPS * NV + 3)

        def segment_max():
            with ExitStack() as ph:
                step, to_pe, from_pe, exp_done = fresh(ph, "max_step", "to_pe", "from_pe", "exp_done")
                fwd = ring[:, 0:HEADS * NV].rearrange("p (h j) -> p h j", h=HEADS)
                seg_max = ring[:, HEADS * NV:2 * HEADS * NV].rearrange("p (h j) -> p h j", h=HEADS)
                rm = rowmax[:, :].rearrange("p (j h) -> p j h", h=HEADS)
                ends = small[:, 0:2 * HEADS]
                tails, heads = small[0:HEADS, 32:32 + P + 1], small[0:HEADS, 192:192 + P + 1]
                cf, cb = small[0:HEADS, 352:352 + P], small[0:HEADS, 512:512 + P]
                cfb = small[:, 680:680 + 2 * HEADS]
                with nc.Block() as block:
                    @block.tensor
                    def _(pe):
                        pe.wait_ge(to_pe, 1)
                        nc.tensor.transpose(bank[0][0:HEADS, 0:P], ends[:, 0:HEADS], ident[:, :])
                        nc.tensor.transpose(bank[1][0:HEADS, 0:P], ends[:, HEADS:2 * HEADS], ident[:, :]).then_inc(from_pe, 1)
                        pe.wait_ge(to_pe, 2)
                        nc.tensor.transpose(bank[2][:, 0:HEADS], cf, ident[0:HEADS, 0:HEADS])
                        nc.tensor.transpose(bank[3][:, 0:HEADS], cb, ident[0:HEADS, 0:HEADS]).then_inc(from_pe, 1)

                    @block.scalar
                    def _(act):
                        act.wait_ge(to_pe, 3)
                        nc.scalar.activation(rowmax[:, :], rowmax[:, :], ACT.Exp).then_inc(exp_done, 1)

                    @block.vector
                    def _(dve):
                        link = Chain(dve, step)
                        for h in range(HEADS):
                            link(nc.vector.tensor_tensor_scan(fwd[:, h, :], reset[:, :], rm[:, :, h], -BIG, ALU.add, ALU.max))
                            link(nc.vector.tensor_tensor_scan(seg_max[:, h, ::-1], rnext[:, ::-1], fwd[:, h, ::-1], -BIG, ALU.add, ALU.max))
                        link(nc.vector.tensor_copy(ends[:, 0:HEADS], fwd[:, :, NV - 1]))
                        link(nc.vector.tensor_copy(ends[:, HEADS:], seg_max[:, :, 0]))
                        nc.vector.engine_nop().then_inc(to_pe, 1)
                        link(nc.vector.memset(tails[:, 0:1], 0.0))
                        link(nc.vector.memset(heads[:, P:P + 1], 0.0))
                        dve.wait_ge(from_pe, 1)
                        link(nc.vector.tensor_copy(tails[:, 1:P + 1], bank[0][0:HEADS, 0:P]))
                        link(nc.vector.tensor_copy(heads[:, 0:P], bank[1][0:HEADS, 0:P]))
                        link(nc.vector.tensor_tensor(tails[:, 0:P], tails[:, 0:P], neg_rows[0:HEADS, 0:P], ALU.add))
                        link(nc.vector.tensor_tensor(heads[:, 1:P + 1], heads[:, 1:P + 1], neg_rows[0:HEADS, 2 * P:3 * P], ALU.add))
                        link(nc.vector.tensor_tensor_scan(cf, neg_rows[0:HEADS, P:2 * P], tails[:, 0:P], -BIG, ALU.add, ALU.max))
                        link(nc.vector.tensor_tensor_scan(cb[:, ::-1], neg_rows[0:HEADS, 3 * P:4 * P][:, ::-1], heads[:, 1:P + 1][:, ::-1], -BIG, ALU.add, ALU.max))
                        nc.vector.engine_nop().then_inc(to_pe, 1)
                        dve.wait_ge(from_pe, 2)
                        link(nc.vector.tensor_copy(cfb[:, 0:HEADS], bank[2][:, 0:HEADS]))
                        link(nc.vector.tensor_copy(cfb[:, HEADS:], bank[3][:, 0:HEADS]))
                        for h in range(HEADS):
                            link(nc.vector.scalar_tensor_tensor(seg_max[:, h, :], fs_neg[:, :], cfb[:, h:h + 1], seg_max[:, h, :], ALU.add, ALU.max))
                            link(nc.vector.scalar_tensor_tensor(seg_max[:, h, :], ls_neg[:, :], cfb[:, HEADS + h:HEADS + h + 1], seg_max[:, h, :], ALU.add, ALU.max))
                        link(nc.vector.tensor_tensor(rm, rm, ring[:, HEADS * NV:2 * HEADS * NV].rearrange("p (h j) -> p j h", h=HEADS), ALU.subtract))
                        nc.vector.engine_nop().then_inc(to_pe, 1)
                        dve.wait_ge(exp_done, 1)
                        body = sums3[:, 1:, 0:D].rearrange("p j (h c) -> p j h c", h=HEADS)
                        link(nc.vector.tensor_tensor(body, body, rm.unsqueeze(3).to_broadcast([P, NV, HEADS, CH]), ALU.mult))
                        link(nc.vector.tensor_tensor(sums3[:, 1:, D:], sums3[:, 1:, D:], rm, ALU.mult))
                        base = link.n
                        with nc.vector.Fori(0, W) as c:
                            col = sums3[:, 1:, bass.ds(c, 1)].rearrange("p j o -> p (j o)")
                            nc.vector.tensor_tensor_scan(col, same_l[:, :], col, 0.0, ALU.mult, ALU.add).then_inc(step, 1)
                        dve.wait_ge(step, base + W)

        def carry_and_gather():
            with ExitStack() as ph:
                g_in, c_in = dma_sems("agg_in", "car_in")
                step, to_pe, from_pe, out_done, car_done, carry_ready = fresh(ph, "carry_step", "to_pe", "from_pe", "sums_out", "carry_out", "carry_ready")
                tails = ring[:, 0:P + 1]
                tails8 = ring[0:HEADS, 200:200 + P + 1]
                c_t, c8 = ring[:, 400:400 + P], ring[0:HEADS, 600:600 + P]
                carry = ring[:, 800:800 + W]
                with nc.Block() as block:
                    @block.sync
                    def _(sp):
                        sp.dma_start(sums_tab[0:ROWS, :].rearrange("(p j) f -> p (j f)", j=NV), sums[:, W:]).then_inc(out_done, 16)
                        sp.wait_ge(carry_ready, 1)
                        sp.dma_start(carry_tab[0:P, :], carry).then_inc(car_done, 16)
                        sp.wait_ge(out_done, 16)
                        sp.wait_ge(car_done, 16)

                    @block.tensor
                    def _(pe):
                        nc.tensor.transpose(bank[0][:, 0:P], sums3[:, NV, 0:D], ident[:, :])
                        nc.tensor.transpose(bank[1][0:HEADS, 0:P], sums3[:, NV, D:], ident[:, :]).then_inc(from_pe, 1)
                        pe.wait_ge(to_pe, 1)
                        nc.tensor.transpose(bank[2][:, 0:D], c_t, ident[:, :])
                        nc.tensor.transpose(bank[3][:, 0:HEADS], c8, ident[0:HEADS, 0:HEADS]).then_inc(from_pe, 1)

                    @block.vector
                    def _(dve):
                        link = Chain(dve, step)
                        link(nc.vector.memset(tails[:, 0:1], 0.0))
                        link(nc.vector.memset(tails8[:, 0:1], 0.0))
                        dve.wait_ge(from_pe, 1)
                        link(nc.vector.tensor_copy(tails[:, 1:], bank[0][:, 0:P]))
                        link(nc.vector.tensor_copy(tails8[:, 1:], bank[1][0:HEADS, 0:P]))
                        link(nc.vector.tensor_tensor(tails[:, 0:P], tails[:, 0:P], link_row[:, :], ALU.mult))
                        link(nc.vector.tensor_tensor(tails8[:, 0:P], tails8[:, 0:P], link_row[0:HEADS, :], ALU.mult))
                        link(nc.vector.tensor_tensor_scan(c_t, cont_row[:, :], tails[:, 0:P], 0.0, ALU.mult, ALU.add))
                        link(nc.vector.tensor_tensor_scan(c8, cont_row[0:HEADS, :], tails8[:, 0:P], 0.0, ALU.mult, ALU.add))
                        nc.vector.engine_nop().then_inc(to_pe, 1)
                        dve.wait_ge(from_pe, 2)
                        link(nc.vector.tensor_copy(carry[:, 0:D], bank[2][:, 0:D]))
                        link(nc.vector.tensor_copy(carry[:, D:], bank[3][:, 0:HEADS]))
                        nc.vector.engine_nop().then_inc(carry_ready, 1)
                        dve.wait_ge(g_in, 16 * NT)
                        dve.wait_ge(c_in, 16 * NT)
                        link(nc.vector.tensor_tensor(agg, agg, car, ALU.add))

                    @block.gpsimd
                    def _(pool):
                        pool.wait_ge(out_done, 16)
                        pool.wait_ge(car_done, 16)
                        for t in range(NT):
                            nc.gpsimd.indirect_dma_start(out=agg[:, t, :], out_offset=None, in_=sums_tab,
                                                         in_offset=bass.IndirectOffsetOnAxis(ap=last_idx[:, 2 * t:2 * t + 1], axis=0)).then_inc(g_in, 16)
                            nc.gpsimd.indirect_dma_start(out=car[:, t, :], out_offset=None, in_=carry_tab,
                                                         in_offset=bass.IndirectOffsetOnAxis(ap=last_idx[:, 2 * t + 1:2 * t + 2], axis=0)).then_inc(c_in, 16)

        def norm_ops(link, act_sqrt, src3, dst3, after=None):
            mean, var, inv, tmp = (col25[:, k * NT:(k + 1) * NT] for k in range(4))
            bc = lambda c: c.unsqueeze(2).to_broadcast([P, NT, D])
            link(nc.vector.tensor_reduce(mean, src3, AX_X, ALU.add))
            link(nc.vector.tensor_scalar(mean, mean, 1.0 / D, None, ALU.mult))
            link(nc.vector.tensor_tensor(dst3, src3, bc(mean), ALU.subtract))
            link(nc.vector.tensor_tensor(sq3, dst3, dst3, ALU.mult))
            link(nc.vector.tensor_reduce(var, sq3, AX_X, ALU.add))
            link(nc.vector.tensor_scalar(var, var, 1.0 / D, LN_EPS, ALU.mult, ALU.add))
            act_sqrt(var, tmp)
            link(nc.vector.reciprocal(inv, tmp))
            link(nc.vector.tensor_tensor(dst3, dst3, bc(inv), ALU.mult))

        def node_math(body, roots):
            with ExitStack() as ph:
                step, to_act, from_act = fresh(ph, "math_step", "to_act", "from_act")
                asked = []
                with nc.Block() as block:
                    @block.vector
                    def _(dve):
                        link = Chain(dve, step)

                        def on_act(func):
                            def run(src, dst, **kw):
                                asked.append((func, src, dst, kw))
                                nc.vector.engine_nop().then_inc(to_act, 1)
                                dve.wait_ge(from_act, len(asked))
                            return run
                        body(link, on_act)

                    @block.scalar
                    def _(act):
                        for n, (func, src, dst, kw) in enumerate(roots):
                            act.wait_ge(to_act, n + 1)
                            nc.scalar.activation(dst, src, func, **kw).then_inc(from_act, 1)
                assert [(f, k) for f, _, _, k in asked] == [(f, k) for f, _, _, k in roots]

        SQRT = (ACT.Sqrt, col25[:, NT:2 * NT], col25[:, 3 * NT:4 * NT], {})

        def node_linear(sources, loads, cols, parts, tabs):
            with ExitStack() as ph:
                w_in, staged, tr_done, copied, mm_done, evac, tab_out = fresh(ph, "w_in", "staged", "tr_done", "copied", "mm_done", "evac", "tab_out")
                ins = (stage_in, stage_in2)[:len(sources)]
                outs = (stage_T, stage_T2)[:len(sources)]
                S = len(sources)
                with nc.Block() as block:
                    @block.sync
                    def _(sp):
                        for dst, src in loads:
                            sp.dma_start(dst, src).then_inc(w_in, 16)
                        sp.wait_ge(w_in, 16 * len(loads))
                        sp.wait_ge(evac, NT * len(parts))
                        for dst, src in tabs:
                            sp.dma_start(dst, src).then_inc(tab_out, 16)
                        sp.wait_ge(tab_out, 16 * len(tabs))

                    @block.scalar
                    def _(act):
                        with nc.scalar.Fori(0, NT // U) as i:
                            for s in range(S):
                                act.wait_ge(tr_done, S * i)
                                nc.scalar.copy(ins[s], sources[s][:, bass.ds(U * D * i, U * D)]).then_inc(staged, 1)
                            for s in range(S):
                                act.wait_ge(tr_done, S * i + s + 1)
                                act.wait_ge(mm_done, U * i)
                                nc.scalar.copy(outs[s][:, 0:512], bank[2 * s][:, 0:512]).then_inc(copied, 1)
                                nc.scalar.copy(outs[s][:, 512:U * D], bank[2 * s + 1][:, 0:U * D - 512]).then_inc(copied, 1)

                    @block.tensor
                    def _(pe):
                        pe.wait_ge(w_in, 16 * len(loads))
                        with nc.tensor.Fori(0, NT // U) as i:
                            for s in range(S):
                                pe.wait_ge(staged, S * i + s + 1)
                                pe.wait_ge(copied, 2 * S * i)
                                for u in range(U):
                                    ins_ = nc.tensor.transpose(bank[2 * s + u // 4][:, (u % 4) * P:(u % 4 + 1) * P], ins[s][:, u * D:(u + 1) * D], ident[:, :])
                                ins_.then_inc(tr_done, 1)
                            pe.wait_ge(copied, 2 * S * (i + 1))
                            for u in range(U):
                                b = bank[4 + u % 4]
                                pe.wait_ge(evac, len(parts) * (U * i + max(u - 3, 0)))
                                for s in range(S):
                                    ins_ = nc.tensor.matmul(b[:, 0:cols], outs[s][:, u * D:(u + 1) * D], wgt[:, s * cols:(s + 1) * cols], start=(s == 0), stop=(s == S - 1))
                                ins_.then_inc(mm_done, 1)

                    @block.vector
                    def _(dve):
                        dve.wait_ge(w_in, 16 * len(loads))
                        with nc.vector.Fori(0, NT // U) as i:
                            for u in range(U):
                                dve.wait_ge(mm_done, U * i + u + 1)
                                for dst, stride, lo, hi in parts:
                                    nc.vector.tensor_tensor(dst[:, bass.ds((U * i + u) * stride, hi - lo)], bank[4 + u % 4][:, lo:hi], bias[:, lo:hi], ALU.add).then_inc(evac, 1)

        def gine_edges():
            with ExitStack() as ph:
                s0, s1, s2, s3 = dma_sems("slot0", "slot1", "slot2", "slot3")
                idx_ready, rec_in0, rec_in1, tr_done, rt_done, mm_done, dve_step, relu_done, run0 = fresh(
                    ph, "idx_ready", "rec_in0", "rec_in1", "tr_done", "rt_done", "mm_done", "dve_step", "relu_done", "run0")
                slot_in = (s0, s1, s2, s3)
                rec_in = (rec_in0, rec_in1)
                PER = 16 * K
                KR = K * REC
                recs_r = ring[:, 4 * K * D:4 * K * D + 4 * KR]
                rec_t = ring[:, 4 * K * D + 512:4 * K * D + 512 + 2 * P]
                rv = recs.rearrange("(p j) c -> p (j c)", j=NS)
                with nc.Block() as block:
                    @block.gpsimd
                    def _(pool):
                        pool.wait_ge(idx_ready, 2)
                        for u in range(4):
                            gather_step(h_tab, D, u, slot_in, False)
                        with nc.gpsimd.Fori(1, STEPS) as i:
                            for u in range(4):
                                if u % 2 == 0:
                                    pool.wait_ge(idx_ready, 2 * i + u // 2 + 1)
                                    nc.gpsimd.nop(nofuse=True)
                                pool.wait_ge(dve_step, 4 * (4 * i + u - 3) - 3)
                                nc.gpsimd.nop(nofuse=True)
                                gather_step(h_tab, D, u, slot_in, False)

                    @block.sync
                    def _(sp):
                        with nc.sync.Fori(0, STEPS) as i:
                            for half in range(2):
                                sp.wait_ge(tr_done, 4 * i)
                                sp.dma_start(recs_r[:, half * 2 * KR:(half + 1) * 2 * KR], rv[:, bass.ds((4 * i + 2 * half) * KR, 2 * KR)]).then_inc(rec_in[half], 16)

                    @block.tensor
                    def _(pe):
                        with nc.tensor.Fori(0, STEPS) as i:
                            for u in range(4):
                                t = 4 * i + u
                                if u % 2 == 0:
                                    pe.wait_ge(rec_in[u // 2], 16 * (i + 1))
                                pe.wait_ge(rt_done, 4 * i + max(u - 1, 0))
                                nc.tensor.transpose(bank[u % 2][0:KR, 0:P], recs_r[:, u * KR:(u + 1) * KR], ident[:, :]).then_inc(tr_done, 1)
                                pe.wait_ge(rt_done, t + 1)
                                pe.wait_ge(dve_step, 4 * 4 * i if u < 2 else 4 * (4 * i + u - 1) - 3)
                                nc.tensor.matmul(bank[2 + u % 2][:, 0:K * D], rec_t[0:KR, (u % 2) * P:(u % 2 + 1) * P], wgt[0:KR, 0:K * D], start=True, stop=True).then_inc(mm_done, 1)

                    @block.scalar
                    def _(act):
                        for half in range(2):
                            index_copies(act, 0, half, (idx_ready,))
                        with nc.scalar.Fori(0, STEPS) as i:
                            for u in range(4):
                                t = 4 * i + u
                                act.wait_ge(tr_done, t + 1)
                                act.wait_ge(mm_done, 4 * i + max(u - 1, 0))
                                nc.scalar.copy(rec_t[0:KR, (u % 2) * P:(u % 2 + 1) * P], bank[u % 2][0:KR, 0:P]).then_inc(rt_done, 1)
                                act.wait_ge(dve_step, 4 * t + 1)
                                pr = prod[:, (u % 2) * K * D:(u % 2 + 1) * K * D]
                                nc.scalar.activation(pr, pr, ACT.Relu).then_inc(relu_done, 1)
                                if u % 2 == 1:
                                    act.wait_ge(slot_in[u - 1], PER * (i + 1))
                                    act.wait_ge(slot_in[u], PER * (i + 1))
                                    index_copies(act, i + 1, u // 2, (idx_ready,))

                    @block.vector
                    def _(dve):
                        nc.vector.memset(sums3[:, 0, :], 0.0).then_inc(run0, 1)
                        nc.vector.memset(sums3[:, 1:, D:], 0.0).then_inc(run0, 1)
                        dve.wait_ge(run0, 2)
                        with nc.vector.Fori(0, STEPS) as i:
                            for u in range(4):
                                t = 4 * i + u
                                pr = prod[:, (u % 2) * K * D:(u % 2 + 1) * K * D]
                                pw = pv[:, 0:K * D]
                                tmp = pv[:, K * D:K * D + D]
                                dve.wait_ge(slot_in[u], PER * (i + 1))
                                dve.wait_ge(mm_done, t + 1)
                                nc.vector.tensor_tensor(pr, bank[2 + u % 2][:, 0:K * D], ring[:, u * K * D:(u + 1) * K * D], ALU.add).then_inc(dve_step, 1)
                                dve.wait_ge(relu_done, t + 1)
                                dve.wait_ge(dve_step, 4 * t)
                                nc.vector.tensor_tensor(pw.rearrange("p (s f) -> p s f", s=K), pr.rearrange("p (s f) -> p s f", s=K),
                                                        weight[:, bass.ds(t * K, K)].unsqueeze(2).to_broadcast([P, K, D]), ALU.mult).then_inc(dve_step, 1)
                                dve.wait_ge(dve_step, 4 * t + 2)
                                nc.vector.tensor_reduce(tmp, pw.rearrange("p (s f) -> p f s", s=K), AX_X, ALU.add).then_inc(dve_step, 1)
                                dve.wait_ge(dve_step, 4 * t + 3)
                                nc.vector.scalar_tensor_tensor(sums[:, bass.ds((t + 1) * W, D)], sums[:, bass.ds(t * W, D)], same_l[:, bass.ds(t, 1)], tmp,
                                                               ALU.mult, ALU.add).then_inc(dve_step, 1)
                        dve.wait_ge(dve_step, 4 * NV)

        bn = sb("bn", 5 * 3)
        bnc = sb("bnc", 4 * 3)
        epsb = sb("epsb", 4)

        def gine_nodes(layer):
            with ExitStack() as ph:
                w_in, step, z_ready, staged, tr_done, copied, m1_done, y_done, m2_done, evac, tab_out, root = fresh(
                    ph, "w_in", "mlp_step", "z_ready", "staged", "tr_done", "copied", "m1_done", "y_done", "m2_done", "evac", "tab_out", "root")
                scale, shift = bnc[:, 0:1], bnc[:, 1:2]
                pick = lambda k: bn[:, 3 * k + layer:3 * k + layer + 1]
                with nc.Block() as block:
                    @block.sync
                    def _(sp):
                        sp.dma_start(wgt[:, 0:D], a["L2_W1"][layer]).then_inc(w_in, 16)
                        sp.dma_start(wgt[:, D:2 * D], a["L2_W2"][layer]).then_inc(w_in, 16)
                        sp.dma_start(bias[:, 0:D], a["L2_b2"][layer:layer + 1, :].to_broadcast([P, D])).then_inc(w_in, 16)
                        sp.wait_ge(evac, 2 * NT)
                        sp.dma_start(table(h_tab), skip3).then_inc(tab_out, 16)
                        sp.wait_ge(tab_out, 16)

                    @block.vector
                    def _(dve):
                        link = Chain(dve, step)
                        link(nc.vector.tensor_scalar(epsb[:, 3:4], epsb[:, layer:layer + 1], 1.0, None, ALU.add))
                        link(nc.vector.scalar_tensor_tensor(work3, skip3, epsb[:, 3:4], agg[:, :, 0:D], ALU.mult, ALU.add))
                        nc.vector.engine_nop().then_inc(z_ready, 1)
                        link(nc.vector.tensor_scalar(bnc[:, 2:3], pick(3), LN_EPS, None, ALU.add))
                        nc.vector.engine_nop().then_inc(z_ready, 1)
                        dve.wait_ge(root, 1)
                        link(nc.vector.reciprocal(bnc[:, 2:3], bnc[:, 3:4]))
                        link(nc.vector.tensor_tensor(scale, bnc[:, 2:3], pick(0), ALU.mult))
                        link(nc.vector.tensor_tensor(bnc[:, 4:5], pick(4), pick(2), ALU.subtract))
                        link(nc.vector.scalar_tensor_tensor(shift, bnc[:, 4:5], scale, pick(1), ALU.mult, ALU.add))
                        nc.vector.engine_nop().then_inc(z_ready, 1)
                        dve.wait_ge(w_in, 48)
                        with nc.vector.Fori(0, NT // U) as i:
                            for u in range(U):
                                h = skip[:, bass.ds((U * i + u) * D, D)]
                                dve.wait_ge(m2_done, U * i + u + 1)
                                nc.vector.tensor_tensor(h, bank[4 + u % 4][:, 0:D], bias[:, 0:D], ALU.add).then_inc(evac, 1)
                                dve.wait_ge(evac, 2 * (U * i + u) + 1)
                                nc.vector.tensor_scalar(h, h, 0.0, None, ALU.max).then_inc(evac, 1)

                    @block.scalar
                    def _(act):
                        act.wait_ge(z_ready, 2)
                        nc.scalar.activation(bnc[:, 3:4], bnc[:, 2:3], ACT.Sqrt).then_inc(root, 1)
                        act.wait_ge(z_ready, 3)
                        with nc.scalar.Fori(0, NT // U) as i:
                            act.wait_ge(tr_done, i)
                            nc.scalar.copy(stage_in, work[:, bass.ds(U * D * i, U * D)]).then_inc(staged, 1)
                            act.wait_ge(tr_done, i + 1)
                            act.wait_ge(m1_done, i)
                            nc.scalar.copy(stage_T[:, 0:512], bank[0][:, 0:512]).then_inc(copied, 1)
                            nc.scalar.copy(stage_T[:, 512:U * D], bank[1][:, 0:U * D - 512]).then_inc(copied, 1)
                            act.wait_ge(m1_done, i + 1)
                            act.wait_ge(m2_done, U * i)
                            nc.scalar.activation(stage_y[:, 0:512], bank[2][:, 0:512], ACT.Relu, bias=shift, scale=scale).then_inc(y_done, 1)
                            nc.scalar.activation(stage_y[:, 512:U * D], bank[3][:, 0:U * D - 512], ACT.Relu, bias=shift, scale=scale).then_inc(y_done, 1)

                    @block.tensor
                    def _(pe):
                        pe.wait_ge(w_in, 48)
                        with nc.tensor.Fori(0, NT // U) as i:
                            pe.wait_ge(staged, i + 1)
                            pe.wait_ge(copied, 2 * i)
                            for u in range(U):
                                ins_ = nc.tensor.transpose(bank[u // 4][:, (u % 4) * P:(u % 4 + 1) * P], stage_in[:, u * D:(u + 1) * D], ident[:, :])
                            ins_.then_inc(tr_done, 1)
                            pe.wait_ge(copied, 2 * (i + 1))
                            pe.wait_ge(y_done, 2 * i)
                            nc.tensor.matmul(bank[2][:, 0:512], wgt[:, 0:D], stage_T[:, 0:512], start=True, stop=True)
                            nc.tensor.matmul(bank[3][:, 0:U * D - 512], wgt[:, 0:D], stage_T[:, 512:U * D], start=True, stop=True).then_inc(m1_done, 1)
                            pe.wait_ge(y_done, 2 * (i + 1))
                            for u in range(U):
                                pe.wait_ge(evac, 2 * (U * i + max(u - 3, 0)))
                                nc.tensor.matmul(bank[4 + u % 4][:, 0:D], stage_y[:, u * D:(u + 1) * D], wgt[:, D:2 * D], start=True, stop=True).then_inc(m2_done, 1)

        for c in range(2):
            src = x if c == 0 else work
            loads = []
            for k, n in enumerate("qkvs"):
                loads.append((wgt[:, k * D:(k + 1) * D], a[f"L0_{n}_w{c}"]))
                loads.append((bias[:, k * D:(k + 1) * D], a[f"L0_{n}_b{c}"].to_broadcast([P, D])))
            node_linear([src[:, :] if c == 0 else work], loads, 4 * D,
                        [(area(10000, NT * 384), 384, 0, 384), (skip[:, :], D, 384, 512)],
                        [(table(q_tab), proj3[:, :, 0:D]), (table(kv_tab), proj3[:, :, D:3 * D])])
            conv_edges()
            segment_max()
            carry_and_gather()

            def conv_nodes(link, on_act):
                den = sq3[:, :, 0:HEADS]
                link(nc.vector.tensor_scalar(den, agg[:, :, D:], 1e-30, None, ALU.max))
                link(nc.vector.reciprocal(den, den))
                body = agg[:, :, 0:D].rearrange("p t (h c) -> p t h c", h=HEADS)
                link(nc.vector.tensor_tensor(body, body, den.unsqueeze(3).to_broadcast([P, NT, HEADS, CH]), ALU.mult))
                link(nc.vector.tensor_tensor(work3, agg[:, :, 0:D], skip3, ALU.add))
                if c == 0:
                    link(nc.vector.tensor_scalar(work, work, 0.0, None, ALU.max))
                else:
                    link(nc.vector.tensor_tensor(work3, work3, x3, ALU.add))
                    norm_ops(link, on_act(ACT.Sqrt), work3, x3)
            node_math(conv_nodes, [] if c == 0 else [SQRT])

        NPF = NP
        cnt_buf = [area(k * NPF, NPF) for k in range(3)]
        own = [area((3 + k) * NPF, NPF) for k in range(3)]
        s1bc, e_steep, e_flat = area(6 * NPF, NPF), area(7 * NPF, NPF), area(8 * NPF + 704, NPF)
        tailoff = 8 * NPF
        a12, s12, s1t, lnwb = (area(tailoff + o_, n_) for o_, n_ in ((0, 2 * D), (256, 2 * NT), (310, P), (440, 2 * D)))
        deg = small[:, 0:NT]
        s2_steep, s2_flat = small[:, 32:32 + NT], small[:, 64:64 + NT]

        def by_src(feat, attention):
            with ExitStack() as ph:
                cin = fresh(ph, "counts_in0", "counts_in1", "counts_in2")
                diff, own_ready, mm_done, e_ready, least, deg_ready = fresh(ph, "diff", "own_ready", "mm_done", "e_ready", "least", "deg_ready")
                with nc.Block() as block:
                    @block.sync
                    def _(sp):
                        for n in range(3):
                            if n == 2:
                                sp.wait_ge(diff, 1)
                            sp.dma_start(cnt_buf[n], count_tab[n * P:(n + 1) * P, :]).then_inc(cin[n], 16)
                        with nc.sync.Fori(0, (NT - 4) // 3) as i:
                            for u in range(3):
                                sp.wait_ge(diff, 3 * i + u + 2)
                                sp.dma_start(cnt_buf[u], count_tab[bass.ds((3 * i + u + 3) * P, P), :]).then_inc(cin[u], 16)
                        sp.wait_ge(diff, NT - 2)
                        sp.dma_start(cnt_buf[(NT - 1) % 3], count_tab[(NT - 1) * P:NT * P, :]).then_inc(cin[(NT - 1) % 3], 16)

                    @block.vector
                    def _(dve):
                        def step(n, u, loads_due, mm_due):
                            dve.wait_ge(cin[u], 16 * loads_due)
                            if mm_due is None:
                                nc.vector.tensor_copy(own[u], cnt_buf[u]).then_inc(diff, 1)
                            else:
                                if mm_due is not False:
                                    dve.wait_ge(mm_done, mm_due)
                                nc.vector.tensor_tensor(own[u], cnt_buf[u], cnt_buf[(u - 1) % 3], ALU.subtract).then_inc(diff, 1)
                            if attention:
                                dve.wait_ge(e_ready, 2 * n + 2)
                                nc.vector.scalar_tensor_tensor(e_steep, e_steep, 3e38, e_flat, ALU.min, ALU.min).then_inc(least, 1)
                                dve.wait_ge(least, n + 1)
                                dve.wait_ge(diff, n + 1)
                                nc.vector.tensor_tensor(own[u], own[u], e_steep, ALU.mult).then_inc(own_ready, 1)
                        step(0, 0, 1, None)
                        for n in (1, 2):
                            step(n, n, 1, False)
                        with nc.vector.Fori(0, (NT - 4) // 3) as i:
                            for u in range(3):
                                step(3 * i + u + 3, u, i + 2, 3 * i + u + 1)
                        step(NT - 1, (NT - 1) % 3, (NT - 1) // 3 + 1, NT - 3)
                        dve.wait_ge(mm_done, NT)
                        if not attention:
                            nc.vector.tensor_scalar(deg, bank[7][:, 0:NT], 1.0, None, ALU.max).then_inc(deg_ready, 1)

                    @block.scalar
                    def _(act):
                        if attention:
                            for n in range(NT):
                                if n > 0:
                                    act.wait_ge(least, n)
                                nc.scalar.activation(e_flat, s1bc, ACT.Exp, scale=-0.2, bias=s2_flat[:, n:n + 1]).then_inc(e_ready, 1)
                                if n > 0:
                                    act.wait_ge(own_ready, n)
                                nc.scalar.activation(e_steep, s1bc, ACT.Exp, scale=-1.0, bias=s2_steep[:, n:n + 1]).then_inc(e_ready, 1)

                    @block.tensor
                    def _(pe):
                        def products(n, u, first):
                            pe.wait_ge(own_ready if attention else diff, n + 1)
                            last_a = NT - 1
                            for a_ in range(NT):
                                w = own[u][:, a_ * P:(a_ + 1) * P]
                                rhs = feat[:, 0:D] if first else feat[:, bass.ds(n * D, D)]
                                kw = dict(start=first and a_ % 4 == 0, stop=True, skip_group_check=True)
                                ins_ = nc.tensor.matmul(bank[a_ // 4][:, (a_ % 4) * D:(a_ % 4 + 1) * D], w, rhs, **kw)
                                if not attention:
                                    ins_ = nc.tensor.matmul(bank[7][:, a_:a_ + 1], w, ones[:, 0:1], start=first and a_ == 0, stop=True, skip_group_check=True)
                            ins_.then_inc(mm_done, 1)
                        products(0, 0, True)
                        for n in (1, 2):
                            products(n, n, False)
                        with nc.tensor.Fori(0, (NT - 4) // 3) as i:
                            for u in range(3):
                                products(3 * i + u + 3, u, False)
                        products(NT - 1, (NT - 1) % 3, False)

        assert (NT - 4) % 3 == 0

        by_src(x, False)

        def mean_nodes(link, on_act):
            inv = s12[:, 0:NT]
            link(nc.vector.reciprocal(inv, deg))
            link(nc.vector.tensor_tensor(mean3, psum[:, 0:NP].rearrange("p (t d) -> p t d", d=D), inv.unsqueeze(2).to_broadcast([P, NT, D]), ALU.mult))
        mean = cnt_buf[0]
        mean3 = mean.rearrange("p (t d) -> p t d", d=D)
        node_math(mean_nodes, [])
        node_linear([x[:, :], mean], [(wgt[:, 0:D], a["L1_WT"][0:D, :]), (wgt[:, D:2 * D], a["L1_WT"][D:2 * D, :]), (bias[:, 0:D], a["L1_b"].to_broadcast([P, D]))],
                    D, [(skip[:, :], D, 0, D)], [])

        def add_norm(link, on_act):
            link(nc.vector.tensor_tensor(work3, skip3, x3, ALU.add))
            norm_ops(link, on_act(ACT.Sqrt), work3, x3)
        node_math(add_norm, [SQRT])

        node_linear([x[:, :]], [(wgt[:, 0:D], a["L2_W_enc"]), (bias[:, 0:D], a["L2_b_enc"].to_broadcast([P, D])),
                                (bn[:, :], a["L2_bn"]), (epsb[:, 0:3], a["L2_eps"].to_broadcast([P, 3]))],
                    D, [(skip[:, :], D, 0, D)], [(table(h_tab), skip3)])
        for layer in range(3):
            with ExitStack() as ph:
                w_in, clear = fresh(ph, "w_in", "clear")
                with nc.Block() as block:
                    @block.vector
                    def _(dve):
                        nc.vector.memset(wgt[:, :], 0.0).then_inc(clear, 1)

                    @block.sync
                    def _(sp):
                        sp.wait_ge(clear, 1)
                        for s in range(K):
                            sp.dma_start(wgt[s * REC:s * REC + EA, s * D:(s + 1) * D], a["L2_W_ee"]).then_inc(w_in, 16)
                            sp.dma_start(wgt[s * REC + R_ONE:s * REC + R_ONE + 1, s * D:(s + 1) * D], a["L2_b_ee"]).then_inc(w_in, 16)
                        sp.wait_ge(w_in, 32 * K)
            gine_edges()
            carry_and_gather()
            gine_nodes(layer)
        node_math(add_norm, [SQRT])

        node_linear([x[:, :]], [(wgt[:, 0:D], a["L3_WT"]), (bias[:, 0:D], a["L3_b"].to_broadcast([P, D])),
                                (a12[:, 0:D], a["L3_a"][:, 0:D].to_broadcast([P, D])), (a12[:, D:], a["L3_a"][:, D:].to_broadcast([P, D])),
                                (lnwb[:, 0:D], a["L3_ln_w"].to_broadcast([P, D])), (lnwb[:, D:], a["L3_ln_b"].to_broadcast([P, D]))], D, [(skip[:, :], D, 0, D)], [])
        hh = cnt_buf[0]
        hh3 = hh.rearrange("p (t d) -> p t d", d=D)
        g_flat = cnt_buf[1]
        with ExitStack() as ph:
            step, to_pe, from_pe, s_ready, s1_out, s1_in = fresh(ph, "gat_step", "to_pe", "from_pe", "s_ready", "s1_out", "s1_in")
            with nc.Block() as block:
                @block.sync
                def _(sp):
                    sp.wait_ge(s_ready, 1)
                    sp.dma_start(s1_tab.rearrange("a (t p) -> (a t) p", p=P), s1t[0:NT, :]).then_inc(s1_out, 16)
                    sp.wait_ge(s1_out, 16)
                    sp.dma_start(s1bc, s1_tab.to_broadcast([P, NP])).then_inc(s1_in, 16)
                    sp.wait_ge(s1_in, 16)

                @block.tensor
                def _(pe):
                    pe.wait_ge(to_pe, 1)
                    nc.tensor.transpose(bank[0][0:NT, 0:P], s12[:, 0:NT], ident[:, :]).then_inc(from_pe, 1)

                @block.vector
                def _(dve):
                    link = Chain(dve, step)
                    for k in range(2):
                        link(nc.vector.tensor_tensor(hh3, skip3, a12[:, k * D:(k + 1) * D].unsqueeze(1).to_broadcast([P, NT, D]), ALU.mult))
                        link(nc.vector.tensor_reduce(s12[:, k * NT:(k + 1) * NT], hh3, AX_X, ALU.add))
                        if k == 0:
                            nc.vector.engine_nop().then_inc(to_pe, 1)
                    link(nc.vector.tensor_scalar(s2_steep, s12[:, NT:], -1.0, None, ALU.mult))
                    link(nc.vector.tensor_scalar(s2_flat, s12[:, NT:], -0.2, None, ALU.mult))
                    dve.wait_ge(from_pe, 1)
                    link(nc.vector.tensor_copy(s1t[0:NT, :], bank[0][0:NT, 0:P]))
                    nc.vector.engine_nop().then_inc(s_ready, 1)
        by_src(skip, True)

        def gat_nodes(link, on_act):
            ln_mean, ln_var, ln_inv, ln_tmp = (small[:, 100 + k * NT:100 + (k + 1) * NT] for k in range(4))
            bc = lambda c: c.unsqueeze(2).to_broadcast([P, NT, D])
            row = lambda r: r.unsqueeze(1).to_broadcast([P, NT, D])

            def norm(src, dst, scratch, sqrt):
                link(nc.vector.tensor_reduce(ln_mean, src, AX_X, ALU.add))
                link(nc.vector.tensor_scalar(ln_mean, ln_mean, 1.0 / D, None, ALU.mult))
                link(nc.vector.tensor_tensor(dst, src, bc(ln_mean), ALU.subtract))
                link(nc.vector.tensor_tensor(scratch, dst, dst, ALU.mult))
                link(nc.vector.tensor_reduce(ln_var, scratch, AX_X, ALU.add))
                link(nc.vector.tensor_scalar(ln_var, ln_var, 1.0 / D, LN_EPS, ALU.mult, ALU.add))
                sqrt(ln_var, ln_tmp)
                link(nc.vector.reciprocal(ln_inv, ln_tmp))
                link(nc.vector.tensor_tensor(dst, dst, bc(ln_inv), ALU.mult))

            norm(psum[:, 0:NP].rearrange("p (t d) -> p t d", d=D), skip3, hh3, on_act(ACT.Sqrt))
            link(nc.vector.tensor_tensor(skip3, skip3, row(lnwb[:, 0:D]), ALU.mult))
            link(nc.vector.tensor_tensor(skip3, skip3, row(lnwb[:, D:]), ALU.add))
            link(nc.vector.tensor_scalar(hh, skip[:, :], 0.0, None, ALU.min))
            on_act(ACT.Exp)(hh, g_flat)
            link(nc.vector.tensor_scalar(skip[:, :], skip[:, :], 0.0, -1.0, ALU.max, ALU.add))
            link(nc.vector.tensor_tensor(skip[:, :], skip[:, :], g_flat, ALU.add))
            link(nc.vector.tensor_tensor(hh3, skip3, x3, ALU.add))
            norm(hh3, x3, skip3, on_act(ACT.Sqrt))
        lv, lt = small[:, 100 + NT:100 + 2 * NT], small[:, 100 + 3 * NT:100 + 4 * NT]
        node_math(gat_nodes, [(ACT.Sqrt, lv, lt, {}), (ACT.Exp, hh, g_flat, {}), (ACT.Sqrt, lv, lt, {})])

        out_done = sem("out_done")
        with nc.Block() as block:
            @block.sync
            def _(sp):
                sp.dma_start(out[0:(NT - 1) * P, :].rearrange("(t p) d -> p t d", p=P), x3[:, 0:NT - 1, :]).then_inc(out_done, 16)
                sp.dma_start(out[(NT - 1) * P:N, :], x3[0:TAIL, NT - 1, :]).then_inc(out_done, 16)
                sp.wait_ge(out_done, 32)


def layout(i):
    import numpy as np

    c = np.ascontiguousarray
    a = {"x": c(i["x"]), "src": c(i["src"]), "dst": c(i["dst"]), "edge_attr": c(i["edge_attr_16"]), "edge_weight": c(np.asarray(i["edge_weight1"]).reshape(-1))}
    for n in "qkvs":
        for l in range(2):
            a[f"L0_{n}_w{l}"] = c(i[f"L0_gnn_{n}_w{l}"])
            a[f"L0_{n}_b{l}"] = c(np.asarray(i[f"L0_gnn_{n}_b{l}"]).reshape(1, -1))
    a["L1_WT"] = c(np.asarray(i["L1_gnn_W"]).T)
    a["L1_b"] = c(np.asarray(i["L1_gnn_b"]).reshape(1, -1))
    for n in ("W_enc", "W_ee", "W1", "W2", "b2"):
        a[f"L2_{n}"] = c(i[f"L2_gnn_{n}"])
    for n in ("b_enc", "b_ee", "eps"):
        a[f"L2_{n}"] = c(np.asarray(i[f"L2_gnn_{n}"]).reshape(1, -1))
    a["L2_bn"] = c(np.concatenate([np.asarray(i[f"L2_gnn_{n}"]).T for n in ("bn_gamma", "bn_beta", "bn_mean", "bn_var", "b1")], axis=1))
    a["L3_WT"] = c(np.asarray(i["L3_gnn_W"]).T)
    for n in ("b", "a", "ln_w", "ln_b"):
        a[f"L3_{n}"] = c(np.asarray(i[f"L3_gnn_{n}"]).reshape(1, -1))
    return a


def kernel(**inputs):
    import concourse.bacc as bacc
    from concourse.bass_utils import run_bass_kernel_spmd

    nc = bacc.Bacc("TRN2", target_bir_lowering=False, num_devices=1)
    arrays, aps = {}, {}
    for name, arr in layout(inputs).items():
        arrays[f"in_{name}"] = arr
        aps[name] = nc.dram_tensor(f"in_{name}", arr.shape, mybir.dt.from_np(arr.dtype), kind="ExternalInput").ap()
    out = nc.dram_tensor("out_x", (N, D), F32, kind="ExternalOutput").ap()
    build(nc, aps, out)
    r = run_bass_kernel_spmd(nc, [arrays], core_ids=[0])
    return r.results[0]["out_x"]
```

```python
from contextlib import ExitStack

import concourse.bass as bass
from concourse import mybir

F32 = mybir.dt.float32
I32 = mybir.dt.int32
ALU = mybir.AluOpType
ACT = mybir.ActivationFunctionType
AX_X = mybir.AxisListType.X

P = 128
N = 3125
E = 100000
D = 128
HEADS = 8
CH = D // HEADS
EA = 16
NT = -(-N // P)
NP = NT * P
TAIL = N - (NT - 1) * P
G = 8
NG = -(-E // (P * G))
J = NG * G
JTAIL = E - (P - 1) * J
K = 4
NV = 216
assert P * NV * K >= P * J + (K - 1) * (N + 1) and NV % 4 == 0
NS = NV * K
PHANTOM = NP
ZROW = N
REC = 20
R_W, R_SRC, R_DST, R_ONE = EA, EA + 1, EA + 2, EA + 3
ITEMS = NG + NT - 1
ROWS = P * NV
W = D + HEADS
BIG = 1e37
MASK = 1e30
LN_EPS = 1e-5
SCALE = CH ** -0.5
U = 5
assert NT % U == 0


class Chain:

    def __init__(self, eng, sem):
        self.eng, self.sem, self.n = eng, sem, 0

    def __call__(self, ins):
        self.n += 1
        ins.then_inc(self.sem, 1)
        self.eng.wait_ge(self.sem, self.n)


def later(eng, sem, value):
    if not isinstance(value, int) or value > 0:
        eng.wait_ge(sem, value)


def build(nc, a, out):
    ctx = ExitStack()
    with ctx:
        def sb(name, cols, dt=F32, parts=P):
            return ctx.enter_context(nc.sbuf_tensor(name, [parts, cols], dt))

        def sem(name):
            return ctx.enter_context(nc.semaphore(name))

        def dram(name, shape, dt=F32):
            return nc.dram_tensor(name, shape, dt, kind="Internal").ap()

        ident, shift_in, shift_back, upper, ones = (sb(n, P) for n in ("ident", "shift_in", "shift_back", "upper", "ones"))
        x = sb("x", NT * D)
        skip = sb("skip", NT * D)
        x3 = x[:, :].rearrange("p (t d) -> p t d", d=D)
        skip3 = skip[:, :].rearrange("p (t d) -> p t d", d=D)
        sums = sb("sums", (NV + 1) * W)
        sums3 = sums[:, :].rearrange("p (j f) -> p j f", f=W)
        ring = sb("ring", 4 * K * 2 * D)
        qring = sb("qring", 4 * D)
        prod = sb("prod", 2 * K * D)
        pv = sb("pv", 2 * K * D)
        rowmax = sb("rowmax", NV * HEADS)
        src_idx = sb("src_idx", NS + 16, I32)
        q_idx = sb("q_idx", NV + 4, I32)
        weight = sb("weight", NS)
        maskneg = sb("maskneg", NS)
        same, same_l, reset, rnext, fs_neg, ls_neg = (sb(n, NV) for n in ("same", "same_l", "reset", "rnext", "fs_neg", "ls_neg"))
        link_row, cont_row = sb("link_row", P), sb("cont_row", P)
        neg_rows = sb("neg_rows", 4 * P)
        last_idx = sb("last_idx", NT, I32)
        first_end = sb("first_end", 1, I32)
        wgt = sb("wgt", 512)
        bias = sb("bias", 512)
        idx_slot = sb("idx_slot", 2 * 2 * K, I32)
        qidx_slot = sb("qidx_slot", 2 * 2, I32)
        small = sb("small", 1200)

        psum = ctx.enter_context(nc.psum_tensor("psum", [P, 8 * 512], F32))
        bank = [psum[:, i * 512:(i + 1) * 512] for i in range(8)]


        def dma_sems(*names):
            count[0] += 1
            return [sem(f"{n}_{count[0]}") for n in names]

        count = [0]

        def fresh(ph, *names):
            count[0] += 1
            sems = [nc.alloc_semaphore(f"{n}_{count[0]}") for n in names]

            def retire():
                for s in sems:
                    nc.gpsimd.sem_clear(s)
                    nc.release_semaphore(s)
            ph.callback(retire)
            return sems

        recs = dram("recs", (P * NS, REC))
        count_tab = dram("count_tab", (NP, NP))
        q_tab = dram("q_tab", (NP, D))
        kv_tab = dram("kv_tab", (NP, 2 * D))
        h_tab = dram("h_tab", (NP, D))
        s1_tab = dram("s1_tab", (1, NP))
        sums_tab = dram("sums_tab", (ROWS + 1, W))
        sums_rows = sums_tab[0:ROWS, :].rearrange("(p j) f -> p (j f)", j=NV)

        def area(off, cols):
            return sums[:, off:off + cols]

        agg = area(0, NT * W).rearrange("p (t f) -> p t f", f=W)
        work = area(2 * NT * W, NT * D)
        work3 = work.rearrange("p (t d) -> p t d", d=D)
        proj3 = area(10000, NT * 384).rearrange("p (t d) -> p t d", d=384)
        sq = area(19600, NT * D)
        sq3 = sq.rearrange("p (t d) -> p t d", d=D)
        col25 = area(22800, 4 * NT)
        stage_in = ring[:, 0:U * D]
        stage_in2 = ring[:, U * D:2 * U * D]
        stage_T = ring[:, 2 * U * D:3 * U * D]
        stage_T2 = ring[:, 3 * U * D:4 * U * D]
        stage_y = ring[:, 4 * U * D:5 * U * D]

        def table(t, cols=None):
            return t.rearrange("(t p) c -> p t c", p=P)

        f = lambda k: area(REC * J + k * J, J)
        rec3 = area(0, REC * J).rearrange("p (j c) -> p j c", c=REC)
        dst_i, src_i = (f(k).bitcast(I32) for k in (0, 1))
        eidx, d1, start, seg, pad, cum = (f(k) for k in (2, 3, 4, 5, 6, 7))
        t0, t1, t2, t3 = (f(k) for k in (8, 9, 10, 11))
        PIECE = 200
        pieces = [(lo, min(lo + PIECE, J)) for lo in range(0, J, PIECE)]
        ea_stage = (skip[:, 0:PIECE * EA], ring[:, 0:PIECE * EA])
        recfill = ring[:, 0:108 * REC]
        assert 108 * 8 == NS
        zrow = small[:, 64:64 + W]
        rows129 = small[0:1, 256:256 + P + 1]
        colA = small[:, 400:430]
        pos1 = pad.bitcast(I32)
        with ExitStack() as ph:
            fills_ready, loads, fills_out, setup, pool_step = fresh(ph, "fills_ready", "loads0", "fills_out", "setup0", "pool_step0")
            with nc.Block() as block:
                @block.gpsimd
                def _(pool):
                    link = Chain(pool, pool_step)
                    for m, base, cm, step in ((ident, 0, 1, -1), (shift_in, -1, -1, 1), (shift_back, 1, -1, 1)):
                        link(nc.gpsimd.memset(m[:, :], 0.0))
                        link(nc.gpsimd.affine_select(out=m[:, :], in_=m[:, :], compare_op=ALU.not_equal, fill=1.0, base=base, pattern=[[step, P]], channel_multiplier=cm))
                    link(nc.gpsimd.memset(ones[:, :], 1.0))
                    link(nc.gpsimd.affine_select(out=upper[:, :], in_=ones[:, :], compare_op=ALU.is_gt, fill=0.0, base=0, pattern=[[1, P]], channel_multiplier=-1))
                    link(nc.gpsimd.iota(eidx, pattern=[[1, J]], base=0, channel_multiplier=J, allow_small_or_imprecise_dtypes=True))

                @block.vector
                def _(dve):
                    link = Chain(dve, setup)
                    nc.vector.memset(x[:, (NT - 1) * D:], 0.0).then_inc(fills_ready, 1)
                    nc.vector.memset(dst_i, PHANTOM).then_inc(fills_ready, 1)
                    nc.vector.memset(src_i, ZROW).then_inc(fills_ready, 1)
                    nc.vector.memset(area(0, REC * J), 0.0).then_inc(fills_ready, 1)
                    rf = recfill.rearrange("p (j c) -> p j c", c=REC)
                    link(nc.vector.memset(recfill, 0.0))
                    link(nc.vector.memset(rf[:, :, R_SRC], float(ZROW)))
                    nc.vector.memset(rf[:, :, R_DST], float(PHANTOM)).then_inc(fills_ready, 1)
                    nc.vector.memset(zrow, 0.0).then_inc(fills_ready, 1)
                    nc.vector.memset(src_idx[:, NS:], 0).then_inc(fills_ready, 1)
                    nc.vector.memset(q_idx[:, NV:], 0).then_inc(fills_ready, 1)

                @block.sync
                def _(sp):
                    sp.wait_ge(fills_ready, 8)
                    sp.dma_start(x3[:, 0:NT - 1, :], a["x"][0:(NT - 1) * P, :].rearrange("(t p) d -> p t d", p=P)).then_inc(loads, 16)
                    sp.dma_start(x3[0:TAIL, NT - 1, :], a["x"][(NT - 1) * P:N, :]).then_inc(loads, 16)
                    for name, tile in (("dst", dst_i), ("src", src_i)):
                        sp.dma_start(tile[0:P - 1, :], a[name][0:(P - 1) * J].rearrange("(p j) -> p j", j=J)).then_inc(loads, 16)
                        sp.dma_start(tile[P - 1:P, 0:JTAIL], a[name][(P - 1) * J:E].rearrange("(p j) -> p j", p=1)).then_inc(loads, 16)
                    r = recs.rearrange("(p i j) c -> i p (j c)", i=8, j=108)
                    for i in range(8):
                        sp.dma_start(r[i], recfill).then_inc(fills_out, 16)
                    sp.dma_start(sums_tab[ROWS:ROWS + 1, :], zrow[0:1, :]).then_inc(fills_out, 16)
                    sp.wait_ge(loads, 6 * 16)
                    sp.wait_ge(fills_out, 9 * 16)

        with ExitStack() as ph:
            rec_step, ea_in0, ea_in1, ea_used, w_in, to_pe, from_pe = fresh(ph, "rec_step", "ea_in0", "ea_in1", "ea_used", "w_in", "to_pe1", "from_pe1")
            ea_v = a["edge_attr"]
            ea_in = (ea_in0, ea_in1)
            wcol = t0
            with nc.Block() as block:
                @block.sync
                def _(sp):
                    sp.wait_ge(rec_step, 3)
                    sp.dma_start(wcol[0:P - 1, :], a["edge_weight"][0:(P - 1) * J].rearrange("(p j) -> p j", j=J)).then_inc(w_in, 16)
                    sp.dma_start(wcol[P - 1:P, 0:JTAIL], a["edge_weight"][(P - 1) * J:E].rearrange("(p j) -> p j", p=1)).then_inc(w_in, 16)
                    full = ea_v[0:(P - 1) * J, :].rearrange("(p j) c -> p (j c)", j=J)
                    tail = ea_v[(P - 1) * J:E, :].rearrange("(p j) c -> p (j c)", p=1)
                    for h, (lo, hi) in enumerate(pieces):
                        st = ea_stage[h % 2]
                        if h >= 2:
                            sp.wait_ge(ea_used, h - 1)
                        n = (min(hi, JTAIL) - lo) * EA
                        sp.dma_start(st[0:P - 1, 0:(hi - lo) * EA], full[:, lo * EA:hi * EA]).then_inc(ea_in[h % 2], 16)
                        if n > 0:
                            sp.dma_start(st[P - 1:P, 0:n], tail[:, lo * EA:lo * EA + n]).then_inc(ea_in[h % 2], 16)

                @block.scalar
                def _(act):
                    due = [0, 0]
                    for h, (lo, hi) in enumerate(pieces):
                        due[h % 2] += 32 if lo < JTAIL else 16
                        act.wait_ge(ea_in[h % 2], due[h % 2])
                        nc.scalar.copy(rec3[:, lo:hi, 0:EA],
                                       ea_stage[h % 2][:, 0:(hi - lo) * EA].rearrange("p (j c) -> p j c", c=EA)).then_inc(ea_used, 1)

                @block.tensor
                def _(pe):
                    pe.wait_ge(to_pe, 1)
                    nc.tensor.matmul(bank[0][:, 0:1], shift_in[:, :], d1[:, J - 1:J], start=True, stop=True).then_inc(from_pe, 1)
                    pe.wait_ge(to_pe, 2)
                    nc.tensor.matmul(bank[1][0:1, 0:P], seg[:, J - 1:J], ident[:, :], start=True, stop=True).then_inc(from_pe, 1)
                    pe.wait_ge(to_pe, 3)
                    nc.tensor.matmul(bank[2][:, 0:1], rows129[:, 0:P], ones[0:1, 0:1], start=True, stop=True).then_inc(from_pe, 1)
                    pe.wait_ge(to_pe, 4)
                    nc.tensor.matmul(bank[3][:, 0:1], shift_in[:, :], seg[:, J - 1:J], start=True, stop=True).then_inc(from_pe, 1)
                    pe.wait_ge(to_pe, 5)
                    nc.tensor.matmul(bank[4][:, 0:1], upper[:, :], cum[:, J - 1:J], start=True, stop=True).then_inc(from_pe, 1)

                @block.vector
                def _(dve):
                    link = Chain(dve, rec_step)
                    link(nc.vector.memset(ea_stage[0], 0.0))
                    link(nc.vector.memset(ea_stage[1], 0.0))
                    link(nc.vector.memset(wcol, 0.0))
                    link(nc.vector.tensor_copy(rec3[:, :, R_DST], dst_i))
                    link(nc.vector.tensor_copy(rec3[:, :, R_SRC], src_i))
                    link(nc.vector.memset(rec3[:, :, R_ONE], 1.0))
                    link(nc.vector.tensor_scalar(d1, rec3[:, :, R_DST], 1.0, None, ALU.add))
                    link(nc.vector.memset(rows129, 0.0))
                    nc.vector.engine_nop().then_inc(to_pe, 1)
                    link(nc.vector.tensor_tensor(start[:, 1:], d1[:, 1:], d1[:, 0:J - 1], ALU.not_equal))
                    dve.wait_ge(from_pe, 1)
                    link(nc.vector.tensor_tensor(start[:, 0:1], d1[:, 0:1], bank[0][:, 0:1], ALU.not_equal))
                    link(nc.vector.tensor_tensor(t1, start, eidx, ALU.mult))
                    link(nc.vector.tensor_tensor_scan(seg, t1, t1, 0.0, ALU.max, ALU.max))
                    nc.vector.engine_nop().then_inc(to_pe, 1)
                    dve.wait_ge(from_pe, 2)
                    link(nc.vector.tensor_copy(t2[0:1, 0:P], bank[1][0:1, 0:P]))
                    link(nc.vector.tensor_tensor_scan(rows129[:, 1:P + 1], t2[0:1, 0:P], t2[0:1, 0:P], 0.0, ALU.max, ALU.max))
                    nc.vector.engine_nop().then_inc(to_pe, 1)
                    dve.wait_ge(from_pe, 3)
                    link(nc.vector.tensor_scalar(seg, seg, bank[2][:, 0:1], None, ALU.max))
                    nc.vector.engine_nop().then_inc(to_pe, 1)
                    link(nc.vector.tensor_tensor(t1[:, 1:], seg[:, 0:J - 1], eidx[:, 1:], ALU.subtract))
                    dve.wait_ge(from_pe, 4)
                    link(nc.vector.tensor_tensor(t1[:, 0:1], bank[3][:, 0:1], eidx[:, 0:1], ALU.subtract))
                    link(nc.vector.tensor_copy(t2.bitcast(I32), t1))
                    link(nc.vector.tensor_scalar(t3.bitcast(I32), t2.bitcast(I32), K - 1, None, ALU.bitwise_and))
                    link(nc.vector.tensor_copy(t2, t3.bitcast(I32)))
                    link(nc.vector.tensor_tensor(pad, start, t2, ALU.mult))
                    link(nc.vector.tensor_tensor_scan(cum, pad, pad, 0.0, ALU.add, ALU.max))
                    nc.vector.engine_nop().then_inc(to_pe, 1)
                    dve.wait_ge(from_pe, 5)
                    link(nc.vector.tensor_copy(colA[:, 0:1], bank[4][:, 0:1]))
                    link(nc.vector.scalar_tensor_tensor(pos1, cum, colA[:, 0:1], eidx, ALU.add, ALU.add))
                    dve.wait_ge(w_in, 32)
                    link(nc.vector.tensor_copy(rec3[:, :, R_W], wcol))

        CHUNK = J // 112
        assert CHUNK * 112 == J
        NC = -(-N // 8) * 8
        QS = NP // 2
        BF, F16 = mybir.dt.bfloat16, mybir.dt.float16
        stage1 = ring[:, 0:2 * CHUNK * REC]
        pstage1 = ring[:, 1000:1000 + 2 * CHUNK].bitcast(I32)
        o = REC * J
        src_lo, src_hi, dst_tm = (area(o + k * 7 * P, 7 * P) for k in range(3))
        dloc = area(o + 2720, 2 * G)
        oh_dst = area(o + 2752, G * P).bitcast(BF)
        nb, ntab = area(o + 3776, ITEMS), area(o + 3900, 3 * ITEMS).bitcast(I32)
        gcol, gend, cmp_i, iota_i = area(o + 4270, 2), area(o + 4272, 2), area(o + 4280, ITEMS), area(o + 4410, ITEMS)
        assert 4410 + ITEMS <= 6 * J and ITEMS <= 124
        snap = area(o + 7 * J, NP)
        oh_src = area(o + 7 * J + NP, NP).bitcast(BF)
        oh_more = skip[:, :].bitcast(BF)
        PIECES = 4

        def oh_slot(k):
            return (oh_src if k % 4 < 2 else oh_more)[:, k % 2 * NP:(k % 2 + 1) * NP]
        iota16 = area(o + 7 * J + 2 * NP, QS // 2).bitcast(F16)
        raw = [skip[:, k * 7 * P:(k + 1) * 7 * P] for k in range(2)]
        rawf = [pv[:, 0:7 * P], prod[:, 0:7 * P]]
        assert o + 7 * J + 2 * NP + QS // 2 <= (NV + 1) * W
        TF = E // P
        with ExitStack() as ph:
            d10, d11 = dma_sems("rec_out0", "rec_out1")
            ready1, pstep, loads_s, iotas, to_pe, from_pe, ohd, ohs, mm_done, piece_done, snapped, stored, cleared_s = fresh(
                ph, "rec_staged", "pair_step", "edges_in", "iotas", "to_pe", "from_pe", "oh_dst", "oh_src", "mm_done", "piece_done", "snapped", "stored", "cleared")
            r1 = area(0, REC * J)
            done = (d10, d11)
            with nc.Block() as block:
                @block.gpsimd
                def _(pool):
                    nc.gpsimd.iota(iota16, pattern=[[1, QS]], base=0, channel_multiplier=0, allow_small_or_imprecise_dtypes=True).then_inc(iotas, 1)
                    nc.gpsimd.iota(iota_i, pattern=[[1, ITEMS]], base=0, channel_multiplier=0, allow_small_or_imprecise_dtypes=True).then_inc(iotas, 1)
                    nc.gpsimd.iota(gcol[:, 1:2], pattern=[[0, 1]], base=0, channel_multiplier=1, allow_small_or_imprecise_dtypes=True).then_inc(iotas, 1)
                    with nc.gpsimd.Fori(0, 56) as i:
                        for u in range(2):
                            pool.wait_ge(ready1, 4 * i + 2 * u + 2)
                            nc.gpsimd.nop(nofuse=True)
                            for c in range(CHUNK):
                                k = u * CHUNK + c
                                nc.gpsimd.indirect_dma_start(
                                    out=recs, out_offset=bass.IndirectOffsetOnAxis(ap=pstage1[:, k:k + 1], axis=0),
                                    in_=stage1[:, k * REC:(k + 1) * REC], in_offset=None).then_inc(done[u], 16)
                    for d in done:
                        pool.wait_ge(d, 16 * CHUNK * 56)

                @block.sync
                def _(sp):
                    sp.wait_ge(cleared_s, 3)
                    for k, n in enumerate(("dst", "src")):
                        for b in range(7):
                            rows = min(P, TF - b * P)
                            sp.dma_start(raw[k].bitcast(I32)[0:rows, b * P:(b + 1) * P],
                                         a[n][b * P * P:(b * P + rows) * P].rearrange("(t e) -> t e", e=P)).then_inc(loads_s, 16)
                        sp.dma_start(raw[k].bitcast(I32)[TF - 6 * P:TF - 6 * P + 1, 6 * P:6 * P + E - TF * P],
                                     a[n][TF * P:E].rearrange("(t e) -> t e", t=1)).then_inc(loads_s, 16)
                    sp.dma_start(gcol.bitcast(I32)[0:NG - 1, 0:1], a["dst"][0:(NG - 1) * G * P].rearrange("(g e) -> g e", e=G * P)[:, G * P - 1:], allow_slow_non_contiguous=True).then_inc(loads_s, 16)
                    with nc.sync.Fori(0, ITEMS // 2) as i:
                        for u in range(2):
                            sp.wait_ge(snapped, PIECES * (2 * i + u + 2))
                            nc.sync.nop(nofuse=True)
                            n = nc.sync.value_load(ntab[0:1, bass.ds(2 * i + u, 1)], min_val=0, max_val=NT - 1)
                            is_last = nc.sync.value_load(ntab[0:1, bass.ds(2 * ITEMS + 2 * i + u, 1)], min_val=0, max_val=1)
                            with nc.sync.If(is_last > 0):
                                sp.dma_start(count_tab[bass.ds(n * P, P), :], snap).then_inc(stored, 16)
                            with nc.sync.Else():
                                nc.sync.nop(nofuse=True).then_inc(stored, 16)
                    sp.wait_ge(stored, 16 * ITEMS + 1)

                @block.tensor
                def _(pe):
                    for k in range(2):
                        pe.wait_ge(to_pe, k + 1)
                        for b in range(7):
                            ins_ = nc.tensor.transpose(bank[2 * k + b // 4][:, (b % 4) * P:(b % 4 + 1) * P], rawf[k][:, b * P:(b + 1) * P], ident[:, :])
                        ins_.then_inc(from_pe, 1)
                    pe.wait_ge(to_pe, 3)
                    nc.tensor.matmul(bank[4][:, 0:ITEMS], ones[:, :], cmp_i, start=True, stop=True).then_inc(from_pe, 1)
                    pe.wait_ge(to_pe, 4)
                    for b in range(7):
                        w = min(512, NP - b * 512)
                        nc.tensor.matmul(bank[b][:, 0:w], oh_dst[:, 0:P], oh_src[:, 0:w], start=True, stop=True)
                    nc.tensor.matmul(bank[7][:, 0:1], ones[:, :], ones[:, 0:1], start=True, stop=True).then_inc(mm_done, 1)
                    nc.tensor.matmul(bank[7][:, 0:1], ones[:, :], ones[:, 0:1], start=True, stop=True).then_inc(piece_done, 1)
                    with nc.tensor.Fori(0, ITEMS // 2) as i:
                        for u in range(2):
                            for q in range(G // 2):
                                pe.wait_ge(ohs, G // 2 * (2 * i + u) + q + 1)
                                for b in range(7):
                                    w = min(512, NC - b * 512)
                                    if q == 0 and b % 2 == 0:
                                        pe.wait_ge(snapped, PIECES * (2 * i + u) + b // 2 + 1)
                                    for k in (2 * q, 2 * q + 1):
                                        ins_ = nc.tensor.matmul(bank[b][:, 0:w], oh_dst[:, (u * G + k) * P:(u * G + k + 1) * P],
                                                                oh_slot(k)[:, b * 512:b * 512 + w], start=False, stop=True, skip_group_check=True)
                                    if q == G // 2 - 1 and (b % 2 == 1 or b == 6):
                                        ins_.then_inc(piece_done, 1)
                                if q < G // 2 - 1:
                                    ins_.then_inc(mm_done, 1)

                @block.scalar
                def _(act):
                    nc.scalar.copy(snap[:, 0:1], ones[:, 0:1]).then_inc(snapped, PIECES)
                    nc.scalar.copy(snap[:, 1:2], ones[:, 0:1]).then_inc(stored, 1)

                    def snapshot(i, u):
                        act.wait_ge(stored, 16 * (2 * i + u) + 1)
                        for k in range(PIECES):
                            act.wait_ge(piece_done, PIECES * (2 * i + u) + k + 2)
                            lo, hi = 1024 * k, min(1024 * (k + 1), NP)
                            nc.scalar.copy(snap[:, lo:hi], psum[:, lo:hi]).then_inc(snapped, 1)
                    def staged_records(i, u):
                        if not isinstance(i, int):
                            act.wait_ge(done[u], 16 * CHUNK * i)
                        r_at, p_at = (2 * i + u) * CHUNK * REC, (2 * i + u) * CHUNK
                        nc.scalar.copy(stage1[:, u * CHUNK * REC:(u + 1) * CHUNK * REC], r1[:, bass.ds(r_at, CHUNK * REC)]).then_inc(ready1, 1)
                        nc.scalar.copy(pstage1[:, u * CHUNK:(u + 1) * CHUNK], pos1[:, bass.ds(p_at, CHUNK)]).then_inc(ready1, 1)
                    for u in range(2):
                        staged_records(0, u)
                        snapshot(0, u)
                    with nc.scalar.Fori(1, 56) as i:
                        for u in range(2):
                            staged_records(i, u)
                            snapshot(i, u)
                    with nc.scalar.Fori(56, ITEMS // 2) as i:
                        for u in range(2):
                            snapshot(i, u)

                @block.vector
                def _(dve):
                    link = Chain(dve, pstep)
                    nc.vector.memset(raw[0].bitcast(I32), PHANTOM).then_inc(cleared_s, 1)
                    nc.vector.memset(raw[1].bitcast(I32), 0).then_inc(cleared_s, 1)
                    nc.vector.memset(gcol.bitcast(I32)[:, 0:1], PHANTOM).then_inc(cleared_s, 1)
                    dve.wait_ge(loads_s, 16 * 17)
                    dve.wait_ge(iotas, 3)
                    link(nc.vector.tensor_copy(rawf[0], raw[0].bitcast(I32)))
                    nc.vector.engine_nop().then_inc(to_pe, 1)
                    link(nc.vector.tensor_copy(rawf[1], raw[1].bitcast(I32)))
                    nc.vector.engine_nop().then_inc(to_pe, 1)
                    link(nc.vector.tensor_scalar(gend.bitcast(I32)[:, 0:1], gcol.bitcast(I32)[:, 0:1], 7, None, ALU.arith_shift_right))
                    link(nc.vector.tensor_copy(gend[:, 1:2], gend.bitcast(I32)[:, 0:1]))
                    link(nc.vector.scalar_tensor_tensor(gend[:, 0:1], gend[:, 1:2], float(NT - 1), gcol[:, 1:2], ALU.min, ALU.add))
                    link(nc.vector.tensor_scalar(cmp_i, iota_i, gend[:, 0:1], None, ALU.is_gt))
                    link(nc.vector.memset(oh_dst, 0.0))
                    link(nc.vector.memset(oh_src, 0.0))
                    nc.vector.engine_nop().then_inc(to_pe, 1)
                    dve.wait_ge(from_pe, 2)
                    link(nc.vector.tensor_copy(dst_tm, psum[:, 0:7 * P]))
                    link(nc.vector.tensor_copy(src_lo, psum[:, 1024:1024 + 7 * P]))
                    link(nc.vector.tensor_scalar(src_hi, src_lo, -float(QS), None, ALU.add))
                    dve.wait_ge(from_pe, 3)
                    link(nc.vector.tensor_copy(nb, bank[4][:, 0:ITEMS]))
                    link(nc.vector.tensor_scalar(ntab[:, ITEMS:2 * ITEMS], nb, float(G), None, ALU.mult))
                    link(nc.vector.tensor_tensor(nb, iota_i, nb, ALU.subtract))
                    link(nc.vector.tensor_copy(ntab[:, 0:ITEMS], nb))
                    link(nc.vector.tensor_tensor(cmp_i[:, 0:ITEMS - 1], nb[:, 1:], nb[:, 0:ITEMS - 1], ALU.subtract))
                    link(nc.vector.memset(cmp_i[:, ITEMS - 1:], 1.0))
                    link(nc.vector.tensor_copy(ntab[:, 2 * ITEMS:], cmp_i))
                    link(nc.vector.tensor_scalar(nb, nb, float(P), None, ALU.mult))
                    nc.vector.engine_nop().then_inc(to_pe, 1)
                    with nc.vector.Fori(0, ITEMS // 2) as i:
                        for u in range(2):
                            t0 = nc.vector.value_load(ntab[0:1, bass.ds(ITEMS + 2 * i + u, 1)], min_val=0, max_val=(NG - 1) * G)
                            dl = dloc[:, u * G:(u + 1) * G]
                            nc.vector.tensor_scalar(dl, dst_tm[:, bass.ds(t0, G)], nb[:, bass.ds(2 * i + u, 1)], None, ALU.subtract).then_inc(ohd, 1)
                            dve.wait_ge(ohd, 2 * i + u + 1)
                            for k in range(G):
                                if k % 2 == 0:
                                    if k == 2:
                                        dve.wait_ge(piece_done, PIECES * (2 * i + u) + 1)
                                    else:
                                        dve.wait_ge(mm_done, (G // 2 - 1) * (2 * i + u) + max(k // 2, 1))
                                oh = oh_slot(k)
                                nc.vector.tensor_scalar(oh_dst[:, (u * G + k) * P:(u * G + k + 1) * P], iota16[:, 0:P], dl[:, k:k + 1], None, ALU.is_equal)
                                nc.vector.tensor_scalar(oh[:, 0:QS], iota16, src_lo[:, bass.ds(t0 + k, 1)], None, ALU.is_equal)
                                ins_ = nc.vector.tensor_scalar(oh[:, QS:NC], iota16[:, 0:NC - QS], src_hi[:, bass.ds(t0 + k, 1)], None, ALU.is_equal)
                                if k % 2 == 1:
                                    ins_.then_inc(ohs, 1)

        back = area(0, NS * REC)
        back4 = back.rearrange("p (j s c) -> p j s c", s=K, c=REC)
        g = lambda k: area(NS * REC + k * NV, NV)
        vn1, snext, fs, ls, node, place = (g(k) for k in range(6))
        srows = area(NS * REC + 11 * NV, NS)
        iota_n = area(NS * REC + 12 * NV + NS, P)
        rows_of, in_all, before = (small[:, 740 + k * NT:740 + (k + 1) * NT] for k in range(3))
        Q = NV // 4
        in_window = ring[:, 0:NV * NT // 2].bitcast(BF)
        places = [back[:, k * NV * P // 8:(k + 1) * NV * P // 8].bitcast(BF) for k in range(2)]

        def at_place(k):
            return places[k % 2]
        with ExitStack() as ph:
            back_in, row_step, to_pe, from_pe, iotas, one_hots, counted = fresh(ph, "back_in", "row_step", "to_pe3", "from_pe3", "iotas3", "one_hots", "counted")
            row0 = small[:, 702:703]
            colB = small[:, 710:730]
            with nc.Block() as block:
                @block.sync
                def _(sp):
                    sp.dma_start(back, recs.rearrange("(p j) c -> p (j c)", j=NS)).then_inc(back_in, 16)
                    sp.wait_ge(back_in, 16)

                @block.gpsimd
                def _(pool):
                    nc.gpsimd.iota(row0, pattern=[[0, 1]], base=0, channel_multiplier=NV, allow_small_or_imprecise_dtypes=True).then_inc(iotas, 1)
                    nc.gpsimd.iota(iota_n, pattern=[[1, P]], base=0, channel_multiplier=0, allow_small_or_imprecise_dtypes=True).then_inc(iotas, 1)

                @block.tensor
                def _(pe):
                    pe.wait_ge(to_pe, 1)
                    nc.tensor.matmul(bank[0][:, 0:1], shift_in[:, :], vn1[:, NV - 1:NV], start=True, stop=True).then_inc(from_pe, 1)
                    pe.wait_ge(to_pe, 2)
                    nc.tensor.matmul(bank[1][:, 0:1], shift_back[:, :], same[:, 0:1], start=True, stop=True).then_inc(from_pe, 1)
                    pe.wait_ge(to_pe, 3)
                    nc.tensor.matmul(bank[2][:, 0:1], shift_in[:, :], fs[:, NV - 1:NV], start=True, stop=True).then_inc(from_pe, 1)
                    nc.tensor.matmul(bank[3][:, 0:1], shift_back[:, :], ls[:, 0:1], start=True, stop=True).then_inc(from_pe, 1)
                    for k in range(4):
                        pe.wait_ge(to_pe, 4 + k)
                        nc.tensor.matmul(bank[4 + k][:, 0:P], srows[:, k * P:(k + 1) * P], ident[:, :], start=True, stop=True).then_inc(from_pe, 1)
                    for k in range(4):
                        pe.wait_ge(one_hots, k + 1)
                        for j in range(Q):
                            ins_ = nc.tensor.matmul(bank[0][:, 0:NT], at_place(k)[:, j * P:(j + 1) * P], in_window[:, (k * Q + j) * NT:(k * Q + j + 1) * NT],
                                                    start=k == 0 and j == 0, stop=k == 3 and j == Q - 1)
                        ins_.then_inc(counted, 1)
                    pe.wait_ge(to_pe, 8)
                    nc.tensor.matmul(bank[1][:, 0:NT], upper[:, :], rows_of, start=True, stop=True)
                    nc.tensor.matmul(bank[2][:, 0:NT], ones[:, :], rows_of, start=True, stop=True).then_inc(from_pe, 1)

                @block.vector
                def _(dve):
                    link = Chain(dve, row_step)
                    dve.wait_ge(iotas, 2)
                    dve.wait_ge(back_in, 16)
                    link(nc.vector.tensor_copy(src_idx[:, 0:NS], back4[:, :, :, R_SRC].rearrange("p j s -> p (j s)")))
                    link(nc.vector.tensor_copy(weight[:, :], back4[:, :, :, R_W].rearrange("p j s -> p (j s)")))
                    link(nc.vector.tensor_scalar(maskneg[:, :], back4[:, :, :, R_SRC].rearrange("p j s -> p (j s)"), float(ZROW), -MASK, ALU.is_ge, ALU.mult))
                    link(nc.vector.tensor_scalar(vn1, back4[:, :, 0, R_DST], 1.0, None, ALU.add))
                    nc.vector.engine_nop().then_inc(to_pe, 1)
                    link(nc.vector.tensor_scalar(q_idx[:, 0:NV], back4[:, :, 0, R_DST], float(NP - 1), None, ALU.min))
                    link(nc.vector.tensor_tensor(same[:, 1:], vn1[:, 1:], vn1[:, 0:NV - 1], ALU.is_equal))
                    dve.wait_ge(from_pe, 1)
                    link(nc.vector.tensor_tensor(same[:, 0:1], vn1[:, 0:1], bank[0][:, 0:1], ALU.is_equal))
                    nc.vector.engine_nop().then_inc(to_pe, 1)
                    link(nc.vector.tensor_copy(same_l[:, 1:], same[:, 1:]))
                    link(nc.vector.memset(same_l[:, 0:1], 0.0))
                    link(nc.vector.tensor_scalar(reset[:, :], same_l[:, :], -1.0, BIG, ALU.add, ALU.mult))
                    link(nc.vector.tensor_copy(snext[:, 0:NV - 1], same[:, 1:]))
                    dve.wait_ge(from_pe, 2)
                    link(nc.vector.tensor_copy(snext[:, NV - 1:NV], bank[1][:, 0:1]))
                    link(nc.vector.tensor_scalar(rnext[:, :], snext, -1.0, BIG, ALU.add, ALU.mult))
                    link(nc.vector.memset(rnext[:, NV - 1:NV], -BIG))
                    link(nc.vector.tensor_tensor_scan(fs, same[:, :], same[:, :], 1.0, ALU.mult, ALU.min))
                    link(nc.vector.tensor_tensor_scan(ls[:, ::-1], snext[:, ::-1], snext[:, ::-1], 1.0, ALU.mult, ALU.min))
                    nc.vector.engine_nop().then_inc(to_pe, 1)
                    link(nc.vector.tensor_scalar(fs_neg[:, :], fs, -1.0, BIG, ALU.add, ALU.mult))
                    link(nc.vector.tensor_scalar(ls_neg[:, :], ls, -1.0, BIG, ALU.add, ALU.mult))
                    dve.wait_ge(from_pe, 4)
                    link(nc.vector.tensor_copy(colB[:, 0:1], same[:, 0:1]))
                    link(nc.vector.tensor_tensor(colB[:, 1:2], same[:, 0:1], bank[2][:, 0:1], ALU.mult))
                    link(nc.vector.tensor_copy(colB[:, 2:3], snext[:, NV - 1:NV]))
                    link(nc.vector.tensor_tensor(colB[:, 3:4], snext[:, NV - 1:NV], bank[3][:, 0:1], ALU.mult))
                    for k in range(4):
                        link(nc.vector.tensor_scalar(srows[:, k * P:(k + 1) * P], ones[:, :], colB[:, k:k + 1], None, ALU.mult))
                        nc.vector.engine_nop().then_inc(to_pe, 1)
                    dve.wait_ge(from_pe, 8)
                    link(nc.vector.tensor_copy(link_row[:, :], bank[4][:, 0:P]))
                    link(nc.vector.tensor_copy(cont_row[:, :], bank[5][:, 0:P]))
                    for k in range(4):
                        link(nc.vector.tensor_scalar(neg_rows[:, k * P:(k + 1) * P], bank[4 + k][:, 0:P], -1.0, BIG, ALU.add, ALU.mult))
                    link(nc.vector.tensor_tensor_scan(fs, snext, snext, 1.0, ALU.mult, ALU.min))
                    link(nc.vector.tensor_reduce(colB[:, 4:5], fs, AX_X, ALU.add))
                    link(nc.vector.scalar_tensor_tensor(first_end[:, :], colB[:, 4:5], float(NV - 1), row0, ALU.min, ALU.add))
                    link(nc.vector.tensor_scalar(node.bitcast(I32), vn1, -1.0, None, ALU.add))
                    link(nc.vector.tensor_scalar(place.bitcast(I32), node.bitcast(I32), P - 1, None, ALU.bitwise_and))
                    link(nc.vector.tensor_copy(place, place.bitcast(I32)))
                    link(nc.vector.tensor_scalar(node.bitcast(I32), node.bitcast(I32), 7, None, ALU.arith_shift_right))
                    link(nc.vector.tensor_copy(node, node.bitcast(I32)))
                    link(nc.vector.tensor_tensor(in_window.rearrange("p (j n) -> p j n", n=NT), node.unsqueeze(2).to_broadcast([P, NV, NT]),
                                                 iota_n[:, 0:NT].unsqueeze(1).to_broadcast([P, NV, NT]), ALU.is_equal))
                    for k in range(4):
                        if k >= 2:
                            dve.wait_ge(counted, k - 1)
                        nc.vector.tensor_tensor(at_place(k).rearrange("p (j n) -> p j n", n=P), place[:, k * Q:(k + 1) * Q].unsqueeze(2).to_broadcast([P, Q, P]),
                                                iota_n.unsqueeze(1).to_broadcast([P, Q, P]), ALU.is_equal).then_inc(one_hots, 1)
                    dve.wait_ge(counted, 4)
                    link(nc.vector.tensor_copy(rows_of, bank[0][:, 0:NT]))
                    nc.vector.engine_nop().then_inc(to_pe, 1)
                    dve.wait_ge(from_pe, 9)
                    link(nc.vector.tensor_copy(in_all, bank[2][:, 0:NT]))
                    link(nc.vector.tensor_tensor_scan(before, in_all, in_all, 0.0, ALU.add, ALU.max))
                    link(nc.vector.tensor_tensor(before, before, in_all, ALU.subtract))
                    link(nc.vector.tensor_tensor(before, before, bank[1][:, 0:NT], ALU.add))
                    link(nc.vector.scalar_tensor_tensor(before, before, -1.0 - ROWS, rows_of, ALU.add, ALU.add))
                    link(nc.vector.scalar_tensor_tensor(before, rows_of, 0.0, before, ALU.is_gt, ALU.mult))
                    link(nc.vector.tensor_scalar(last_idx[:, :], before, float(ROWS), None, ALU.add))

        STEPS = NV // 4

        def index_copies(act, i, half, with_q):
            nc.scalar.copy(idx_slot[:, half * 2 * K:(half + 1) * 2 * K], src_idx[:, bass.ds(4 * K * i + 2 * K * half, 2 * K)] if not isinstance(i, int)
                           else src_idx[:, 4 * K * i + 2 * K * half:4 * K * i + 2 * K * half + 2 * K]).then_inc(with_q[0], 1)
            if len(with_q) > 1:
                nc.scalar.copy(qidx_slot[:, half * 2:(half + 1) * 2], q_idx[:, bass.ds(4 * i + 2 * half, 2)] if not isinstance(i, int)
                               else q_idx[:, 4 * i + 2 * half:4 * i + 2 * half + 2]).then_inc(with_q[0], 1)

        def gather_step(tab, width, u, slot_in, q):
            for s in range(K):
                nc.gpsimd.indirect_dma_start(
                    out=ring[:, (u * K + s) * width:(u * K + s + 1) * width], out_offset=None, in_=tab,
                    in_offset=bass.IndirectOffsetOnAxis(ap=idx_slot[:, u * K + s:u * K + s + 1], axis=0)).then_inc(slot_in[u], 16)
            if q:
                nc.gpsimd.indirect_dma_start(
                    out=qring[:, u * D:(u + 1) * D], out_offset=None, in_=q_tab,
                    in_offset=bass.IndirectOffsetOnAxis(ap=qidx_slot[:, u:u + 1], axis=0)).then_inc(slot_in[u], 16)

        def conv_edges():
            with ExitStack() as ph:
                s0, s1, s2, s3 = dma_sems("slot0", "slot1", "slot2", "slot3")
                idx_ready, dve_step, exp_done, cleared = fresh(ph, "idx_ready", "dve_step", "exp_done", "cleared")
                slot_in = (s0, s1, s2, s3)
                PER = 16 * (K + 1)
                OPS = 8
                kv = ring[:, :].rearrange("p (u s c) -> p u s c", u=4, s=K)
                al = small[:, 0:2 * 3 * K * HEADS].rearrange("p (r k c) -> p r k c", r=2, k=3)
                ex = small[:, 256:256 + 2 * K * HEADS].rearrange("p (r c) -> p r c", r=2)
                with nc.Block() as block:
                    @block.gpsimd
                    def _(pool):
                        pool.wait_ge(idx_ready, 4)
                        for u in range(4):
                            if u == 3:
                                pool.wait_ge(dve_step, 2)
                            gather_step(kv_tab, 2 * D, u, slot_in, True)
                        with nc.gpsimd.Fori(1, STEPS) as i:
                            for u in range(4):
                                if u % 2 == 0:
                                    pool.wait_ge(idx_ready, 4 * i + 2 * (u // 2) + 2)
                                    nc.gpsimd.nop(nofuse=True)
                                pool.wait_ge(dve_step, OPS * (4 * i + u - 3) + 2)
                                nc.gpsimd.nop(nofuse=True)
                                gather_step(kv_tab, 2 * D, u, slot_in, True)

                    @block.scalar
                    def _(act):
                        for half in range(2):
                            index_copies(act, 0, half, (idx_ready, True))
                        with nc.scalar.Fori(0, STEPS) as i:
                            for u in range(4):
                                act.wait_ge(dve_step, OPS * (4 * i + u + 1))
                                nc.scalar.activation(ex[:, u % 2, :], al[:, u % 2, 2, :], ACT.Exp).then_inc(exp_done, 1)
                                if u % 2 == 1:
                                    act.wait_ge(slot_in[u - 1], PER * (i + 1))
                                    act.wait_ge(slot_in[u], PER * (i + 1))
                                    index_copies(act, i + 1, u // 2, (idx_ready, True))

                    @block.vector
                    def _(dve):
                        nc.vector.memset(kv[:, 3, :, :], 0.0).then_inc(cleared, 1)
                        nc.vector.memset(ex[:, 1, :], 0.0).then_inc(cleared, 1)
                        dve.wait_ge(cleared, 2)

                        def weigh(u, at, k):
                            w = (u - 1) % 4
                            nc.vector.tensor_tensor(
                                pv[:, (u - 1) % 2 * K * D:((u - 1) % 2 + 1) * K * D].rearrange("p (s h c) -> p s h c", s=K, h=HEADS),
                                kv[:, w, :, D:].rearrange("p s (h c) -> p s h c", h=HEADS),
                                ex[:, (u - 1) % 2, :].rearrange("p (s h) -> p s h", s=K).unsqueeze(3).to_broadcast([P, K, HEADS, CH]),
                                ALU.mult).then_inc(dve_step, 1)

                        def add_up(u, at, first):
                            dve.wait_ge(dve_step, first)
                            nc.vector.tensor_reduce(sums[:, bass.ds(at * W, D)],
                                                    pv[:, (u - 1) % 2 * K * D:((u - 1) % 2 + 1) * K * D].rearrange("p (s f) -> p f s", s=K), AX_X, ALU.add).then_inc(dve_step, 1)
                            nc.vector.tensor_reduce(sums[:, bass.ds(at * W + D, HEADS)],
                                                    ex[:, (u - 1) % 2, :].rearrange("p (s h) -> p h s", s=K), AX_X, ALU.add).then_inc(dve_step, 1)

                        def step_of_rows(i):
                            for u in range(4):
                                t = 4 * i + u
                                r = u % 2
                                done = OPS * t
                                pr = prod[:, r * K * D:(r + 1) * K * D]
                                dve.wait_ge(slot_in[u], PER * (i + 1))
                                nc.vector.tensor_tensor(pr.rearrange("p (s c) -> p s c", s=K), kv[:, u, :, 0:D],
                                                        qring[:, u * D:(u + 1) * D].unsqueeze(1).to_broadcast([P, K, D]), ALU.mult).then_inc(dve_step, 1)
                                later(dve, exp_done, t)
                                weigh(u, t, 2)
                                dve.wait_ge(dve_step, done + 1)
                                nc.vector.tensor_reduce(al[:, r, 0, :], pr.rearrange("p (a c) -> p a c", c=CH), AX_X, ALU.add).then_inc(dve_step, 1)
                                add_up(u, t, done + 2)
                                a0 = al[:, r, 0, :].rearrange("p (s h) -> p s h", s=K)
                                a1 = al[:, r, 1, :].rearrange("p (s h) -> p s h", s=K)
                                a2 = al[:, r, 2, :].rearrange("p (s h) -> p s h", s=K)
                                dve.wait_ge(dve_step, done + 3)
                                nc.vector.scalar_tensor_tensor(a1, a0, SCALE, maskneg[:, bass.ds(t * K, K)].unsqueeze(2).to_broadcast([P, K, HEADS]),
                                                               ALU.mult, ALU.add).then_inc(dve_step, 1)
                                dve.wait_ge(dve_step, done + 6)
                                nc.vector.tensor_reduce(rowmax[:, bass.ds(t * HEADS, HEADS)], al[:, r, 1, :].rearrange("p (s h) -> p h s", s=K), AX_X, ALU.max).then_inc(dve_step, 1)
                                dve.wait_ge(dve_step, done + 7)
                                nc.vector.tensor_tensor(a2, a1, rowmax[:, bass.ds(t * HEADS, HEADS)].unsqueeze(1).to_broadcast([P, K, HEADS]), ALU.subtract).then_inc(dve_step, 1)
                        step_of_rows(0)
                        with nc.vector.Fori(1, STEPS) as i:
                            step_of_rows(i)
                        dve.wait_ge(exp_done, NV)
                        weigh(4, NV, 2)
                        add_up(4, NV, OPS * NV + 1)
                        dve.wait_ge(dve_step, OPS * NV + 3)

        def segment_max():
            with ExitStack() as ph:
                step, to_pe, from_pe, exp_done, scaled, run, sums_out = fresh(ph, "max_step", "to_pe", "from_pe", "exp_done", "scaled", "run", "sums_out")
                BLOCK = NV // 4
                fwd = ring[:, 0:HEADS * NV].rearrange("p (h j) -> p h j", h=HEADS)
                seg_max = ring[:, HEADS * NV:2 * HEADS * NV].rearrange("p (h j) -> p h j", h=HEADS)
                rm = rowmax[:, :].rearrange("p (j h) -> p j h", h=HEADS)
                ends = small[:, 0:2 * HEADS]
                tails, heads = small[0:HEADS, 32:32 + P + 1], small[0:HEADS, 192:192 + P + 1]
                cf, cb = small[0:HEADS, 352:352 + P], small[0:HEADS, 512:512 + P]
                cfb = small[:, 680:680 + 2 * HEADS]
                with nc.Block() as block:
                    @block.tensor
                    def _(pe):
                        pe.wait_ge(to_pe, 1)
                        nc.tensor.transpose(bank[0][0:HEADS, 0:P], ends[:, 0:HEADS], ident[:, :])
                        nc.tensor.transpose(bank[1][0:HEADS, 0:P], ends[:, HEADS:2 * HEADS], ident[:, :]).then_inc(from_pe, 1)
                        pe.wait_ge(to_pe, 2)
                        nc.tensor.transpose(bank[2][:, 0:HEADS], cf, ident[0:HEADS, 0:HEADS])
                        nc.tensor.transpose(bank[3][:, 0:HEADS], cb, ident[0:HEADS, 0:HEADS]).then_inc(from_pe, 1)

                    @block.sync
                    def _(sp):
                        for b in range(NV // BLOCK):
                            sp.wait_ge(run, W * (b + 1))
                            lo, hi = max(b * BLOCK - 1, 0), (b + 1) * BLOCK - (1 if (b + 1) * BLOCK < NV else 0)
                            sp.dma_start(sums_rows[:, lo * W:hi * W], sums[:, (lo + 1) * W:(hi + 1) * W]).then_inc(sums_out, 16)
                        sp.wait_ge(sums_out, 16 * NV // BLOCK)

                    @block.scalar
                    def _(act):
                        act.wait_ge(to_pe, 3)
                        nc.scalar.activation(rowmax[:, :], rowmax[:, :], ACT.Exp).then_inc(exp_done, 1)

                    @block.vector
                    def _(dve):
                        link = Chain(dve, step)
                        for h in range(HEADS):
                            link(nc.vector.tensor_tensor_scan(fwd[:, h, :], reset[:, :], rm[:, :, h], -BIG, ALU.add, ALU.max))
                            link(nc.vector.tensor_tensor_scan(seg_max[:, h, ::-1], rnext[:, ::-1], fwd[:, h, ::-1], -BIG, ALU.add, ALU.max))
                        link(nc.vector.tensor_copy(ends[:, 0:HEADS], fwd[:, :, NV - 1]))
                        link(nc.vector.tensor_copy(ends[:, HEADS:], seg_max[:, :, 0]))
                        nc.vector.engine_nop().then_inc(to_pe, 1)
                        link(nc.vector.memset(tails[:, 0:1], 0.0))
                        link(nc.vector.memset(heads[:, P:P + 1], 0.0))
                        dve.wait_ge(from_pe, 1)
                        link(nc.vector.tensor_copy(tails[:, 1:P + 1], bank[0][0:HEADS, 0:P]))
                        link(nc.vector.tensor_copy(heads[:, 0:P], bank[1][0:HEADS, 0:P]))
                        link(nc.vector.tensor_tensor(tails[:, 0:P], tails[:, 0:P], neg_rows[0:HEADS, 0:P], ALU.add))
                        link(nc.vector.tensor_tensor(heads[:, 1:P + 1], heads[:, 1:P + 1], neg_rows[0:HEADS, 2 * P:3 * P], ALU.add))
                        link(nc.vector.tensor_tensor_scan(cf, neg_rows[0:HEADS, P:2 * P], tails[:, 0:P], -BIG, ALU.add, ALU.max))
                        link(nc.vector.tensor_tensor_scan(cb[:, ::-1], neg_rows[0:HEADS, 3 * P:4 * P][:, ::-1], heads[:, 1:P + 1][:, ::-1], -BIG, ALU.add, ALU.max))
                        nc.vector.engine_nop().then_inc(to_pe, 1)
                        dve.wait_ge(from_pe, 2)
                        link(nc.vector.tensor_copy(cfb[:, 0:HEADS], bank[2][:, 0:HEADS]))
                        link(nc.vector.tensor_copy(cfb[:, HEADS:], bank[3][:, 0:HEADS]))
                        for h in range(HEADS):
                            link(nc.vector.scalar_tensor_tensor(seg_max[:, h, :], fs_neg[:, :], cfb[:, h:h + 1], seg_max[:, h, :], ALU.add, ALU.max))
                            link(nc.vector.scalar_tensor_tensor(seg_max[:, h, :], ls_neg[:, :], cfb[:, HEADS + h:HEADS + h + 1], seg_max[:, h, :], ALU.add, ALU.max))
                        link(nc.vector.tensor_tensor(rm, rm, ring[:, HEADS * NV:2 * HEADS * NV].rearrange("p (h j) -> p j h", h=HEADS), ALU.subtract))
                        nc.vector.engine_nop().then_inc(to_pe, 1)
                        dve.wait_ge(exp_done, 1)
                        for b in range(NV // BLOCK):
                            lo = b * BLOCK
                            r = rm[:, lo:lo + BLOCK, :]
                            body, den = sums3[:, 1 + lo:1 + lo + BLOCK, 0:D].rearrange("p j (h c) -> p j h c", h=HEADS), sums3[:, 1 + lo:1 + lo + BLOCK, D:]
                            nc.vector.tensor_tensor(body, body, r.unsqueeze(3).to_broadcast([P, BLOCK, HEADS, CH]), ALU.mult).then_inc(scaled, 1)
                            nc.vector.tensor_tensor(den, den, r, ALU.mult).then_inc(scaled, 1)
                            dve.wait_ge(scaled, 2 * b + 2)
                            if b > 0:
                                dve.wait_ge(run, W * b)
                            first = max(lo - 1, 0)
                            with nc.vector.Fori(0, HEADS) as i:
                                for k in range(W // HEADS):
                                    col = sums3[:, 1 + first:1 + lo + BLOCK, bass.ds(W // HEADS * i + k, 1)].rearrange("p j o -> p (j o)")
                                    nc.vector.tensor_tensor_scan(col, same_l[:, first:lo + BLOCK], col, 0.0, ALU.mult, ALU.add).then_inc(run, 1)
                        dve.wait_ge(run, W * NV // BLOCK)

        def carry_parts(ph):
            r_in, r_out, *g_in = dma_sems("first_in", "first_out", *[f"agg_in{i}" for i in range(NT // U)])
            to_pe, from_pe, carry_ready = fresh(ph, "carry_to_pe", "carry_from_pe", "carry_ready")
            tails = ring[:, 0:P + 1]
            tails8 = ring[0:HEADS, 200:200 + P + 1]
            c_t, c8 = ring[:, 400:400 + P], ring[0:HEADS, 600:600 + P]
            carry, first = ring[:, 800:800 + W], ring[:, 1000:1000 + W]

            def on_pe(pe):
                nc.tensor.transpose(bank[0][:, 0:P], sums3[:, NV, 0:D], ident[:, :])
                nc.tensor.transpose(bank[1][0:HEADS, 0:P], sums3[:, NV, D:], ident[:, :]).then_inc(from_pe, 1)
                pe.wait_ge(to_pe, 1)
                nc.tensor.transpose(bank[2][:, 0:D], c_t, ident[:, :])
                nc.tensor.transpose(bank[3][:, 0:HEADS], c8, ident[0:HEADS, 0:HEADS]).then_inc(from_pe, 1)

            def on_dve(dve, link):
                link(nc.vector.memset(tails[:, 0:1], 0.0))
                link(nc.vector.memset(tails8[:, 0:1], 0.0))
                dve.wait_ge(from_pe, 1)
                link(nc.vector.tensor_copy(tails[:, 1:], bank[0][:, 0:P]))
                link(nc.vector.tensor_copy(tails8[:, 1:], bank[1][0:HEADS, 0:P]))
                link(nc.vector.tensor_tensor(tails[:, 0:P], tails[:, 0:P], link_row[:, :], ALU.mult))
                link(nc.vector.tensor_tensor(tails8[:, 0:P], tails8[:, 0:P], link_row[0:HEADS, :], ALU.mult))
                link(nc.vector.tensor_tensor_scan(c_t, cont_row[:, :], tails[:, 0:P], 0.0, ALU.mult, ALU.add))
                link(nc.vector.tensor_tensor_scan(c8, cont_row[0:HEADS, :], tails8[:, 0:P], 0.0, ALU.mult, ALU.add))
                nc.vector.engine_nop().then_inc(to_pe, 1)
                dve.wait_ge(from_pe, 2)
                link(nc.vector.tensor_copy(carry[:, 0:D], bank[2][:, 0:D]))
                link(nc.vector.tensor_copy(carry[:, D:], bank[3][:, 0:HEADS]))
                dve.wait_ge(r_in, 16)
                link(nc.vector.tensor_tensor(carry, carry, first, ALU.add))
                nc.vector.engine_nop().then_inc(carry_ready, 1)

            def on_pool(pool):
                nc.gpsimd.indirect_dma_start(out=first, out_offset=None, in_=sums_tab,
                                             in_offset=bass.IndirectOffsetOnAxis(ap=first_end[:, 0:1], axis=0)).then_inc(r_in, 16)
                pool.wait_ge(carry_ready, 1)
                nc.gpsimd.indirect_dma_start(out=sums_tab, out_offset=bass.IndirectOffsetOnAxis(ap=first_end[:, 0:1], axis=0),
                                             in_=carry, in_offset=None).then_inc(r_out, 16)
                pool.wait_ge(r_out, 16)
                for t in range(NT):
                    nc.gpsimd.indirect_dma_start(out=agg[:, t, :], out_offset=None, in_=sums_tab,
                                                 in_offset=bass.IndirectOffsetOnAxis(ap=last_idx[:, t:t + 1], axis=0)).then_inc(g_in[t // U], 16)
                for g in g_in:
                    pool.wait_ge(g, 16 * U)
            return on_pe, on_dve, on_pool, g_in

        def carry_and_gather():
            with ExitStack() as ph:
                on_pe, on_dve, on_pool, _ = carry_parts(ph)
                step, = fresh(ph, "carry_step")
                with nc.Block() as block:
                    @block.tensor
                    def _(pe):
                        on_pe(pe)

                    @block.vector
                    def _(dve):
                        on_dve(dve, Chain(dve, step))

                    @block.gpsimd
                    def _(pool):
                        on_pool(pool)

        def norm_ops(link, act_sqrt, src3, dst3):
            mean, var, inv, tmp = (col25[:, k * NT:(k + 1) * NT] for k in range(4))
            bc = lambda c: c.unsqueeze(2).to_broadcast([P, NT, D])
            link(nc.vector.tensor_reduce(mean, src3, AX_X, ALU.add))
            link(nc.vector.tensor_scalar(mean, mean, 1.0 / D, None, ALU.mult))
            link(nc.vector.tensor_tensor(dst3, src3, bc(mean), ALU.subtract))
            link(nc.vector.tensor_tensor(sq3, dst3, dst3, ALU.mult))
            link(nc.vector.tensor_reduce(var, sq3, AX_X, ALU.add))
            link(nc.vector.tensor_scalar(var, var, 1.0 / D, LN_EPS, ALU.mult, ALU.add))
            act_sqrt(var, tmp)
            link(nc.vector.reciprocal(inv, tmp))
            link(nc.vector.tensor_tensor(dst3, dst3, bc(inv), ALU.mult))

        def node_math(body, roots):
            with ExitStack() as ph:
                step, to_act, from_act = fresh(ph, "math_step", "to_act", "from_act")
                asked = []
                with nc.Block() as block:
                    @block.vector
                    def _(dve):
                        link = Chain(dve, step)

                        def on_act(func):
                            def run(src, dst, **kw):
                                asked.append((func, src, dst, kw))
                                nc.vector.engine_nop().then_inc(to_act, 1)
                                dve.wait_ge(from_act, len(asked))
                            return run
                        body(link, on_act)

                    @block.scalar
                    def _(act):
                        for n, (func, src, dst, kw) in enumerate(roots):
                            act.wait_ge(to_act, n + 1)
                            nc.scalar.activation(dst, src, func, **kw).then_inc(from_act, 1)
                assert [(f, k) for f, _, _, k in asked] == [(f, k) for f, _, _, k in roots]

        SQRT = (ACT.Sqrt, col25[:, NT:2 * NT], col25[:, 3 * NT:4 * NT], {})

        def node_linear(sources, loads, cols, parts, tabs):
            with ExitStack() as ph:
                w_in, staged, tr_done, copied, mm_done, evac, tab_out = fresh(ph, "w_in", "staged", "tr_done", "copied", "mm_done", "evac", "tab_out")
                ins = (stage_in, stage_in2)[:len(sources)]
                outs = (stage_T, stage_T2)[:len(sources)]
                S = len(sources)
                with nc.Block() as block:
                    @block.sync
                    def _(sp):
                        for dst, src in loads:
                            sp.dma_start(dst, src).then_inc(w_in, 16)
                        sp.wait_ge(w_in, 16 * len(loads))
                        for i in range(NT // U if tabs else 0):
                            sp.wait_ge(evac, U * (i + 1) * len(parts))
                            w = slice(U * i, U * (i + 1))
                            for dst, src in tabs:
                                sp.dma_start(dst[:, w, :], src[:, w, :]).then_inc(tab_out, 16)
                        if tabs:
                            sp.wait_ge(tab_out, 16 * len(tabs) * NT // U)

                    @block.scalar
                    def _(act):
                        def step_of_windows(i):
                            for s in range(S):
                                later(act, tr_done, S * i)
                                nc.scalar.copy(ins[s], sources[s][:, bass.ds(U * D * i, U * D)]).then_inc(staged, 1)
                            for s in range(S):
                                act.wait_ge(tr_done, S * i + s + 1)
                                later(act, mm_done, U * i)
                                nc.scalar.copy(outs[s][:, 0:512], bank[2 * s][:, 0:512]).then_inc(copied, 1)
                                nc.scalar.copy(outs[s][:, 512:U * D], bank[2 * s + 1][:, 0:U * D - 512]).then_inc(copied, 1)
                        step_of_windows(0)
                        with nc.scalar.Fori(1, NT // U) as i:
                            step_of_windows(i)

                    @block.tensor
                    def _(pe):
                        pe.wait_ge(w_in, 16 * len(loads))
                        def step_of_windows(i):
                            for s in range(S):
                                pe.wait_ge(staged, S * i + s + 1)
                                later(pe, copied, 2 * S * i)
                                for u in range(U):
                                    ins_ = nc.tensor.transpose(bank[2 * s + u // 4][:, (u % 4) * P:(u % 4 + 1) * P], ins[s][:, u * D:(u + 1) * D], ident[:, :])
                                ins_.then_inc(tr_done, 1)
                            pe.wait_ge(copied, 2 * S * (i + 1))
                            for u in range(U):
                                b = bank[4 + u % 4]
                                later(pe, evac, len(parts) * (U * i + max(u - 3, 0)))
                                for s in range(S):
                                    ins_ = nc.tensor.matmul(b[:, 0:cols], outs[s][:, u * D:(u + 1) * D], wgt[:, s * cols:(s + 1) * cols], start=(s == 0), stop=(s == S - 1))
                                ins_.then_inc(mm_done, 1)
                        step_of_windows(0)
                        with nc.tensor.Fori(1, NT // U) as i:
                            step_of_windows(i)

                    @block.vector
                    def _(dve):
                        dve.wait_ge(w_in, 16 * len(loads))
                        with nc.vector.Fori(0, NT // U) as i:
                            for u in range(U):
                                dve.wait_ge(mm_done, U * i + u + 1)
                                for dst, stride, lo, hi in parts:
                                    nc.vector.tensor_tensor(dst[:, bass.ds((U * i + u) * stride, hi - lo)], bank[4 + u % 4][:, lo:hi], bias[:, lo:hi], ALU.add).then_inc(evac, 1)

        def gine_edges():
            with ExitStack() as ph:
                s0, s1, s2, s3 = dma_sems("slot0", "slot1", "slot2", "slot3")
                idx_ready, rec_in0, rec_in1, tr_done, rt_done, mm_done, dve_step, relu_done, run0, sums_out = fresh(
                    ph, "idx_ready", "rec_in0", "rec_in1", "tr_done", "rt_done", "mm_done", "dve_step", "relu_done", "run0", "sums_out")
                slot_in = (s0, s1, s2, s3)
                rec_in = (rec_in0, rec_in1)
                PER = 16 * K
                KR = K * REC
                recs_r = ring[:, 4 * K * D:4 * K * D + 4 * KR]
                rec_t = ring[:, 4 * K * D + 512:4 * K * D + 512 + 2 * P]
                rv = recs.rearrange("(p j) c -> p (j c)", j=NS)
                with nc.Block() as block:
                    @block.gpsimd
                    def _(pool):
                        pool.wait_ge(idx_ready, 2)
                        for u in range(4):
                            gather_step(h_tab, D, u, slot_in, False)
                        with nc.gpsimd.Fori(1, STEPS) as i:
                            for u in range(4):
                                if u % 2 == 0:
                                    pool.wait_ge(idx_ready, 2 * i + u // 2 + 1)
                                    nc.gpsimd.nop(nofuse=True)
                                pool.wait_ge(dve_step, 4 * (4 * i + u - 3) - 3)
                                nc.gpsimd.nop(nofuse=True)
                                gather_step(h_tab, D, u, slot_in, False)

                    @block.sync
                    def _(sp):
                        def records(i):
                            for half in range(2):
                                if not isinstance(i, int):
                                    sp.wait_ge(tr_done, 4 * i)
                                sp.dma_start(recs_r[:, half * 2 * KR:(half + 1) * 2 * KR], rv[:, bass.ds((4 * i + 2 * half) * KR, 2 * KR)]).then_inc(rec_in[half], 16)

                        def store(i):
                            sp.wait_ge(dve_step, 16 * (i + 1))
                            sp.dma_start(sums_rows[:, bass.ds(4 * i * W, 4 * W)], sums[:, bass.ds((4 * i + 1) * W, 4 * W)]).then_inc(sums_out, 16)
                        records(0)
                        with nc.sync.Fori(1, STEPS) as i:
                            records(i)
                            store(i - 1)
                        store(STEPS - 1)
                        sp.wait_ge(sums_out, 16 * STEPS)

                    @block.tensor
                    def _(pe):
                        def step_of_rows(i):
                            for u in range(4):
                                t = 4 * i + u
                                if u % 2 == 0:
                                    pe.wait_ge(rec_in[u // 2], 16 * (i + 1))
                                later(pe, rt_done, 4 * i + max(u - 1, 0))
                                nc.tensor.transpose(bank[u % 2][0:KR, 0:P], recs_r[:, u * KR:(u + 1) * KR], ident[:, :]).then_inc(tr_done, 1)
                                pe.wait_ge(rt_done, t + 1)
                                later(pe, dve_step, 4 * 4 * i if u < 2 else 4 * (4 * i + u - 1) - 3)
                                nc.tensor.matmul(bank[2 + u % 2][:, 0:K * D], rec_t[0:KR, (u % 2) * P:(u % 2 + 1) * P], wgt[0:KR, 0:K * D], start=True, stop=True).then_inc(mm_done, 1)
                        step_of_rows(0)
                        with nc.tensor.Fori(1, STEPS) as i:
                            step_of_rows(i)

                    @block.scalar
                    def _(act):
                        for half in range(2):
                            index_copies(act, 0, half, (idx_ready,))
                        def step_of_rows(i):
                            for u in range(4):
                                t = 4 * i + u
                                act.wait_ge(tr_done, t + 1)
                                later(act, mm_done, 4 * i + max(u - 1, 0))
                                nc.scalar.copy(rec_t[0:KR, (u % 2) * P:(u % 2 + 1) * P], bank[u % 2][0:KR, 0:P]).then_inc(rt_done, 1)
                                act.wait_ge(dve_step, 4 * t + 1)
                                pr = prod[:, (u % 2) * K * D:(u % 2 + 1) * K * D]
                                nc.scalar.activation(pr, pr, ACT.Relu).then_inc(relu_done, 1)
                                if u % 2 == 1:
                                    act.wait_ge(slot_in[u - 1], PER * (i + 1))
                                    act.wait_ge(slot_in[u], PER * (i + 1))
                                    index_copies(act, i + 1, u // 2, (idx_ready,))
                        step_of_rows(0)
                        with nc.scalar.Fori(1, STEPS) as i:
                            step_of_rows(i)

                    @block.vector
                    def _(dve):
                        nc.vector.memset(sums3[:, 0, :], 0.0).then_inc(run0, 1)
                        nc.vector.memset(sums3[:, 1:, D:], 0.0).then_inc(run0, 1)
                        dve.wait_ge(run0, 2)
                        def step_of_rows(i):
                            for u in range(4):
                                t = 4 * i + u
                                pr = prod[:, (u % 2) * K * D:(u % 2 + 1) * K * D]
                                pw = pv[:, 0:K * D]
                                tmp = pv[:, K * D:K * D + D]
                                dve.wait_ge(slot_in[u], PER * (i + 1))
                                dve.wait_ge(mm_done, t + 1)
                                nc.vector.tensor_tensor(pr, bank[2 + u % 2][:, 0:K * D], ring[:, u * K * D:(u + 1) * K * D], ALU.add).then_inc(dve_step, 1)
                                dve.wait_ge(relu_done, t + 1)
                                later(dve, dve_step, 4 * t)
                                nc.vector.tensor_tensor(pw.rearrange("p (s f) -> p s f", s=K), pr.rearrange("p (s f) -> p s f", s=K),
                                                        weight[:, bass.ds(t * K, K)].unsqueeze(2).to_broadcast([P, K, D]), ALU.mult).then_inc(dve_step, 1)
                                dve.wait_ge(dve_step, 4 * t + 2)
                                nc.vector.tensor_reduce(tmp, pw.rearrange("p (s f) -> p f s", s=K), AX_X, ALU.add).then_inc(dve_step, 1)
                                dve.wait_ge(dve_step, 4 * t + 3)
                                nc.vector.scalar_tensor_tensor(sums[:, bass.ds((t + 1) * W, D)], sums[:, bass.ds(t * W, D)], same_l[:, bass.ds(t, 1)], tmp,
                                                               ALU.mult, ALU.add).then_inc(dve_step, 1)
                        step_of_rows(0)
                        with nc.vector.Fori(1, STEPS) as i:
                            step_of_rows(i)
                        dve.wait_ge(dve_step, 4 * NV)

        bn = sb("bn", 5 * 3)
        bnc = sb("bnc", 4 * 3)
        epsb = sb("epsb", 4)

        def gine_nodes(layer):
            with ExitStack() as ph:
                on_pe, on_dve, on_pool, g_in = carry_parts(ph)
                w_in, step, z_ready, norm_step, staged, tr_done, copied, m1_done, y_done, m2_done, evac, tab_out, root = fresh(
                    ph, "w_in", "mlp_step", "z_ready", "norm_step", "staged", "tr_done", "copied", "m1_done", "y_done", "m2_done", "evac", "tab_out", "root")
                w1, w2 = bias[:, D:2 * D], bias[:, 2 * D:3 * D]
                scale, shift = bnc[:, 0:1], bnc[:, 1:2]
                pick = lambda k: bn[:, 3 * k + layer:3 * k + layer + 1]
                with nc.Block() as block:
                    @block.sync
                    def _(sp):
                        sp.dma_start(w1, a["L2_W1"][layer]).then_inc(w_in, 16)
                        sp.dma_start(w2, a["L2_W2"][layer]).then_inc(w_in, 16)
                        sp.dma_start(bias[:, 0:D], a["L2_b2"][layer:layer + 1, :].to_broadcast([P, D])).then_inc(w_in, 16)
                        for i in range(NT // U):
                            sp.wait_ge(evac, 2 * U * (i + 1))
                            sp.dma_start(table(h_tab)[:, U * i:U * (i + 1), :], skip3[:, U * i:U * (i + 1), :]).then_inc(tab_out, 16)
                        sp.wait_ge(tab_out, 16 * NT // U)

                    @block.gpsimd
                    def _(pool):
                        on_pool(pool)

                    @block.vector
                    def _(dve):
                        link = Chain(dve, step)
                        link(nc.vector.tensor_scalar(epsb[:, 3:4], epsb[:, layer:layer + 1], 1.0, None, ALU.add))
                        link(nc.vector.tensor_scalar(bnc[:, 2:3], pick(3), LN_EPS, None, ALU.add))
                        nc.vector.engine_nop().then_inc(norm_step, 1)
                        on_dve(dve, link)
                        dve.wait_ge(root, 1)
                        link(nc.vector.reciprocal(bnc[:, 2:3], bnc[:, 3:4]))
                        link(nc.vector.tensor_tensor(scale, bnc[:, 2:3], pick(0), ALU.mult))
                        link(nc.vector.tensor_tensor(bnc[:, 4:5], pick(4), pick(2), ALU.subtract))
                        link(nc.vector.scalar_tensor_tensor(shift, bnc[:, 4:5], scale, pick(1), ALU.mult, ALU.add))
                        nc.vector.engine_nop().then_inc(norm_step, 1)
                        dve.wait_ge(w_in, 48)

                        def z(i):
                            w = slice(U * i, U * (i + 1))
                            dve.wait_ge(g_in[i], 16 * U)
                            nc.vector.scalar_tensor_tensor(work3[:, w, :], skip3[:, w, :], epsb[:, 3:4], agg[:, w, 0:D], ALU.mult, ALU.add).then_inc(z_ready, 1)
                            dve.wait_ge(z_ready, i + 1)
                        z(0)
                        for i in range(NT // U):
                            if i + 1 < NT // U:
                                z(i + 1)
                            for u in range(U):
                                h = skip3[:, U * i + u, :]
                                dve.wait_ge(m2_done, U * i + u + 1)
                                nc.vector.tensor_tensor(h, bank[4 + u % 4][:, 0:D], bias[:, 0:D], ALU.add).then_inc(evac, 1)
                                dve.wait_ge(evac, 2 * (U * i + u) + 1)
                                nc.vector.tensor_scalar(h, h, 0.0, None, ALU.max).then_inc(evac, 1)

                    @block.scalar
                    def _(act):
                        act.wait_ge(norm_step, 1)
                        nc.scalar.activation(bnc[:, 3:4], bnc[:, 2:3], ACT.Sqrt).then_inc(root, 1)
                        act.wait_ge(norm_step, 2)
                        def step_of_windows(i):
                            act.wait_ge(z_ready, i + 1)
                            later(act, tr_done, i)
                            nc.scalar.copy(stage_in, work[:, bass.ds(U * D * i, U * D)]).then_inc(staged, 1)
                            act.wait_ge(tr_done, i + 1)
                            later(act, m1_done, i)
                            nc.scalar.copy(stage_T[:, 0:512], bank[0][:, 0:512]).then_inc(copied, 1)
                            nc.scalar.copy(stage_T[:, 512:U * D], bank[1][:, 0:U * D - 512]).then_inc(copied, 1)
                            act.wait_ge(m1_done, i + 1)
                            later(act, m2_done, U * i)
                            nc.scalar.activation(stage_y[:, 0:512], bank[2][:, 0:512], ACT.Relu, bias=shift, scale=scale).then_inc(y_done, 1)
                            nc.scalar.activation(stage_y[:, 512:U * D], bank[3][:, 0:U * D - 512], ACT.Relu, bias=shift, scale=scale).then_inc(y_done, 1)
                        step_of_windows(0)
                        with nc.scalar.Fori(1, NT // U) as i:
                            step_of_windows(i)

                    @block.tensor
                    def _(pe):
                        on_pe(pe)
                        pe.wait_ge(w_in, 48)
                        def step_of_windows(i):
                            pe.wait_ge(staged, i + 1)
                            later(pe, copied, 2 * i)
                            for u in range(U):
                                ins_ = nc.tensor.transpose(bank[u // 4][:, (u % 4) * P:(u % 4 + 1) * P], stage_in[:, u * D:(u + 1) * D], ident[:, :])
                            ins_.then_inc(tr_done, 1)
                            pe.wait_ge(copied, 2 * (i + 1))
                            later(pe, y_done, 2 * i)
                            nc.tensor.matmul(bank[2][:, 0:512], w1, stage_T[:, 0:512], start=True, stop=True)
                            nc.tensor.matmul(bank[3][:, 0:U * D - 512], w1, stage_T[:, 512:U * D], start=True, stop=True).then_inc(m1_done, 1)
                            pe.wait_ge(y_done, 2 * (i + 1))
                            for u in range(U):
                                later(pe, evac, 2 * (U * i + max(u - 3, 0)))
                                nc.tensor.matmul(bank[4 + u % 4][:, 0:D], stage_y[:, u * D:(u + 1) * D], w2, start=True, stop=True).then_inc(m2_done, 1)
                        step_of_windows(0)
                        with nc.tensor.Fori(1, NT // U) as i:
                            step_of_windows(i)

        for c in range(2):
            src = x if c == 0 else work
            loads = []
            for k, n in enumerate("qkvs"):
                loads.append((wgt[:, k * D:(k + 1) * D], a[f"L0_{n}_w{c}"]))
                loads.append((bias[:, k * D:(k + 1) * D], a[f"L0_{n}_b{c}"].to_broadcast([P, D])))
            node_linear([src[:, :] if c == 0 else work], loads, 4 * D,
                        [(area(10000, NT * 384), 384, 0, 384), (skip[:, :], D, 384, 512)],
                        [(table(q_tab), proj3[:, :, 0:D]), (table(kv_tab), proj3[:, :, D:3 * D])])
            conv_edges()
            segment_max()
            carry_and_gather()

            def conv_nodes(link, on_act):
                den = sq3[:, :, 0:HEADS]
                link(nc.vector.tensor_scalar(den, agg[:, :, D:], 1e-30, None, ALU.max))
                link(nc.vector.reciprocal(den, den))
                body = agg[:, :, 0:D].rearrange("p t (h c) -> p t h c", h=HEADS)
                link(nc.vector.tensor_tensor(body, body, den.unsqueeze(3).to_broadcast([P, NT, HEADS, CH]), ALU.mult))
                link(nc.vector.tensor_tensor(work3, agg[:, :, 0:D], skip3, ALU.add))
                if c == 0:
                    link(nc.vector.tensor_scalar(work, work, 0.0, None, ALU.max))
                else:
                    link(nc.vector.tensor_tensor(work3, work3, x3, ALU.add))
                    norm_ops(link, on_act(ACT.Sqrt), work3, x3)
            node_math(conv_nodes, [] if c == 0 else [SQRT])

        NPF = NP
        cnt_buf = [area(k * NPF, NPF) for k in range(3)]
        own = [area((3 + k) * NPF, NPF) for k in range(3)]
        s1bc, e_steep, e_flat = area(6 * NPF, NPF), area(7 * NPF, NPF), area(8 * NPF + 704, NPF)
        tailoff = 8 * NPF
        a12, s12, s1t, lnwb = (area(tailoff + o_, n_) for o_, n_ in ((0, 2 * D), (256, 2 * NT), (310, P), (440, 2 * D)))
        deg = small[:, 0:NT]
        s2_steep, s2_flat = small[:, 32:32 + NT], small[:, 64:64 + NT]

        def by_src(feat, attention):
            with ExitStack() as ph:
                cin = fresh(ph, "counts_in0", "counts_in1", "counts_in2")
                diff, own_ready, mm_done, e_ready, least, deg_ready = fresh(ph, "diff", "own_ready", "mm_done", "e_ready", "least", "deg_ready")
                with nc.Block() as block:
                    @block.sync
                    def _(sp):
                        for n in range(3):
                            if n == 2:
                                sp.wait_ge(diff, 1)
                            sp.dma_start(cnt_buf[n], count_tab[n * P:(n + 1) * P, :]).then_inc(cin[n], 16)
                        with nc.sync.Fori(0, (NT - 4) // 3) as i:
                            for u in range(3):
                                sp.wait_ge(diff, 3 * i + u + 2)
                                sp.dma_start(cnt_buf[u], count_tab[bass.ds((3 * i + u + 3) * P, P), :]).then_inc(cin[u], 16)
                        sp.wait_ge(diff, NT - 2)
                        sp.dma_start(cnt_buf[(NT - 1) % 3], count_tab[(NT - 1) * P:NT * P, :]).then_inc(cin[(NT - 1) % 3], 16)

                    @block.vector
                    def _(dve):
                        def step(n, u, loads_due, mm_due):
                            dve.wait_ge(cin[u], 16 * loads_due)
                            if mm_due is None:
                                nc.vector.tensor_copy(own[u], cnt_buf[u]).then_inc(diff, 1)
                            else:
                                if mm_due is not False:
                                    dve.wait_ge(mm_done, mm_due)
                                nc.vector.tensor_tensor(own[u], cnt_buf[u], cnt_buf[(u - 1) % 3], ALU.subtract).then_inc(diff, 1)
                            if attention:
                                dve.wait_ge(e_ready, 2 * n + 2)
                                nc.vector.scalar_tensor_tensor(e_steep, e_steep, 3e38, e_flat, ALU.min, ALU.min).then_inc(least, 1)
                                dve.wait_ge(least, n + 1)
                                dve.wait_ge(diff, n + 1)
                                nc.vector.tensor_tensor(own[u], own[u], e_steep, ALU.mult).then_inc(own_ready, 1)
                        step(0, 0, 1, None)
                        for n in (1, 2):
                            step(n, n, 1, False)
                        with nc.vector.Fori(0, (NT - 4) // 3) as i:
                            for u in range(3):
                                step(3 * i + u + 3, u, i + 2, 3 * i + u + 1)
                        step(NT - 1, (NT - 1) % 3, (NT - 1) // 3 + 1, NT - 3)
                        dve.wait_ge(mm_done, NT)
                        if not attention:
                            nc.vector.tensor_scalar(deg, bank[7][:, 0:NT], 1.0, None, ALU.max).then_inc(deg_ready, 1)

                    @block.scalar
                    def _(act):
                        if attention:
                            for n in range(NT):
                                if n > 0:
                                    act.wait_ge(least, n)
                                nc.scalar.activation(e_flat, s1bc, ACT.Exp, scale=-0.2, bias=s2_flat[:, n:n + 1]).then_inc(e_ready, 1)
                                if n > 0:
                                    act.wait_ge(own_ready, n)
                                nc.scalar.activation(e_steep, s1bc, ACT.Exp, scale=-1.0, bias=s2_steep[:, n:n + 1]).then_inc(e_ready, 1)

                    @block.tensor
                    def _(pe):
                        def products(n, u, first):
                            pe.wait_ge(own_ready if attention else diff, n + 1)
                            for a_ in range(NT):
                                w = own[u][:, a_ * P:(a_ + 1) * P]
                                rhs = feat[:, 0:D] if first else feat[:, bass.ds(n * D, D)]
                                kw = dict(start=first and a_ % 4 == 0, stop=True, skip_group_check=True)
                                ins_ = nc.tensor.matmul(bank[a_ // 4][:, (a_ % 4) * D:(a_ % 4 + 1) * D], w, rhs, **kw)
                                if not attention:
                                    ins_ = nc.tensor.matmul(bank[7][:, a_:a_ + 1], w, ones[:, 0:1], start=first and a_ == 0, stop=True, skip_group_check=True)
                            ins_.then_inc(mm_done, 1)
                        products(0, 0, True)
                        for n in (1, 2):
                            products(n, n, False)
                        with nc.tensor.Fori(0, (NT - 4) // 3) as i:
                            for u in range(3):
                                products(3 * i + u + 3, u, False)
                        products(NT - 1, (NT - 1) % 3, False)

        assert (NT - 4) % 3 == 0

        by_src(x, False)

        def mean_nodes(link, on_act):
            inv = s12[:, 0:NT]
            link(nc.vector.reciprocal(inv, deg))
            link(nc.vector.tensor_tensor(mean3, psum[:, 0:NP].rearrange("p (t d) -> p t d", d=D), inv.unsqueeze(2).to_broadcast([P, NT, D]), ALU.mult))
        mean = cnt_buf[0]
        mean3 = mean.rearrange("p (t d) -> p t d", d=D)
        node_math(mean_nodes, [])
        node_linear([x[:, :], mean], [(wgt[:, 0:D], a["L1_WT"][0:D, :]), (wgt[:, D:2 * D], a["L1_WT"][D:2 * D, :]), (bias[:, 0:D], a["L1_b"].to_broadcast([P, D]))],
                    D, [(skip[:, :], D, 0, D)], [])

        def add_norm(link, on_act):
            link(nc.vector.tensor_tensor(work3, skip3, x3, ALU.add))
            norm_ops(link, on_act(ACT.Sqrt), work3, x3)
        node_math(add_norm, [SQRT])

        node_linear([x[:, :]], [(wgt[:, 0:D], a["L2_W_enc"]), (bias[:, 0:D], a["L2_b_enc"].to_broadcast([P, D])),
                                (bn[:, :], a["L2_bn"]), (epsb[:, 0:3], a["L2_eps"].to_broadcast([P, 3]))],
                    D, [(skip[:, :], D, 0, D)], [(table(h_tab), skip3)])
        with ExitStack() as ph:
            w_in, clear = fresh(ph, "w_in", "clear")
            with nc.Block() as block:
                @block.vector
                def _(dve):
                    nc.vector.memset(wgt[:, :], 0.0).then_inc(clear, 1)

                @block.sync
                def _(sp):
                    sp.wait_ge(clear, 1)
                    for s in range(K):
                        sp.dma_start(wgt[s * REC:s * REC + EA, s * D:(s + 1) * D], a["L2_W_ee"]).then_inc(w_in, 16)
                        sp.dma_start(wgt[s * REC + R_ONE:s * REC + R_ONE + 1, s * D:(s + 1) * D], a["L2_b_ee"]).then_inc(w_in, 16)
                    sp.wait_ge(w_in, 32 * K)
        for layer in range(3):
            gine_edges()
            gine_nodes(layer)
        node_math(add_norm, [SQRT])

        node_linear([x[:, :]], [(wgt[:, 0:D], a["L3_WT"]), (bias[:, 0:D], a["L3_b"].to_broadcast([P, D])),
                                (a12[:, 0:D], a["L3_a"][:, 0:D].to_broadcast([P, D])), (a12[:, D:], a["L3_a"][:, D:].to_broadcast([P, D])),
                                (lnwb[:, 0:D], a["L3_ln_w"].to_broadcast([P, D])), (lnwb[:, D:], a["L3_ln_b"].to_broadcast([P, D]))], D, [(skip[:, :], D, 0, D)], [])
        hh = cnt_buf[0]
        hh3 = hh.rearrange("p (t d) -> p t d", d=D)
        g_flat = cnt_buf[1]
        with ExitStack() as ph:
            step, to_pe, from_pe, s_ready, s1_out, s1_in = fresh(ph, "gat_step", "to_pe", "from_pe", "s_ready", "s1_out", "s1_in")
            with nc.Block() as block:
                @block.sync
                def _(sp):
                    sp.wait_ge(s_ready, 1)
                    sp.dma_start(s1_tab.rearrange("a (t p) -> (a t) p", p=P), s1t[0:NT, :]).then_inc(s1_out, 16)
                    sp.wait_ge(s1_out, 16)
                    sp.dma_start(s1bc, s1_tab.to_broadcast([P, NP])).then_inc(s1_in, 16)
                    sp.wait_ge(s1_in, 16)

                @block.tensor
                def _(pe):
                    pe.wait_ge(to_pe, 1)
                    nc.tensor.transpose(bank[0][0:NT, 0:P], s12[:, 0:NT], ident[:, :]).then_inc(from_pe, 1)

                @block.vector
                def _(dve):
                    link = Chain(dve, step)
                    for k in range(2):
                        link(nc.vector.tensor_tensor(hh3, skip3, a12[:, k * D:(k + 1) * D].unsqueeze(1).to_broadcast([P, NT, D]), ALU.mult))
                        link(nc.vector.tensor_reduce(s12[:, k * NT:(k + 1) * NT], hh3, AX_X, ALU.add))
                        if k == 0:
                            nc.vector.engine_nop().then_inc(to_pe, 1)
                    link(nc.vector.tensor_scalar(s2_steep, s12[:, NT:], -1.0, None, ALU.mult))
                    link(nc.vector.tensor_scalar(s2_flat, s12[:, NT:], -0.2, None, ALU.mult))
                    dve.wait_ge(from_pe, 1)
                    link(nc.vector.tensor_copy(s1t[0:NT, :], bank[0][0:NT, 0:P]))
                    nc.vector.engine_nop().then_inc(s_ready, 1)
        by_src(skip, True)

        def gat_nodes(link, on_act):
            ln_mean, ln_var, ln_inv, ln_tmp = (small[:, 100 + k * NT:100 + (k + 1) * NT] for k in range(4))
            bc = lambda c: c.unsqueeze(2).to_broadcast([P, NT, D])
            row = lambda r: r.unsqueeze(1).to_broadcast([P, NT, D])

            def norm(src, dst, scratch, sqrt):
                link(nc.vector.tensor_reduce(ln_mean, src, AX_X, ALU.add))
                link(nc.vector.tensor_scalar(ln_mean, ln_mean, 1.0 / D, None, ALU.mult))
                link(nc.vector.tensor_tensor(dst, src, bc(ln_mean), ALU.subtract))
                link(nc.vector.tensor_tensor(scratch, dst, dst, ALU.mult))
                link(nc.vector.tensor_reduce(ln_var, scratch, AX_X, ALU.add))
                link(nc.vector.tensor_scalar(ln_var, ln_var, 1.0 / D, LN_EPS, ALU.mult, ALU.add))
                sqrt(ln_var, ln_tmp)
                link(nc.vector.reciprocal(ln_inv, ln_tmp))
                link(nc.vector.tensor_tensor(dst, dst, bc(ln_inv), ALU.mult))

            norm(psum[:, 0:NP].rearrange("p (t d) -> p t d", d=D), skip3, hh3, on_act(ACT.Sqrt))
            link(nc.vector.tensor_tensor(skip3, skip3, row(lnwb[:, 0:D]), ALU.mult))
            link(nc.vector.tensor_tensor(skip3, skip3, row(lnwb[:, D:]), ALU.add))
            link(nc.vector.tensor_scalar(hh, skip[:, :], 0.0, None, ALU.min))
            on_act(ACT.Exp)(hh, g_flat)
            link(nc.vector.tensor_scalar(skip[:, :], skip[:, :], 0.0, -1.0, ALU.max, ALU.add))
            link(nc.vector.tensor_tensor(skip[:, :], skip[:, :], g_flat, ALU.add))
            link(nc.vector.tensor_tensor(hh3, skip3, x3, ALU.add))
            norm(hh3, x3, skip3, on_act(ACT.Sqrt))
        lv, lt = small[:, 100 + NT:100 + 2 * NT], small[:, 100 + 3 * NT:100 + 4 * NT]
        node_math(gat_nodes, [(ACT.Sqrt, lv, lt, {}), (ACT.Exp, hh, g_flat, {}), (ACT.Sqrt, lv, lt, {})])

        out_done = sem("out_done")
        with nc.Block() as block:
            @block.sync
            def _(sp):
                sp.dma_start(out[0:(NT - 1) * P, :].rearrange("(t p) d -> p t d", p=P), x3[:, 0:NT - 1, :]).then_inc(out_done, 16)
                sp.dma_start(out[(NT - 1) * P:N, :], x3[0:TAIL, NT - 1, :]).then_inc(out_done, 16)
                sp.wait_ge(out_done, 32)


def layout(i):
    import numpy as np

    c = np.ascontiguousarray
    a = {"x": c(i["x"]), "src": c(i["src"]), "dst": c(i["dst"]), "edge_attr": c(i["edge_attr_16"]), "edge_weight": c(np.asarray(i["edge_weight1"]).reshape(-1))}
    for n in "qkvs":
        for l in range(2):
            a[f"L0_{n}_w{l}"] = c(i[f"L0_gnn_{n}_w{l}"])
            a[f"L0_{n}_b{l}"] = c(np.asarray(i[f"L0_gnn_{n}_b{l}"]).reshape(1, -1))
    a["L1_WT"] = c(np.asarray(i["L1_gnn_W"]).T)
    a["L1_b"] = c(np.asarray(i["L1_gnn_b"]).reshape(1, -1))
    for n in ("W_enc", "W_ee", "W1", "W2", "b2"):
        a[f"L2_{n}"] = c(i[f"L2_gnn_{n}"])
    for n in ("b_enc", "b_ee", "eps"):
        a[f"L2_{n}"] = c(np.asarray(i[f"L2_gnn_{n}"]).reshape(1, -1))
    a["L2_bn"] = c(np.concatenate([np.asarray(i[f"L2_gnn_{n}"]).T for n in ("bn_gamma", "bn_beta", "bn_mean", "bn_var", "b1")], axis=1))
    a["L3_WT"] = c(np.asarray(i["L3_gnn_W"]).T)
    for n in ("b", "a", "ln_w", "ln_b"):
        a[f"L3_{n}"] = c(np.asarray(i[f"L3_gnn_{n}"]).reshape(1, -1))
    return a


def kernel(**inputs):
    import concourse.bacc as bacc
    from concourse.bass_utils import run_bass_kernel_spmd

    nc = bacc.Bacc("TRN2", target_bir_lowering=False, num_devices=1)
    arrays, aps = {}, {}
    for name, arr in layout(inputs).items():
        arrays[f"in_{name}"] = arr
        aps[name] = nc.dram_tensor(f"in_{name}", arr.shape, mybir.dt.from_np(arr.dtype), kind="ExternalInput").ap()
    out = nc.dram_tensor("out_x", (N, D), F32, kind="ExternalOutput").ap()
    build(nc, aps, out)
    r = run_bass_kernel_spmd(nc, [arrays], core_ids=[0])
    return r.results[0]["out_x"]
```
